# Optimizing a Trainium2 kernel written in Bass

```python
import numpy as np
import jax
import jax.numpy as jnp

def _softmax(x, axis=-1):
    return jax.nn.softmax(x, axis=axis)

def _gelu(x):
    return jax.nn.gelu(x, approximate=True)

def _silu(x):
    return jax.nn.silu(x)

def _sigmoid(x):
    return jax.nn.sigmoid(x)

def _layernorm(x, axis=-1, eps=1e-05):
    m = jnp.mean(x, axis=axis, keepdims=True)
    v = jnp.var(x, axis=axis, keepdims=True)
    return (x - m) / jnp.sqrt(v + eps)

def _scatter_add(tgt, idx, src, axis=0):
    return tgt.at[idx].add(src)

def _segment_sum(src, seg, n):
    return jax.ops.segment_sum(src, seg, n)
kernel_name = 'mk_flamingo_gated_d2_seqx_r4_040c79'

def setup_inputs(seed: int=0):
    np.random.seed(seed)
    _w = jnp.asarray

    def _rec_inputs():
        import jax
        import jax.numpy as jnp
        _rk = jax.random.key(seed)
        x = 7.22e-05 + 1 * jax.random.normal(jax.random.fold_in(_rk, 1), (2, 1024, 256), jnp.float32)
        _lenS = 1024 - jax.random.randint(jax.random.fold_in(_rk, 7), (2,), 0, max(1, 1024 // 4) + 1, jnp.int32)
        _lenS2 = 154 - jax.random.randint(jax.random.fold_in(_rk, 8), (2,), 0, max(1, 154 // 4) + 1, jnp.int32)
        _ctx_768P = jax.random.normal(jax.random.fold_in(_rk, 11), (2, 16, 192), jnp.float32)
        _ctx_768c = jax.random.dirichlet(jax.random.fold_in(_rk, 511), 0.3 * jnp.ones((16,), jnp.float32), (2, 154))
        _ctx_768t = jnp.einsum('bsk,bkd->bsd', _ctx_768c, _ctx_768P)
        _ctx_768t = _ctx_768t * jax.lax.rsqrt(jnp.mean(jnp.square(_ctx_768t)) + 1e-12) * 0.953939
        ctx_768 = 2.09791e-05 + 1.00001 * (_ctx_768t + 0.3 * jax.random.normal(jax.random.fold_in(_rk, 611), (2, 154, 192), jnp.float32))
        _g = jax.random.normal(jax.random.fold_in(_rk, 9001), (2, 2), jnp.float32)
        _g = jnp.sign(_g) * jnp.maximum(jnp.abs(_g), 1.0) + (_g == 0) * 1.0
        g_xattn = _g[0]
        g_ffn = _g[1]
        return (x, ctx_768, g_xattn, g_ffn)
    x, ctx_768, g_xattn, g_ffn = _rec_inputs()

    def _L0_xattn_setup():
        import jax, jax.numpy as jnp
        import numpy as np
        HEADS = 16
        DIM_HEAD = 64
        key = jax.random.key(seed)
        ks = jax.random.split(key, 7)
        B, Nq, Dq = (4, 512, 256)
        Nk, Dc = (256, 192)
        inner = HEADS * DIM_HEAD
        sq = 1.0 / np.sqrt(Dq)
        sc = 1.0 / np.sqrt(Dc)
        si = 1.0 / np.sqrt(inner)
        return {'x': jax.random.normal(ks[0], (B, Nq, Dq), dtype=jnp.float32), 'context': jax.random.normal(ks[1], (B, Nk, Dc), dtype=jnp.float32), 'Wq': jax.random.normal(ks[2], (Dq, inner), dtype=jnp.float32) * sq, 'Wk': jax.random.normal(ks[3], (Dc, inner), dtype=jnp.float32) * sc, 'Wv': jax.random.normal(ks[4], (Dc, inner), dtype=jnp.float32) * sc, 'Wo': jax.random.normal(ks[5], (inner, Dq), dtype=jnp.float32) * si, 'bo': jax.random.normal(ks[6], (Dq,), dtype=jnp.float32) * 0.01}
    _L0_xattn_all = _L0_xattn_setup()
    _L0_xattn_in = {k: v for k, v in _L0_xattn_all.items() if k in ('Wq', 'Wk', 'Wv', 'Wo', 'bo')}
    del _L0_xattn_all

    def _L0_ffn_setup():
        import jax, jax.numpy as jnp
        import numpy as np
        D = 256
        H = 512
        E = 8
        K = 2
        B, T = (4, 512)
        key = jax.random.key(seed)
        ks = jax.random.split(key, 7)
        s = 0.02
        return {'x': jax.random.normal(ks[0], (B, T, D), dtype=jnp.float32), 'W1': jax.random.normal(ks[1], (E, D, 2 * H), dtype=jnp.float32) * s, 'b1': jnp.zeros((E, 2 * H), dtype=jnp.float32), 'W2': jax.random.normal(ks[2], (E, H, D), dtype=jnp.float32) * s, 'b2': jnp.zeros((E, D), dtype=jnp.float32), 'Wr': jax.random.normal(ks[3], (D, E), dtype=jnp.float32) * s, 'br': jnp.zeros((E,), dtype=jnp.float32)}
    _L0_ffn_all = _L0_ffn_setup()
    _L0_ffn_in = {k: v for k, v in _L0_ffn_all.items() if k in ('W1', 'b1', 'W2', 'b2', 'Wr', 'br')}
    del _L0_ffn_all

    def _L1_xattn_setup():
        import jax, jax.numpy as jnp
        import numpy as np
        HEADS = 8
        DIM_HEAD = 128
        ATTN_MATRIX_SCALE = 1.5
        SCALE = DIM_HEAD ** (-0.5)

        def _split_heads(t):
            b, n, _ = t.shape
            t = t.reshape(b, n, HEADS, DIM_HEAD)
            return t.transpose(2, 0, 1, 3).reshape(HEADS, b * n, DIM_HEAD)
        key = jax.random.key(seed)
        ks = jax.random.split(key, 7)
        b, n, m = (2, 512, 512)
        qd, cd, inner = (256, 192, HEADS * DIM_HEAD)
        x = jax.random.normal(ks[0], (b, n, qd), dtype=jnp.float32)
        context = jax.random.normal(ks[1], (b, m, cd), dtype=jnp.float32)
        Wq = jax.random.normal(ks[2], (qd, inner), dtype=jnp.float32) * qd ** (-0.5)
        Wk = jax.random.normal(ks[3], (cd, inner), dtype=jnp.float32) * cd ** (-0.5)
        Wv = jax.random.normal(ks[4], (cd, inner), dtype=jnp.float32) * cd ** (-0.5)
        Wout = jax.random.normal(ks[5], (inner, qd), dtype=jnp.float32) * inner ** (-0.5)
        bout = jnp.zeros((qd,), dtype=jnp.float32)
        return {'x': x, 'context': context, 'Wq': Wq, 'Wk': Wk, 'Wv': Wv, 'Wout': Wout, 'bout': bout}
    _L1_xattn_all = _L1_xattn_setup()
    _L1_xattn_in = {k: v for k, v in _L1_xattn_all.items() if k in ('Wq', 'Wk', 'Wv', 'Wout', 'bout')}
    del _L1_xattn_all

    def _L1_ffn_setup():
        import jax, jax.numpy as jnp
        import numpy as np
        B, S, DIM = (4, 1024, 256)
        BASE_COUPLING = 0.1
        NUM_CYCLES = 3

        def _gelu(x):
            return jax.nn.gelu(x, approximate=False)

        def _coupling_net(h, w1, b1, w2, b2, w3, b3, w4, b4):
            h = _gelu(h @ w1 + b1)
            h = _gelu(h @ w2 + b2)
            h = _gelu(h @ w3 + b3)
            return jax.nn.sigmoid(h @ w4 + b4)

        def _global_net(h, w1, b1, w2, b2, w3, b3):
            h = _gelu(h @ w1 + b1)
            h = _gelu(h @ w2 + b2)
            return jax.nn.sigmoid(h @ w3 + b3)

        def _twist(x):
            o_r, o_i, p_r, p_i = jnp.split(x, 4, axis=-1)
            return jnp.concatenate([p_r, -p_i, -o_r, o_i], axis=-1)
        key = jax.random.key(seed)
        ks = jax.random.split(key, 9)
        d = DIM

        def w(k, fan_in, fan_out):
            return jax.random.normal(k, (fan_in, fan_out), dtype=jnp.float32) / np.sqrt(fan_in).astype(np.float32)
        inp = {'x': jax.random.normal(ks[0], (B, S, d), dtype=jnp.float32)}
        cn_dims = [(d, d), (d, d // 2), (d // 2, d // 4), (d // 4, 1)]
        for i, (a, b) in enumerate(cn_dims):
            inp[f'cn_w{i + 1}'] = w(ks[1 + i], a, b)
            inp[f'cn_b{i + 1}'] = jnp.zeros((b,), dtype=jnp.float32)
        gc_dims = [(d, d // 2), (d // 2, d // 4), (d // 4, 1)]
        for i, (a, b) in enumerate(gc_dims):
            inp[f'gc_w{i + 1}'] = w(ks[5 + i], a, b)
            inp[f'gc_b{i + 1}'] = jnp.zeros((b,), dtype=jnp.float32)
        inp['adaptive_range'] = jnp.full((1,), 0.2, dtype=jnp.float32)
        return inp
    _L1_ffn_all = _L1_ffn_setup()
    _L1_ffn_in = {k: v for k, v in _L1_ffn_all.items() if k in ('cn_w1', 'cn_b1', 'cn_w2', 'cn_b2', 'cn_w3', 'cn_b3', 'cn_w4', 'cn_b4', 'gc_w1', 'gc_b1', 'gc_w2', 'gc_b2', 'gc_w3', 'gc_b3', 'adaptive_range')}
    del _L1_ffn_all
    return {'x': x, 'ctx_768': ctx_768, 'g_xattn': g_xattn, 'g_ffn': g_ffn, 'L0_xattn_Wq': _L0_xattn_in['Wq'], 'L0_xattn_Wk': _L0_xattn_in['Wk'], 'L0_xattn_Wv': _L0_xattn_in['Wv'], 'L0_xattn_Wo': _L0_xattn_in['Wo'], 'L0_xattn_bo': _L0_xattn_in['bo'], 'L0_ffn_W1': _L0_ffn_in['W1'], 'L0_ffn_b1': _L0_ffn_in['b1'], 'L0_ffn_W2': _L0_ffn_in['W2'], 'L0_ffn_b2': _L0_ffn_in['b2'], 'L0_ffn_Wr': _L0_ffn_in['Wr'], 'L0_ffn_br': _L0_ffn_in['br'], 'L1_xattn_Wq': _L1_xattn_in['Wq'], 'L1_xattn_Wk': _L1_xattn_in['Wk'], 'L1_xattn_Wv': _L1_xattn_in['Wv'], 'L1_xattn_Wout': _L1_xattn_in['Wout'], 'L1_xattn_bout': _L1_xattn_in['bout'], 'L1_ffn_cn_w1': _L1_ffn_in['cn_w1'], 'L1_ffn_cn_b1': _L1_ffn_in['cn_b1'], 'L1_ffn_cn_w2': _L1_ffn_in['cn_w2'], 'L1_ffn_cn_b2': _L1_ffn_in['cn_b2'], 'L1_ffn_cn_w3': _L1_ffn_in['cn_w3'], 'L1_ffn_cn_b3': _L1_ffn_in['cn_b3'], 'L1_ffn_cn_w4': _L1_ffn_in['cn_w4'], 'L1_ffn_cn_b4': _L1_ffn_in['cn_b4'], 'L1_ffn_gc_w1': _L1_ffn_in['gc_w1'], 'L1_ffn_gc_b1': _L1_ffn_in['gc_b1'], 'L1_ffn_gc_w2': _L1_ffn_in['gc_w2'], 'L1_ffn_gc_b2': _L1_ffn_in['gc_b2'], 'L1_ffn_gc_w3': _L1_ffn_in['gc_w3'], 'L1_ffn_gc_b3': _L1_ffn_in['gc_b3'], 'L1_ffn_adaptive_range': _L1_ffn_in['adaptive_range']}

def reference(x, ctx_768, g_xattn, g_ffn, L0_xattn_Wq, L0_xattn_Wk, L0_xattn_Wv, L0_xattn_Wo, L0_xattn_bo, L0_ffn_W1, L0_ffn_b1, L0_ffn_W2, L0_ffn_b2, L0_ffn_Wr, L0_ffn_br, L1_xattn_Wq, L1_xattn_Wk, L1_xattn_Wv, L1_xattn_Wout, L1_xattn_bout, L1_ffn_cn_w1, L1_ffn_cn_b1, L1_ffn_cn_w2, L1_ffn_cn_b2, L1_ffn_cn_w3, L1_ffn_cn_b3, L1_ffn_cn_w4, L1_ffn_cn_b4, L1_ffn_gc_w1, L1_ffn_gc_b1, L1_ffn_gc_w2, L1_ffn_gc_b2, L1_ffn_gc_w3, L1_ffn_gc_b3, L1_ffn_adaptive_range):
    import jax
    import jax.numpy as jnp

    def _L0_xattn_ref(x, context, Wq, Wk, Wv, Wo, bo):
        import jax, jax.numpy as jnp
        import numpy as np
        HEADS = 16
        DIM_HEAD = 64
        B, Nq, _ = x.shape
        Nk = context.shape[1]
        h, dh = (HEADS, DIM_HEAD)
        q = (x @ Wq).reshape(B, Nq, h, dh)
        k = (context @ Wk).reshape(B, Nk, h, dh)
        v = (context @ Wv).reshape(B, Nk, h, dh)
        scale = 1.0 / jnp.sqrt(jnp.asarray(dh, dtype=x.dtype))
        scores = jnp.einsum('bqhd,bkhd->bhqk', q, k) * scale
        attn = jax.nn.softmax(scores, axis=-1)
        out = jnp.einsum('bhqk,bkhd->bqhd', attn, v).reshape(B, Nq, h * dh)
        return out @ Wo + bo

    def _L0_ffn_ref(x, W1, b1, W2, b2, Wr, br):
        import jax, jax.numpy as jnp
        import numpy as np
        D = 256
        H = 512
        E = 8
        K = 2
        B, T = (4, 512)
        Bb, Tt, Dd = x.shape
        xf = x.reshape(-1, Dd)
        logits = xf @ Wr + br
        topk_val, topk_idx = jax.lax.top_k(logits, K)
        scores = jax.nn.softmax(topk_val, axis=-1)
        h = jnp.einsum('nd,edh->enh', xf, W1) + b1[:, None, :]
        a, g = jnp.split(h, 2, axis=-1)
        act = jax.nn.silu(a) * g
        out_e = jnp.einsum('enh,ehd->end', act, W2) + b2[:, None, :]
        out_ne = out_e.transpose(1, 0, 2)
        gathered = jnp.take_along_axis(out_ne, topk_idx[:, :, None], axis=1)
        out = jnp.sum(gathered * scores[:, :, None], axis=1)
        return out.reshape(Bb, Tt, Dd)

    def _L1_xattn_ref(x, context, Wq, Wk, Wv, Wout, bout):
        import jax, jax.numpy as jnp
        import numpy as np
        HEADS = 8
        DIM_HEAD = 128
        ATTN_MATRIX_SCALE = 1.5
        SCALE = DIM_HEAD ** (-0.5)

        def _split_heads(t):
            b, n, _ = t.shape
            t = t.reshape(b, n, HEADS, DIM_HEAD)
            return t.transpose(2, 0, 1, 3).reshape(HEADS, b * n, DIM_HEAD)
        b, n, _ = x.shape
        qh = _split_heads(jnp.einsum('bnq,qi->bni', x, Wq))
        kh = _split_heads(jnp.einsum('bmc,ci->bmi', context, Wk))
        vh = _split_heads(jnp.einsum('bmc,ci->bmi', context, Wv))
        sim = jnp.einsum('hid,hjd->hij', qh, kh) * SCALE
        mean = jnp.mean(sim, axis=-1, keepdims=True)
        sim = (sim - mean) * ATTN_MATRIX_SCALE + mean
        attn = jax.nn.softmax(sim, axis=-1)
        out = jnp.einsum('hij,hjd->hid', attn, vh)
        out = out.reshape(HEADS, b, n, DIM_HEAD).transpose(1, 2, 0, 3)
        out = out.reshape(b, n, HEADS * DIM_HEAD)
        return jnp.einsum('bni,iq->bnq', out, Wout) + bout

    def _L1_ffn_ref(x, cn_w1, cn_b1, cn_w2, cn_b2, cn_w3, cn_b3, cn_w4, cn_b4, gc_w1, gc_b1, gc_w2, gc_b2, gc_w3, gc_b3, adaptive_range):
        import jax, jax.numpy as jnp
        import numpy as np
        B, S, DIM = (4, 1024, 256)
        BASE_COUPLING = 0.1
        NUM_CYCLES = 3

        def _gelu(x):
            return jax.nn.gelu(x, approximate=False)

        def _coupling_net(h, w1, b1, w2, b2, w3, b3, w4, b4):
            h = _gelu(h @ w1 + b1)
            h = _gelu(h @ w2 + b2)
            h = _gelu(h @ w3 + b3)
            return jax.nn.sigmoid(h @ w4 + b4)

        def _global_net(h, w1, b1, w2, b2, w3, b3):
            h = _gelu(h @ w1 + b1)
            h = _gelu(h @ w2 + b2)
            return jax.nn.sigmoid(h @ w3 + b3)

        def _twist(x):
            o_r, o_i, p_r, p_i = jnp.split(x, 4, axis=-1)
            return jnp.concatenate([p_r, -p_i, -o_r, o_i], axis=-1)
        global_context = x.mean(axis=1, keepdims=True)
        gf = _global_net(global_context, gc_w1, gc_b1, gc_w2, gc_b2, gc_w3, gc_b3)
        out = x
        for _ in range(NUM_CYCLES):
            tf = _coupling_net(out, cn_w1, cn_b1, cn_w2, cn_b2, cn_w3, cn_b3, cn_w4, cn_b4)
            combined = 0.7 * gf + 0.3 * tf
            coupling = BASE_COUPLING + adaptive_range * (combined - 0.5) * 2.0
            out = out + coupling * _twist(out)
        return out
    x = x + jnp.tanh(g_xattn[0]) * _L0_xattn_ref(_layernorm(x, axis=-1), ctx_768, L0_xattn_Wq, L0_xattn_Wk, L0_xattn_Wv, L0_xattn_Wo, L0_xattn_bo)
    x = x + jnp.tanh(g_ffn[0]) * _L0_ffn_ref(_layernorm(x, axis=-1), L0_ffn_W1, L0_ffn_b1, L0_ffn_W2, L0_ffn_b2, L0_ffn_Wr, L0_ffn_br)
    x = x + jnp.tanh(g_xattn[1]) * _L1_xattn_ref(_layernorm(x, axis=-1), ctx_768, L1_xattn_Wq, L1_xattn_Wk, L1_xattn_Wv, L1_xattn_Wout, L1_xattn_bout)
    x = x + jnp.tanh(g_ffn[1]) * _L1_ffn_ref(_layernorm(x, axis=-1), L1_ffn_cn_w1, L1_ffn_cn_b1, L1_ffn_cn_w2, L1_ffn_cn_b2, L1_ffn_cn_w3, L1_ffn_cn_b3, L1_ffn_cn_w4, L1_ffn_cn_b4, L1_ffn_gc_w1, L1_ffn_gc_b1, L1_ffn_gc_w2, L1_ffn_gc_b2, L1_ffn_gc_w3, L1_ffn_gc_b3, L1_ffn_adaptive_range)
    return x

_drawn_inputs = setup_inputs


def setup_inputs(seed=0):
    import zlib

    import numpy as np

    out = dict(_drawn_inputs(seed))
    spreads = {'g_ffn': (-1.0, 0.2),
     'L0_ffn_b1': (0.0, 0.8),
     'L0_ffn_b2': (0.0, 0.1),
     'L0_ffn_br': (0.0, 0.1),
     'L1_xattn_bout': (0.0, 0.1),
     'L1_ffn_cn_b1': (0.0, 2.0),
     'L1_ffn_cn_b2': (0.0, 2.0),
     'L1_ffn_cn_b3': (0.0, 2.0),
     'L1_ffn_gc_b1': (0.0, 0.8),
     'L1_ffn_gc_b2': (0.0, 2.0)}
    factors = {'L0_xattn_bo': 6.989,
     'L0_ffn_W1': 3.952,
     'L0_ffn_W2': 3.932,
     'L1_ffn_cn_w1': 2.787,
     'L1_ffn_gc_w2': 4.708,
     'L1_ffn_gc_w3': 3.142}
    for name, (base, spread) in spreads.items():
        noise = np.random.default_rng([zlib.crc32(name.encode()), seed]).standard_normal(out[name].shape)
        drawn = base * np.exp(spread * noise) if base else spread * noise
        out[name] = jnp.asarray(drawn.astype(out[name].dtype))
    for name, factor in factors.items():
        out[name] = (out[name] * factor).astype(out[name].dtype)
    return out
```

```python
from contextlib import ExitStack

import numpy as np

import concourse.bass as bass
from concourse import mybir

F32 = mybir.dt.float32
U32 = mybir.dt.uint32
ALU = mybir.AluOpType
ACT = mybir.ActivationFunctionType
AX = mybir.AxisListType

P = 128
EPS = 1e-5


class Attention:

    def __init__(self, index, heads_per_step, keys, remainder_width, scale, bodies):
        self.index = index
        self.hs = heads_per_step
        self.dh = 256 // heads_per_step
        self.keys = keys
        self.rw = remainder_width
        self.chunks = 4 // heads_per_step
        self.rem = keys - 128 * self.chunks
        self.width = 128 * self.chunks + remainder_width
        self.scale = scale
        self.bodies = bodies
        self.batches = 2 if keys == 154 else 1
        self.score_cols = 308 + index


def flamingo(nc, t_in, out):
    B, S, D = t_in["x"].shape
    T = B * S
    NT = T // P
    DK = D // P
    _, NKEY, DC = t_in["ctx_768"].shape
    CK = DC // 2
    KEYS = B * NKEY
    INNER = t_in["L0_xattn_Wq"].shape[1]
    NC = INNER // P
    E, _, H2 = t_in["L0_ffn_W1"].shape
    H = H2 // 2
    HK = H // P

    L0 = Attention(0, 4, NKEY, 32, 64 ** -0.5,
                   [(0, 1, True, 0, 0, 0), (1, 3, False, 0, 0, 0), (3, 4, True, 0, 0, 1),
                    (4, 5, True, 0, 1, 1), (5, 7, False, 1, 1, 1), (7, 8, True, 1, 1, 1)])
    L1 = Attention(1, 2, KEYS, 64, 1.5 * 128 ** -0.5,
                   [(0, 1, True, 0, 0, 0), (1, 7, False, 0, 0, 0), (7, 8, True, 0, 0, 0)])
    STEPS = 4 * NT
    TOP = 2
    SLOTS = (TOP * T + E * (P - 1)) // P
    SLOTS += SLOTS % 2

    with ExitStack() as ctx:
        def sb(name, shape, dt=F32):
            return ctx.enter_context(nc.sbuf_tensor(name, shape, dt))

        sems = {}

        def sem(name):
            if name not in sems:
                sems[name] = ctx.enter_context(nc.semaphore(name))
            return sems[name]

        banks = ctx.enter_context(nc.psum_tensor("banks", [P, 8, 512], F32))
        x = sb("x", [P, NT, D])
        ident = sb("ident", [P, P])
        gates = sb("gates", [P, 4])
        stats = sb("stats", [P, NT, 6])
        mean_var = sb("mean_var", [P, NT, 2])
        std = sb("std", [P, NT])
        rstd = sb("rstd", [P, NT])
        xn = sb("xn", [P, D])
        x_biased = sb("x_biased", [P, 2, D])
        xT = sb("xT", [P, 2, DK, P])
        gated_bo = sb("gated_bo", [P, D])
        ctxT = sb("ctxT", [CK, 2, KEYS])
        ctx_rem1 = sb("ctx_rem1", [CK, 2, P])
        eps = sb("eps", [P, 1])
        BLK = 4 * P
        NB = T // BLK
        CYCLES = 3
        ones = sb("ones", [P, P])
        before = sb("before", [P, P])
        w1_region = sb("W1", [P, E * DK * H2])
        W1 = w1_region[:].rearrange("p (e k n) -> p e k n", e=E, k=DK)
        class Region:
            def __init__(self, name, size):
                self.buffer, self.at = sb(name, [P, size]), 0

            def part(self, n, pattern="p n -> p n", rows=P, dt=F32, **dims):
                view = self.buffer[0:rows, self.at:self.at + n]
                self.at += n
                if dt != F32:
                    view = view.bitcast(dt)
                return view.rearrange(pattern, **dims) if dims else view

        reg_a = Region("region_a", 2 * NC * 308 + 2 * NC * 3 * P + 6 * 640 + 4 * NC * P)
        K0 = reg_a.part(2 * NC * 308, "p (b c n) -> p b c n", b=2, c=NC)
        V = reg_a.part(2 * NC * 3 * P, "p (b c i n) -> p b c i n", b=2, c=NC, i=3)
        probs = reg_a.part(2 * 640, "p (r n) -> p r n", r=2)
        normed = reg_a.part(2 * 640, "p (r n) -> p r n", r=2)
        probsT = reg_a.part(2 * 640, "p (r n) -> p r n", r=2)
        q = reg_a.part(2 * NC * P, "p (r c n) -> p r c n", r=2, c=NC)
        oT = reg_a.part(2 * NC * P, "p (r c n) -> p r c n", r=2, c=NC)
        ctx_rem = q.rearrange("p r c n -> p (r c n)")[0:CK, 0:4 * P].rearrange("p (k b n) -> p k b n", k=2, b=2)
        ctx_rows = probsT.rearrange("p r n -> p (r n)")[:, 0:3 * DC].rearrange("p (r d) -> p r d", r=3)
        K1 = K0.rearrange("p b c n -> p (b c n)")[:, 0:NC * 309].rearrange("p (c n) -> p c n", c=NC)
        reg_a.at = 0
        b1 = reg_a.part(E * H2, "p (e n) -> p e n", e=E)
        W2 = reg_a.part(E * HK * D, "p (e k n) -> p e k n", e=E, k=HK)
        b2 = reg_a.part(E * D, "p (e n) -> p e n", e=E)
        y_pair = b2.rearrange("p e n -> p (e n)").rearrange("p (r i d) -> p r i d", r=4, i=2)
        reg_a.at = 0
        h1T = reg_a.part(NB * 2 * BLK, "p (j m n) -> p j m n", j=NB, m=2)
        h2T = reg_a.part(NB * BLK, "p (j n) -> p j n", j=NB)
        h3T = reg_a.part(NB * BLK, "p (j n) -> p j n", j=NB)
        twist = reg_a.part(4 * D * NB, "p (t d) -> p t d", d=D)

        reg_b = Region("region_b", 8704)
        Wk = reg_b.part(2 * INNER, "p (k n) -> p k n", rows=CK, k=2)
        Wv = reg_b.part(2 * INNER, "p (k n) -> p k n", rows=CK, k=2)
        Wq = reg_b.part(DK * INNER, "p (k n) -> p k n", k=DK)
        Wo = reg_b.part(NC * D, "p (c n) -> p c n", c=NC)
        reg_b.at = 0
        xn_all = reg_b.part(NT * D, "p (t d) -> p t d", t=NT)
        xg = reg_b.part(2 * D, "p (r d) -> p r d", r=2)
        xgT = reg_b.part(2 * D, "p (r k n) -> p r k n", r=2, k=DK)
        y_slot = reg_b.part(2 * D, "p (r d) -> p r d", r=2)
        a_act = reg_b.part(2 * H, "p (r n) -> p r n", r=2)
        g_act = reg_b.part(2 * H, "p (r n) -> p r n", r=2)
        actT = reg_b.part(2 * H, "p (r k n) -> p r k n", r=2, k=HK)

        at = [0]

        def late(n, pattern="p n -> p n", rows=P, **dims):
            view = w1_region[0:rows, at[0]:at[0] + n]
            at[0] += n
            return view.rearrange(pattern, **dims) if dims else view

        cur = late(NT * D, "p (t d) -> p t d", t=NT)
        curT = late(NB * DK * BLK, "p (j k n) -> p j k n", j=NB, k=DK)
        cw1 = late(DK * 256, "p (k n) -> p k n", k=DK)
        cw2 = late(2 * 128, "p (k n) -> p k n", k=2)
        cw3, cw4 = late(64), late(1, rows=64)
        cb1, cb2, cb3, cb4 = late(2), late(1), late(1, rows=64), late(1)
        gw1 = late(DK * 128, "p (k n) -> p k n", k=DK)
        gw2, gw3 = late(64), late(1, rows=64)
        gb1, gb2, gb3 = late(1), late(1, rows=64), late(1)
        reach = late(1)
        gw3_wide = late(P, rows=64)
        mean_sb = late(4, "p (k b) -> p k b", k=DK)
        g1, g2, g3 = late(2), late(2, rows=64), late(2)
        half_b4, half_gb3 = late(1), late(1)
        slope = late(2)
        level = late(4, "p (q b) -> p q b", q=2)
        level_part = late(2)
        tf = late(NT)
        coef = late(NT * 4, "p (t q) -> p t q", t=NT)

        Wr = sb("Wr", [P, DK, E])
        br = sb("br", [P, E])
        logits = sb("logits", [P, NT, E])
        top = sb("top", [P, NT, 8])
        top_at = sb("top_at", [P, NT, 8], U32)
        top_atf = sb("top_atf", [P, NT, TOP])
        chosen = sb("chosen", [P, TOP, NT, E])
        either = sb("either", [P, NT, E])
        totals = sb("totals", [P, NT, E])
        upto = sb("upto", [P, NT, E])
        place = sb("place", [P, NT, E])
        place_i = sb("place_i", [P, NT, E])
        slot_f = sb("slot_f", [P, TOP, NT])
        slot = sb("slot", [P, TOP, NT], U32)
        weight = sb("weight", [P, 4, NT])
        tiles_cmp = sb("tiles_cmp", [P, E, NT])
        tiles_of = sb("tiles_of", [P, E])
        tiles_end = sb("tiles_end", [P, E])
        tiles_base = sb("tiles_base", [P, E])
        iota_e = sb("iota_e", [P, E])
        iota_t = sb("iota_t", [P, NT])
        iota_s = sb("iota_s", [1, SLOTS])
        owner_cmp = xT.ap().rearrange("p r k n -> p (r k n)")[0:1, 0:SLOTS * E].rearrange("p (s e) -> p s e", s=SLOTS)
        owner_f = sb("owner_f", [1, SLOTS])
        owner = sb("owner", [1, SLOTS], mybir.dt.int32)
        zeros = x_biased[:, 0, :]
        x_slots = nc.dram_tensor("x_slots", [SLOTS * P, D], F32, kind="Internal").ap()
        y_slots = nc.dram_tensor("y_slots", [SLOTS * P, D], F32, kind="Internal").ap()

        negmax = sb("negmax", [P, 2, 4])
        bias1 = sb("bias1", [P, 2, 4])
        shifted = sb("shifted", [P, 2, 4])
        sums = sb("sums", [P, 2, 4])
        recip = sb("recip", [P, 2, 4])
        kmean = sb("kmean", [P, NC])

        scores = banks[:, 0:4, :].rearrange("p (r u) n -> p r u n", r=2)
        probsT_ps = banks[:, 4:6, :].rearrange("p u n -> p (u n)")
        o_ps = banks[:, 6, :]
        misc_ps = banks[:, 7, :]

        block = ctx.enter_context(nc.Block())

        def finals(eng, *names_counts):
            for name, count in names_counts:
                eng.wait_ge(sem(name), count)

        def load_attention(eng, layer):
            n = f"L{layer}_xattn_"
            wk, wv = (t_in[n + w].rearrange("(k p) n -> p k n", p=CK) for w in ("Wk", "Wv"))
            eng.dma_start(Wk[:], wk).then_inc(sem("wk_in"), 16)
            eng.dma_start(Wv[:], wv).then_inc(sem("wv_in"), 16)
            eng.dma_start(Wq[:], t_in[n + "Wq"].rearrange("(k p) n -> p k n", p=P)).then_inc(sem("wq_in"), 16)
            wo, bo = ("Wo", "bo") if layer == 0 else ("Wout", "bout")
            eng.dma_start(Wo[:], t_in[n + wo].rearrange("(k p) n -> p k n", p=P)).then_inc(sem("wo_in"), 16)
            eng.dma_start(gated_bo[:], t_in[n + bo].partition_broadcast(P)).then_inc(sem("bo_in"), 16)

        def kv_units(L):
            units = [("k", c, 0) for c in range(NC)]
            if L.index == 0:
                units += [("v", b, half) for b in range(2) for half in range(2)]
            else:
                units += [("v", chunk, half) for chunk in range(2) for half in range(2)]
            units += [("r", b, half) for b in range(L.batches) for half in range(2)]
            return units

        KV0 = len(kv_units(L0))

        def pe_kv(pe, L):
            base = KV0 * L.index
            pe.wait_ge(sem("wk_in"), 16 * (L.index + 1))
            for n, (kind, a, half) in enumerate(kv_units(L)):
                if n == NC:
                    pe.wait_ge(sem("wv_in"), 16 * (L.index + 1))
                    pe.wait_ge(sem("rem_ready"), 2)
                if n >= 4:
                    pe.wait_ge(sem("kv_sb"), base + n - 3)
                bank = banks[:, n % 4]
                for k in range(2):
                    if kind == "k":
                        o, l, r = bank[:, 0:KEYS], Wk[:, k, a * P:(a + 1) * P], ctxT[:, k, :]
                    else:
                        r = Wv[:, k, half * 512:(half + 1) * 512]
                        start = a * (NKEY if L.index == 0 else P)
                        l = ctxT[:, k, start:start + P] if kind == "v" else (
                            ctx_rem[:, k, a, :] if L.index == 0 else ctx_rem1[:, k, :])
                        o = bank
                    mm = pe.matmul(o, l, r, start=(k == 0), stop=(k == 1))
                mm.then_inc(sem("kv_ps"), 1)

        def dve_kv(dve, L):
            base = KV0 * L.index
            for n, (kind, a, half) in enumerate(kv_units(L)):
                dve.wait_ge(sem("kv_ps"), base + n + 1)
                bank = banks[:, n % 4]
                if kind == "k" and L.index == 0:
                    for i in range(2):
                        rows = slice(64 * i, 64 * i + 64)
                        last = dve.tensor_scalar_mul(K0[rows, :, a, i * NKEY:(i + 1) * NKEY],
                                                     bank[rows, 0:KEYS].rearrange("p (b n) -> p b n", b=2), L.scale)
                elif kind == "k":
                    last = dve.tensor_scalar(K1[:, a, 0:KEYS], bank[:, 0:KEYS], L.scale, 0.0, ALU.mult, ALU.add,
                                             accum_out=kmean[:, a:a + 1])
                elif kind == "v" and L.index == 0:
                    for i in range(2):
                        last = dve.tensor_copy(
                            V[:, a, half * 4:half * 4 + 4, i, i * 64:(i + 1) * 64],
                            bank.rearrange("p (c i n) -> p c i n", c=4, i=2)[:, :, i, :])
                elif kind == "v":
                    last = dve.tensor_copy(V[:, 0, half * 4:half * 4 + 4, a, :],
                                           bank.rearrange("p (c n) -> p c n", c=4))
                else:
                    for j in range(L.hs):
                        rows = slice(L.rw * j, L.rw * (j + 1))
                        blk = (2 * j) // L.hs
                        col = (j * L.dh) % P
                        for g in range(2):
                            last = dve.tensor_copy(
                                V[rows, a, half * 4 + 2 * g + blk, 2, col:col + L.dh],
                                bank[rows, (g * L.hs + j) * L.dh:(g * L.hs + j + 1) * L.dh])
                last.then_inc(sem("kv_sb"), 1)

        def bodies(eng, L, emit):
            for first, end, peeled, before, batch, after in L.bodies:
                if peeled:
                    emit(first, first == 0, end == NT // 2, before, batch, after)
                else:
                    with eng.Fori(first, end) as i:
                        emit(i, False, False, before, batch, after)

        def pe_scores(pe, L, s, g, r, b):
            for u in range(2):
                K = K0[:, b, 2 * g + u, :] if L.index == 0 else K1[:, 2 * g + u, :]
                mm = pe.matmul(scores[:, g % 2, u, 0:L.score_cols], q[:, r, 2 * g + u, :], K, start=True, stop=True)
            mm.then_inc(sem("s_ps"), 1)

        def pe_transpose_x(pe, src):
            for k in range(DK):
                mm = pe.transpose(misc_ps[:, k * P:(k + 1) * P], src[:, k * P:(k + 1) * P], ident[:])
            mm.then_inc(sem("xt_ps"), 1)

        def pe_q(pe, r, half):
            for c in range(4):
                for k in range(DK):
                    mm = pe.matmul(misc_ps[:, c * P:(c + 1) * P], Wq[:, k, (4 * half + c) * P:(4 * half + c + 1) * P],
                                   xT[:, r, k, :], start=(k == 0), stop=(k == DK - 1))
            mm.then_inc(sem("q_ps"), 1)

        def pe_probsT(pe, L, g):
            for m in range(5):
                mm = pe.transpose(probsT_ps[:, m * P:(m + 1) * P], normed[:, g % 2, m * P:(m + 1) * P], ident[:])
            mm.then_inc(sem("pt_ps"), 1)

        def pe_pv(pe, g, b):
            for u in range(2):
                for i in range(3):
                    m = 2 * u + i if i < 2 else 4
                    mm = pe.matmul(o_ps[:, u * P:(u + 1) * P], V[:, b, 2 * g + u, i, :],
                                   probsT[:, g % 2, m * P:(m + 1) * P], start=(i == 0), stop=(i == 2))
            mm.then_inc(sem("o_ps"), 1)

        def pe_out(pe, r):
            for c in range(NC):
                mm = pe.matmul(misc_ps[:, 0:D], oT[:, r, c, :], Wo[:, c, :], start=(c == 0), stop=(c == NC - 1))
            mm.then_inc(sem("y_ps"), 1)

        def pe_attention(pe, L):
            t0, s0 = NT * L.index, STEPS * L.index
            pe.wait_ge(sem("xn_ready"), t0 + 1)
            pe_transpose_x(pe, xn)
            pe.wait_ge(sem("wq_in"), 16 * (L.index + 1))
            for half in range(2):
                if half == 0:
                    pe.wait_ge(sem("xt_sb"), t0 + 1)
                else:
                    pe.wait_ge(sem("q_sb"), 2 * t0 + 1)
                pe_q(pe, 0, half)
            pe.wait_ge(sem("q_sb"), 2 * t0 + 1)
            pe.wait_ge(sem("kv_sb"), KV0 if L.index == 0 else KV0 + len(kv_units(L1)))
            if L.index == 1:
                pe.wait_ge(sem("kmean_done"), 1)
            pe_scores(pe, L, 0, 0, 0, 0)

            def emit(i, first, last, before, batch, after):
                for r in range(2):
                    t = 2 * i + r
                    t_first, t_last = first and r == 0, last and r == 1
                    for g in range(4):
                        s = 4 * t + g
                        if not (t_last and g == 3):
                            gn = (g + 1) % 4
                            if gn == 0:
                                pe.wait_ge(sem("q_sb"), 2 * (t0 + t) + 3)
                            elif gn == 2:
                                pe.wait_ge(sem("q_sb"), 2 * (t0 + t) + 2)
                            if not (t_first and g == 0):
                                pe.wait_ge(sem("p_exp"), s0 + s)
                            nb = after if (g == 3 and r == 1) else batch
                            pe_scores(pe, L, s + 1, gn, r if g < 3 else 1 - r, nb)
                        if not (t_first and g == 0):
                            pe.wait_ge(sem("p_norm"), s0 + s)
                            if not (t_first and g == 1):
                                pe.wait_ge(sem("pt_sb_act"), s0 + s - 1)
                                pe.wait_ge(sem("pt_sb_dve"), s0 + s - 1)
                            pe_probsT(pe, L, (g - 1) % 4)
                        if g == 0 and not t_last:
                            pe.wait_ge(sem("q_sb"), 2 * (t0 + t) + 2)
                            if not first:
                                pe.wait_ge(sem("y_done"), t0 + t - 1)
                            pe.wait_ge(sem("xn_ready"), t0 + t + 2)
                            pe_transpose_x(pe, xn)
                        if g == 1 and not t_last:
                            pe.wait_ge(sem("xt_sb"), t0 + t + 2)
                            pe_q(pe, 1 - r, 0)
                        if g == 2 and not t_last:
                            pe.wait_ge(sem("q_sb"), 2 * (t0 + t) + 3)
                            pe_q(pe, 1 - r, 1)
                        if g == 3 and not t_first:
                            if not t_last:
                                pe.wait_ge(sem("q_sb"), 2 * (t0 + t) + 4)
                            else:
                                pe.wait_ge(sem("y_done"), t0 + t - 1)
                            pe.wait_ge(sem("o_sb"), s0 + 4 * t)
                            pe_out(pe, 1 - r)
                        if not (t_first and g < 2):
                            pe.wait_ge(sem("pt_sb_act"), s0 + s - 1)
                            pe.wait_ge(sem("pt_sb_dve"), s0 + s - 1)
                            if not (t_first and g == 2):
                                pe.wait_ge(sem("o_sb"), s0 + s - 2)
                            pe_pv(pe, (g - 2) % 4, before if (g < 2 and r == 0) else batch)

            if L.index == 0:
                pe.wait_ge(sem("wo_in"), 16)
            else:
                pe.wait_ge(sem("wo_in"), 32)
            bodies(pe, L, emit)
            pe.wait_ge(sem("p_norm"), s0 + STEPS)
            pe.wait_ge(sem("pt_sb_act"), s0 + STEPS - 1)
            pe.wait_ge(sem("pt_sb_dve"), s0 + STEPS - 1)
            pe_probsT(pe, L, 3)
            for s in (STEPS - 2, STEPS - 1):
                pe.wait_ge(sem("pt_sb_act"), s0 + s + 1)
                pe.wait_ge(sem("pt_sb_dve"), s0 + s + 1)
                pe.wait_ge(sem("o_sb"), s0 + s)
                pe_pv(pe, s % 4, L.bodies[-1][4])
            pe.wait_ge(sem("o_sb"), s0 + STEPS)
            pe.wait_ge(sem("y_done"), t0 + NT - 1)
            pe_out(pe, 1)

        def dve_stats(dve, phase):
            if phase:
                dve.wait_ge(sem("mixed" if phase == 2 else "y_done"), 2 * NT if phase == 3 else NT)
            for t in range(NT):
                if phase == 0 and t == 0:
                    dve.wait_ge(sem("x_first"), 16)
                if phase == 0 and t == 4:
                    dve.wait_ge(sem("x_rest"), 16)
                dve.bn_stats(stats[:, t, :], x[:, t, :]).then_inc(sem("stats_done"), 1)
            for t in range(NT):
                dve.wait_ge(sem("stats_done"), phase * NT + t + 1)
                mv = dve.bn_aggr(mean_var[:, t, :], stats[:, t, :])
            mv.then_inc(sem("var_done"), 1)
            dve.wait_ge(sem("std_done"), phase + 1)
            dve.reciprocal(rstd[:], std[:]).then_inc(sem("rstd_done"), 1)
            dve.wait_ge(sem("rstd_done"), phase + 1)

        def act_std(act, phase):
            act.wait_ge(sem("var_done"), phase + 1)
            act.activation(std[:], mean_var[:, :, 1], ACT.Sqrt, bias=eps[:, 0:1]).then_inc(sem("std_done"), 1)

        def tile_of(buf, t):
            if isinstance(t, int):
                return buf[:, t, :]
            return buf[:, bass.ds(t, 1), :].rearrange("p a d -> p (a d)")

        def column_of(buf, t):
            return buf[:, t:t + 1] if isinstance(t, int) else buf[:, bass.ds(t, 1)]

        def dve_normalize(dve, t):
            dve.tensor_scalar(xn[:], tile_of(x, t), column_of(mean_var[:, :, 0], t), column_of(rstd, t),
                              ALU.subtract, ALU.mult).then_inc(sem("xn_ready"), 1)

        def dve_attention(dve, L):
            t0, s0 = NT * L.index, STEPS * L.index
            if L.index == 1:
                dve.wait_ge(sem("kv_sb"), KV0 + NC)
                dve.tensor_scalar_mul(K1[:, :, KEYS], kmean[:, :], -1.0 / (3 * KEYS)).then_inc(sem("kmean_done"), 1)
            dve_normalize(dve, 0)
            dve.wait_ge(sem("xt_ps"), t0 + 1)
            dve_normalize(dve, 1)

            def row_max(g, s):
                dve.wait_ge(sem("s_ps"), s0 + s + 1)
                if L.index == 0:
                    dve.tensor_reduce(negmax[:, g % 2, :].rearrange("p (u i) -> p u i", u=2),
                                      scores[:, g % 2, :, 0:KEYS].rearrange("p u (i n) -> p u i n", i=2),
                                      AX.X, ALU.max, negate=True).then_inc(sem("bias_ready"), 1)
                    return
                m = scores[:, g % 2, :, KEYS]
                dve.tensor_reduce(negmax[:, g % 2, 0:2], scores[:, g % 2, :, 0:KEYS], AX.X, ALU.max,
                                  negate=True).then_inc(sem("negmax_done"), 1)
                dve.wait_ge(sem("negmax_done"), s + 1)
                dve.tensor_tensor(shifted[:, g % 2, 0:2], negmax[:, g % 2, 0:2], m,
                                  ALU.subtract).then_inc(sem("shifted_done"), 1)
                dve.wait_ge(sem("shifted_done"), s + 1)
                dve.tensor_tensor(bias1[:, g % 2, 0:2], shifted[:, g % 2, 0:2], m, ALU.add).then_inc(sem("bias_ready"), 1)

            row_max(0, 0)

            def evacuate_probsT(s, parity):
                dve.wait_ge(sem("pt_ps"), s0 + s + 1)
                dve.tensor_copy(probsT[:, parity, 0:512], probsT_ps[:, 0:512]).then_inc(sem("pt_sb_dve"), 1)

            def evacuate_o(s, g, r):
                dve.wait_ge(sem("o_ps"), s0 + s + 1)
                dve.tensor_copy(oT[:, r, 2 * g:2 * g + 2, :],
                                o_ps[:, 0:2 * P].rearrange("p (u n) -> p u n", u=2)).then_inc(sem("o_sb"), 1)

            def add_y(t, r):
                dve.wait_ge(sem("y_ps"), t0 + t + 1)
                dve.wait_ge(sem("xb_ready"), t0 + t + 1)
                dve.scalar_tensor_tensor(tile_of(x, t), misc_ps[:, 0:D], gates[:, L.index:L.index + 1],
                                         x_biased[:, r, :], ALU.mult, ALU.add).then_inc(sem("y_done"), 1)

            def emit(i, first, last, before, batch, after):
                for r in range(2):
                    t = 2 * i + r
                    t_first, t_last = first and r == 0, last and r == 1
                    for g in range(4):
                        s = 4 * t + g
                        dve.wait_ge(sem("p_exp"), s0 + s + 1)
                        dve.reciprocal(recip[:, g % 2, 0:L.hs], sums[:, g % 2, 0:L.hs]).then_inc(sem("recip_ready"), 1)
                        if not (t_last and g == 3):
                            row_max((g + 1) % 4, s + 1)
                        if not (t_first and g == 0):
                            evacuate_probsT(s - 1, (g - 1) % 2)
                        if not (t_first and g < 2):
                            evacuate_o(s - 2, (g - 2) % 4, r if g >= 2 else 1 - r)
                        if g == 1 and not last:
                            dve.wait_ge(sem("xt_ps"), t0 + t + 2)
                            dve_normalize(dve, t + 2)
                        if g == 3 and not t_first:
                            add_y(t - 1, 1 - r)

            bodies(dve, L, emit)
            evacuate_probsT(STEPS - 1, 1)
            evacuate_o(STEPS - 2, 2, 1)
            evacuate_o(STEPS - 1, 3, 1)
            add_y(NT - 1, 1)

        def act_attention(act, L):
            t0, s0 = NT * L.index, STEPS * L.index

            def evacuate_xT(t, r):
                act.wait_ge(sem("xt_ps"), t0 + t + 1)
                act.copy(xT[:, r], misc_ps[:, 0:D].rearrange("p (k n) -> p k n", k=DK)).then_inc(sem("xt_sb"), 1)

            def evacuate_probsT(s, parity):
                act.wait_ge(sem("pt_ps"), s0 + s + 1)
                act.copy(probsT[:, parity, 512:640], probsT_ps[:, 512:640]).then_inc(sem("pt_sb_act"), 1)

            def evacuate_q(t, r, half):
                act.wait_ge(sem("q_ps"), 2 * (t0 + t) + half + 1)
                act.copy(q[:, r, 4 * half:4 * half + 4, :],
                         misc_ps.rearrange("p (c n) -> p c n", c=4)).then_inc(sem("q_sb"), 1)

            def exponentials(g, s):
                act.wait_ge(sem("bias_ready"), s0 + s + 1)
                bias = negmax if L.index == 0 else bias1
                pr = probs[:, g % 2, :].rearrange("p (j n) -> p j n", j=L.hs)
                for j in range(L.hs):
                    u, i = (j // 2, j % 2) if L.index == 0 else (j, 0)
                    e = act.activation(pr[:, j, 0:L.keys], scores[:, g % 2, u, i * L.keys:(i + 1) * L.keys], ACT.Exp,
                                       bias=bias[:, g % 2, j:j + 1], accum_out=sums[:, g % 2, j:j + 1])
                e.then_inc(sem("p_exp"), 1)

            evacuate_xT(0, 0)
            evacuate_q(0, 0, 0)
            evacuate_q(0, 0, 1)
            act.wait_ge(sem("pads_zero"), 1 + L.index)
            exponentials(0, 0)

            def emit(i, first, last, before, batch, after):
                for r in range(2):
                    t = 2 * i + r
                    t_first, t_last = first and r == 0, last and r == 1
                    for g in range(4):
                        s = 4 * t + g
                        if not (t_last and g == 3):
                            if not (t_first and g == 0):
                                act.wait_ge(sem("p_norm"), s0 + s)
                            exponentials((g + 1) % 4, s + 1)
                        if not (t_first and g == 0):
                            evacuate_probsT(s - 1, (g - 1) % 2)
                        if not t_last:
                            if g == 0:
                                evacuate_xT(t + 1, 1 - r)
                            if g == 1:
                                evacuate_q(t + 1, 1 - r, 0)
                            if g == 2:
                                evacuate_q(t + 1, 1 - r, 1)

            bodies(act, L, emit)
            evacuate_probsT(STEPS - 1, 1)

        def pool_attention(pool, L):
            t0, s0 = NT * L.index, STEPS * L.index

            def emit(i, first, last, before, batch, after):
                for r in range(2):
                    t = 2 * i + r
                    for g in range(4):
                        s = 4 * t + g
                        pool.wait_ge(sem("recip_ready"), s0 + s + 1)
                        if not (first and r == 0 and g < 2):
                            pool.wait_ge(sem("pt_ps"), s0 + s - 1)
                        pr = probs[:, g % 2, :].rearrange("p (j n) -> p j n", j=L.hs)
                        whole = normed[:, g % 2, 0:512].rearrange("p (j n) -> p j n", j=L.hs)
                        rest = normed[:, g % 2, 512:640].rearrange("p (j n) -> p j n", j=L.hs)
                        rc = recip[:, g % 2, 0:L.hs].unsqueeze(2)
                        split = L.chunks * P
                        pool.tensor_tensor(whole, pr[:, :, 0:split], rc.broadcast_to([P, L.hs, split]), ALU.mult)
                        pool.tensor_tensor(rest, pr[:, :, split:L.width], rc.broadcast_to([P, L.hs, L.rw]),
                                           ALU.mult).then_inc(sem("p_norm"), 1)
                        if g == 2:
                            if not first:
                                pool.wait_ge(sem("y_done"), t0 + t - 1)
                            pool.tensor_tensor(x_biased[:, r, :], tile_of(x, t), gated_bo[:],
                                               ALU.add).then_inc(sem("xb_ready"), 1)

            bodies(pool, L, emit)

        def pe_routing(pe):
            pe.wait_ge(sem("y_done"), NT)
            pe.wait_ge(sem("wr_in"), 32)
            with pe.Fori(0, NT // 2) as i:
                for r in range(2):
                    t = 2 * i + r
                    pe.wait_ge(sem("xe_ready"), t + 1)
                    for k in range(DK):
                        mm = pe.transpose(banks[:, 4 + r, k * P:(k + 1) * P], x_biased[:, r, k * P:(k + 1) * P],
                                          ident[:])
                    mm.then_inc(sem("xet_ps"), 1)
                    pe.wait_ge(sem("xet_sb"), t + 1)
                    for k in range(DK):
                        mm = pe.matmul(misc_ps[:, bass.ds(t * E, E)], xT[:, r, k, :], Wr[:, k, :],
                                       start=(k == 0), stop=(k == DK - 1), skip_group_check=True)
                    mm.then_inc(sem("logit_ps"), 1)
            pe.wait_ge(sem("either_ready"), 1)
            pe.matmul(banks[:, 4, 0:NT * E], before[:], either.rearrange("p t e -> p (t e)"), start=True, stop=True)
            pe.matmul(banks[:, 5, 0:NT * E], ones[:], either.rearrange("p t e -> p (t e)"), start=True, stop=True)\
                .then_inc(sem("rank_ps"), 1)

        def dve_routing(dve):
            steps = [0]

            def link(ins):
                steps[0] += 1
                ins.then_inc(sem("route_step"), 1)
                dve.wait_ge(sem("route_step"), steps[0])

            dve_stats(dve, 1)

            def normalize(i, wait_free):
                for r in range(2):
                    t = 2 * i + r
                    if wait_free:
                        dve.wait_ge(sem("xet_ps"), t - 1)
                        dve.wait_ge(sem("xe_kept"), t - 1)
                    dve.tensor_scalar(x_biased[:, r, :], tile_of(x, t), column_of(mean_var[:, :, 0], t),
                                      column_of(rstd, t), ALU.subtract, ALU.mult).then_inc(sem("xe_ready"), 1)

            normalize(0, False)
            with dve.Fori(1, NT // 2) as i:
                normalize(i, True)
            dve.wait_ge(sem("logit_ps"), NT)
            link(dve.tensor_tensor(logits[:], misc_ps[:, 0:NT * E].rearrange("p (t e) -> p t e", t=NT),
                                   br[:, :].unsqueeze(1).broadcast_to([P, NT, E]), ALU.add))
            for t in range(NT):
                last = dve.max(top[:, t, :], logits[:, t, :])
            link(last)
            for t in range(NT):
                last = dve.max_index(top_at[:, t, :], top[:, t, :], logits[:, t, :])
            link(last)
            dve.tensor_tensor(weight[:, 0, :], top[:, :, 1], top[:, :, 0], ALU.subtract).then_inc(sem("margin_ready"), 1)
            link(dve.tensor_copy(top_atf[:], top_at[:, :, 0:TOP]))
            for c in range(TOP):
                last = dve.tensor_tensor(chosen[:, c], iota_e[:].unsqueeze(1).broadcast_to([P, NT, E]),
                                         top_atf[:, :, c].unsqueeze(2).broadcast_to([P, NT, E]), ALU.is_equal)
            link(last)
            dve.tensor_tensor(either[:], chosen[:, 0], chosen[:, 1], ALU.add).then_inc(sem("either_ready"), 1)
            dve.wait_ge(sem("rank_ps"), 1)
            link(dve.tensor_copy(totals[:], banks[:, 5, 0:NT * E].rearrange("p (t e) -> p t e", t=NT)))
            for e in range(E):
                last = dve.tensor_tensor_scan(upto[:, :, e], ones[:, 0:NT], totals[:, :, e], 0.0, ALU.mult, ALU.add)
            link(last)
            link(dve.tensor_tensor(tiles_cmp[:], upto[:, NT - 1, :].unsqueeze(2).broadcast_to([P, E, NT]),
                                   iota_t[:].unsqueeze(1).broadcast_to([P, E, NT]), ALU.is_gt))
            link(dve.tensor_reduce(tiles_of[:], tiles_cmp[:], AX.X, ALU.add))
            link(dve.tensor_tensor_scan(tiles_end[:], ones[:, 0:E], tiles_of[:], 0.0, ALU.mult, ALU.add))
            link(dve.tensor_tensor(owner_cmp, iota_s[:].unsqueeze(2).broadcast_to([1, SLOTS, E]),
                                   tiles_end[0:1, :].unsqueeze(1).broadcast_to([1, SLOTS, E]), ALU.is_ge))
            link(dve.tensor_reduce(owner_f[:], owner_cmp, AX.X, ALU.add))
            dve.tensor_scalar(owner[:], owner_f[:], float(E - 1), None, ALU.min).then_inc(sem("owner_ready"), 1)
            link(dve.tensor_tensor(tiles_base[:], tiles_end[:], tiles_of[:], ALU.subtract))
            link(dve.tensor_tensor(place_i[:], upto[:], totals[:], ALU.subtract))
            link(dve.tensor_tensor(place[:], place_i[:], banks[:, 4, 0:NT * E].rearrange("p (t e) -> p t e", t=NT), ALU.add))
            link(dve.scalar_tensor_tensor(place_i[:], tiles_base[:].unsqueeze(1).broadcast_to([P, NT, E]), float(P),
                                          place[:], ALU.mult, ALU.add))
            for c in range(TOP):
                link(dve.tensor_tensor(place[:], chosen[:, c], place_i[:], ALU.mult))
                link(dve.tensor_reduce(slot_f[:, c, :], place[:], AX.X, ALU.add))
            dve.tensor_copy(slot[:], slot_f[:]).then_inc(sem("slot_ready"), 1)
            dve.wait_ge(sem("margin_exp"), 1)
            link(dve.tensor_scalar_add(weight[:, 2, :], weight[:, 1, :], 1.0))
            link(dve.reciprocal(weight[:, 0, :], weight[:, 2, :]))
            link(dve.tensor_scalar_mul(weight[:, 2, :], weight[:, 0, :], gates[:, 2:3]))
            dve.tensor_tensor(weight[:, 3, :], weight[:, 1, :], weight[:, 2, :], ALU.mult).then_inc(sem("weight_ready"), 1)

        def act_routing(act):
            act_std(act, 1)
            with act.Fori(0, NT // 2) as i:
                for r in range(2):
                    t = 2 * i + r
                    act.wait_ge(sem("xet_ps"), t + 1)
                    act.copy(xT[:, r], banks[:, 4 + r, 0:D].rearrange("p (k n) -> p k n", k=DK)).then_inc(sem("xet_sb"), 1)
            act.wait_ge(sem("margin_ready"), 1)
            act.activation(weight[:, 1, :], weight[:, 0, :], ACT.Exp).then_inc(sem("margin_exp"), 1)

        def pool_scatter(pool):
            pool.wait_ge(sem("y_done"), NT)
            with pool.Fori(0, NT // 2) as i:
                for r in range(2):
                    t = 2 * i + r
                    pool.wait_ge(sem("xe_ready"), t + 1)
                    pool.tensor_copy(tile_of(xn_all, t), x_biased[:, r, :]).then_inc(sem("xe_kept"), 1)
            pool.wait_ge(sem("xe_kept"), NT)
            pool.wait_ge(sem("slot_ready"), 1)
            pool.wait_ge(sem("zero_filled"), 16)
            for t in range(NT):
                for c in range(TOP):
                    pool.indirect_dma_start(out=x_slots, out_offset=bass.IndirectOffsetOnAxis(ap=slot[:, c, t:t + 1], axis=0),
                                            in_=xn_all[:, t, :], in_offset=None).then_inc(sem("scattered"), 16)

        def slot_bodies(eng, emit):
            emit(0, True, False)
            with eng.Fori(1, SLOTS // 2 - 1) as i:
                emit(i, False, False)
            emit(SLOTS // 2 - 1, False, True)

        def owner_of(eng, j):
            return eng.value_load(owner[0:1, j:j + 1] if isinstance(j, int) else owner[0:1, bass.ds(j, 1)],
                                  min_val=0, max_val=E - 1)

        def sp_experts(sp):
            xs = x_slots.rearrange("(j p) d -> p j d", p=P)
            ys = y_slots.rearrange("(j p) d -> p j d", p=P)
            sp.wait_ge(sem("scattered"), 16 * TOP * NT)
            for r in range(2):
                sp.dma_start(xg[:, r], xs[:, r]).then_inc(sem(f"xg_in{r}"), 16)

            def emit(i, first, last):
                for r in range(2):
                    j = 2 * i + r
                    if not last:
                        sp.wait_ge(sem("xgt_ps"), j + 1)
                        sp.dma_start(xg[:, r], tile_of(xs, j + 2)).then_inc(sem(f"xg_in{r}"), 16)
                    sp.wait_ge(sem("ey_sb"), j + 1)
                    sp.dma_start(tile_of(ys, j), y_slot[:, r]).then_inc(sem(f"ey_out{r}"), 16)

            slot_bodies(sp, emit)

        def pe_experts(pe):
            pe.wait_ge(sem("w1_in"), 16)
            pe.wait_ge(sem("owner_ready"), 1)
            pe.wait_ge(sem("slot_ready"), 1)

            def turn_x(j, i, r):
                pe.wait_ge(sem(f"xg_in{r}"), 16 * (i + 1))
                for k in range(DK):
                    mm = pe.transpose(misc_ps[:, k * P:(k + 1) * P], xg[:, r, k * P:(k + 1) * P], ident[:])
                mm.then_inc(sem("xgt_ps"), 1)

            def hidden(e, r, part):
                for k in range(DK):
                    w = W1[:, bass.ds(e, 1), k, part * H:(part + 1) * H].rearrange("p a n -> p (a n)")
                    mm = pe.matmul(banks[:, 2 * r + part, :], xgT[:, r, k, :], w, start=(k == 0), stop=(k == DK - 1))
                mm.then_inc(sem("hg_ps" if part else "ha_ps"), 1)

            turn_x(0, 0, 0)
            pe.wait_ge(sem("xgt_sb"), 1)
            turn_x(1, 0, 1)
            e = owner_of(pe, 0)
            hidden(e, 0, 0)
            hidden(e, 0, 1)
            pe.wait_ge(sem("w2_in"), 16)

            def emit(i, first, last):
                for r in range(2):
                    j = 2 * i + r
                    final = last and r == 1
                    if not final:
                        e_next = owner_of(pe, j + 1)
                        pe.wait_ge(sem("xgt_sb"), j + 2)
                        if not (first and r == 0):
                            pe.wait_ge(sem("a_read"), j)
                        hidden(e_next, 1 - r, 0)
                    pe.wait_ge(sem("act_ready"), j + 1)
                    if not first:
                        pe.wait_ge(sem("at_sb"), j - 1)
                    for k in range(HK):
                        mm = pe.transpose(banks[:, 4 + r, k * P:(k + 1) * P], a_act[:, r, k * P:(k + 1) * P], ident[:])
                    mm.then_inc(sem("at_ps"), 1)
                    if not final:
                        if not (first and r == 0):
                            pe.wait_ge(sem("g_read"), j)
                        hidden(e_next, 1 - r, 1)
                    if not last:
                        turn_x(j + 2, i + 1, r)
                    e = owner_of(pe, j)
                    pe.wait_ge(sem("at_sb"), j + 1)
                    if not (first and r == 0):
                        pe.wait_ge(sem("ey_sb"), j)
                    for k in range(HK):
                        w = W2[:, bass.ds(e, 1), k, :].rearrange("p a n -> p (a n)")
                        mm = pe.matmul(o_ps[:, 0:D], actT[:, r, k, :], w, start=(k == 0), stop=(k == HK - 1))
                    mm.then_inc(sem("ey_ps"), 1)

            slot_bodies(pe, emit)

        def act_experts(act):
            def evacuate_x(j, r):
                act.wait_ge(sem("xgt_ps"), j + 1)
                act.copy(xgT[:, r], misc_ps[:, 0:D].rearrange("p (k n) -> p k n", k=DK)).then_inc(sem("xgt_sb"), 1)

            def silu(j, r):
                act.wait_ge(sem("a_read"), j + 1)
                act.activation(a_act[:, r, :], a_act[:, r, :], ACT.Silu).then_inc(sem("silu_done"), 1)

            evacuate_x(0, 0)
            evacuate_x(1, 1)
            silu(0, 0)

            def emit(i, first, last):
                for r in range(2):
                    j = 2 * i + r
                    act.wait_ge(sem("at_ps"), j + 1)
                    if not first:
                        act.wait_ge(sem("ey_ps"), j - 1)
                    act.copy(actT[:, r], banks[:, 4 + r, :].rearrange("p (k n) -> p k n", k=HK)).then_inc(sem("at_sb"), 1)
                    if not (last and r == 1):
                        silu(j + 1, 1 - r)
                    if not last:
                        evacuate_x(j + 2, r)

            slot_bodies(act, emit)

        def dve_experts(dve):
            dve.wait_ge(sem("owner_ready"), 1)
            dve.wait_ge(sem("b12_in"), 32)

            def inputs(j, r, wait_free):
                e = owner_of(dve, j)
                for part, buf, ps, read in ((0, a_act, "ha_ps", "a_read"), (1, g_act, "hg_ps", "g_read")):
                    dve.wait_ge(sem(ps), j + 1)
                    if wait_free:
                        if part == 0:
                            dve.wait_ge(sem("at_ps"), j - 1)
                        else:
                            dve.wait_ge(sem("act_ready"), j - 1)
                    dve.tensor_tensor(buf[:, r, :], banks[:, 2 * r + part, :],
                                      b1[:, bass.ds(e, 1), part * H:(part + 1) * H].rearrange("p a n -> p (a n)"),
                                      ALU.add).then_inc(sem(read), 1)

            inputs(0, 0, False)

            def emit(i, first, last):
                for r in range(2):
                    j = 2 * i + r
                    if not (last and r == 1):
                        inputs(j + 1, 1 - r, not (first and r == 0))
                    e = owner_of(dve, j)
                    dve.wait_ge(sem("ey_ps"), j + 1)
                    if not first:
                        dve.wait_ge(sem(f"ey_out{r}"), 16 * i)
                    dve.tensor_tensor(y_slot[:, r], o_ps[:, 0:D], b2[:, bass.ds(e, 1), :].rearrange("p a n -> p (a n)"),
                                      ALU.add).then_inc(sem("ey_sb"), 1)

            slot_bodies(dve, emit)

        def pool_experts(pool):
            def emit(i, first, last):
                for r in range(2):
                    j = 2 * i + r
                    pool.wait_ge(sem("silu_done"), j + 1)
                    pool.wait_ge(sem("g_read"), j + 1)
                    pool.tensor_tensor(a_act[:, r, :], a_act[:, r, :], g_act[:, r, :], ALU.mult).then_inc(sem("act_ready"), 1)

            slot_bodies(pool, emit)

        def pool_gather(pool):
            for r in range(2):
                pool.wait_ge(sem(f"ey_out{r}"), 16 * (SLOTS // 2))
            for t in range(NT):
                if t >= 4:
                    pool.wait_ge(sem("mixed"), t - 3)
                for c in range(TOP):
                    pool.indirect_dma_start(out=y_pair[:, t % 4, c, :], out_offset=None, in_=y_slots,
                                            in_offset=bass.IndirectOffsetOnAxis(ap=slot[:, c, t:t + 1], axis=0))\
                        .then_inc(sem(f"gathered{t % 4}"), 16)

        def dve_mix(dve):
            dve.wait_ge(sem("weight_ready"), 1)
            for t in range(NT):
                dve.wait_ge(sem(f"gathered{t % 4}"), 32 * (t // 4 + 1))
                for c in range(TOP):
                    last = dve.scalar_tensor_tensor(x[:, t, :], y_pair[:, t % 4, c, :], weight[:, 2 + c, t:t + 1],
                                                    x[:, t, :], ALU.mult, ALU.add)
                    if c == 0:
                        last.then_inc(sem("mixed_first"), 1)
                        dve.wait_ge(sem("mixed_first"), t + 1)
                last.then_inc(sem("mixed"), 1)

        def load_coupling(eng):
            n = "L1_ffn_"
            def ld(dst, src):
                eng.dma_start(dst, src).then_inc(sem("coupling_in"), 16)
            ld(cw1, t_in[n + "cn_w1"].rearrange("(k p) n -> p k n", p=P))
            ld(cw2, t_in[n + "cn_w2"].rearrange("(k p) n -> p k n", p=P))
            ld(cw3, t_in[n + "cn_w3"])
            ld(cw4, t_in[n + "cn_w4"])
            ld(gw1, t_in[n + "gc_w1"].rearrange("(k p) n -> p k n", p=P))
            ld(gw2, t_in[n + "gc_w2"])
            ld(gw3, t_in[n + "gc_w3"])
            for m in range(2):
                ld(cb1[:, m:m + 1], t_in[n + "cn_b1"][m * P:(m + 1) * P].unsqueeze(1))
            for dst, src in ((cb2, "cn_b2"), (cb3, "cn_b3"), (gb1, "gc_b1"), (gb2, "gc_b2")):
                ld(dst, t_in[n + src].unsqueeze(1))
            for dst, src in ((cb4, "cn_b4"), (gb3, "gc_b3"), (reach, "adaptive_range")):
                ld(dst, t_in[n + src].partition_broadcast(P))

        LOADS = 16

        def pe_coupling(pe):
            pe.wait_ge(sem("cur_ready"), NB)
            pe.wait_ge(sem("coupling_in"), 16 * LOADS)
            for k in range(DK):
                for b in range(B):
                    for t in range(NT // B):
                        mm = pe.matmul(banks[:, 0, 2 * k + b:2 * k + b + 1], cur[:, b * NT // B + t, k * P:(k + 1) * P],
                                       ones[:, 0:1], start=(t == 0), stop=(t == NT // B - 1))
            mm.then_inc(sem("mean_ps"), 1)
            pe.wait_ge(sem("mean_sb"), 1)
            for k in range(DK):
                mm = pe.matmul(banks[:, 1, 0:2], gw1[:, k, :], mean_sb[:, k, :], start=(k == 0), stop=(k == DK - 1))
            mm.then_inc(sem("g_ps"), 1)
            pe.wait_ge(sem("g_sb"), 1)
            pe.matmul(banks[0:64, 2, 0:2], gw2, g1, start=True, stop=True).then_inc(sem("g_ps"), 1)
            pe.wait_ge(sem("g_sb"), 2)
            pe.wait_ge(sem("gw3_wide_ready"), 1)
            pe.matmul(banks[:, 3, 0:2], gw3_wide, g2, start=True, stop=True).then_inc(sem("g_ps"), 1)
            pe.wait_ge(sem("g_sb"), 3)

            with pe.Fori(0, CYCLES) as c:
                for j in range(NB):
                    pe.wait_ge(sem("cur_ready"), NB * c + j + 1)
                    for k in range(DK):
                        for t in range(4):
                            mm = pe.transpose(banks[:, 2 * j + k, t * P:(t + 1) * P],
                                              cur[:, 4 * j + t, k * P:(k + 1) * P], ident[:])
                    mm.then_inc(sem("turn_ps"), 1)
                for j in range(NB):
                    pe.wait_ge(sem("turn_sb"), NB * c + j + 1)
                    for m in range(2):
                        for k in range(DK):
                            mm = pe.matmul(banks[:, 2 * j + m, :], cw1[:, k, m * P:(m + 1) * P], curT[:, j, k, :],
                                           start=(k == 0), stop=(k == DK - 1))
                    mm.then_inc(sem("l1_ps"), 1)
                for j in range(NB):
                    pe.wait_ge(sem("l1_sb"), NB * c + j + 1)
                    for k in range(2):
                        mm = pe.matmul(banks[:, 2 * j, :], cw2[:, k, :], h1T[:, j, k, :], start=(k == 0), stop=(k == 1))
                    mm.then_inc(sem("l2_ps"), 1)
                for j in range(NB):
                    pe.wait_ge(sem("l2_sb"), NB * c + j + 1)
                    pe.matmul(banks[0:64, 2 * j + 1, :], cw3, h2T[:, j, :], start=True, stop=True).then_inc(sem("l3_ps"), 1)
                for j in range(NB):
                    pe.wait_ge(sem("l3_sb"), NB * c + j + 1)
                    for t in range(4):
                        mm = pe.matmul(banks[:, 2 * j, t:t + 1], h3T[0:64, j, t * P:(t + 1) * P], cw4, start=True, stop=True)
                    mm.then_inc(sem("l4_ps"), 1)

        def act_coupling(act):
            act.wait_ge(sem("coupling_in"), 16 * LOADS)
            act.wait_ge(sem("halves_ready"), 1)
            for n, (dst, src, bias) in enumerate(((g1, banks[:, 1, 0:2], gb1), (g2, banks[0:64, 2, 0:2], gb2))):
                act.wait_ge(sem("g_ps"), n + 1)
                act.activation(dst, src, ACT.Gelu, bias=bias).then_inc(sem("g_sb"), 1)
            act.wait_ge(sem("g_ps"), 3)
            act.activation(g3, banks[:, 3, 0:2], ACT.Tanh, bias=half_gb3, scale=0.5).then_inc(sem("g_sb"), 1)
            with act.Fori(0, CYCLES) as c:
                for j in range(NB):
                    act.wait_ge(sem("l1_ps"), NB * c + j + 1)
                    for m in range(2):
                        a = act.activation(h1T[:, j, m, :], banks[:, 2 * j + m, :], ACT.Gelu, bias=cb1[:, m:m + 1])
                    a.then_inc(sem("l1_sb"), 1)
                for j in range(NB):
                    act.wait_ge(sem("l2_ps"), NB * c + j + 1)
                    act.activation(h2T[:, j, :], banks[:, 2 * j, :], ACT.Gelu, bias=cb2).then_inc(sem("l2_sb"), 1)
                for j in range(NB):
                    act.wait_ge(sem("l3_ps"), NB * c + j + 1)
                    act.activation(h3T[0:64, j, :], banks[0:64, 2 * j + 1, :], ACT.Gelu, bias=cb3).then_inc(sem("l3_sb"), 1)
                for j in range(NB):
                    act.wait_ge(sem("l4_ps"), NB * c + j + 1)
                    act.activation(tf[:, 4 * j:4 * j + 4], banks[:, 2 * j, 0:4], ACT.Tanh, bias=half_b4,
                                   scale=0.5).then_inc(sem("tf_ready"), 1)

        def dve_coupling(dve):
            dve.wait_ge(sem("coupling_in"), 16 * LOADS)
            dve.tensor_scalar_mul(half_b4, cb4, 0.5)
            dve.tensor_scalar_mul(half_gb3, gb3, 0.5).then_inc(sem("halves_ready"), 1)
            dve.tensor_scalar_mul(slope[:, 0:1], reach, 0.3)
            dve.tensor_scalar_mul(slope[:, 1:2], reach, -0.3)
            dve.tensor_copy(gw3_wide, gw3.broadcast_to([64, P])).then_inc(sem("gw3_wide_ready"), 1)
            dve_stats(dve, 3)
            with dve.Fori(0, NB) as j:
                for t in range(4):
                    n = dve.tensor_scalar(tile_of(cur, 4 * j + t), tile_of(x, 4 * j + t),
                                          column_of(mean_var[:, :, 0], 4 * j + t), column_of(rstd, 4 * j + t),
                                          ALU.subtract, ALU.mult)
                n.then_inc(sem("cur_ready"), 1)
            dve.wait_ge(sem("mean_ps"), 1)
            dve.tensor_scalar_mul(mean_sb, banks[:, 0, 0:4].rearrange("p (k b) -> p k b", k=DK), 1.0 / S)\
                .then_inc(sem("mean_sb"), 1)
            dve.wait_ge(sem("g_sb"), 3)
            dve.tensor_scalar(level_part, g3, reach, 0.7, ALU.mult, ALU.mult).then_inc(sem("level_step"), 1)
            dve.wait_ge(sem("level_step"), 1)
            dve.tensor_scalar(level[:, 0, :], level_part, 1.0, 0.1, ALU.mult, ALU.add)
            dve.tensor_scalar(level[:, 1, :], level_part, -1.0, -0.1, ALU.mult, ALU.add).then_inc(sem("level_step"), 1)
            dve.wait_ge(sem("level_step"), 2)
            with dve.Fori(0, CYCLES) as c:
                for j in range(NB):
                    dve.wait_ge(sem("turn_ps"), NB * c + j + 1)
                    dve.tensor_copy(curT[:, j], banks[:, 2 * j:2 * j + 2, :]).then_inc(sem("turn_sb"), 1)
                for j in range(NB):
                    b = j // (NB // B)
                    tiles = slice(4 * j, 4 * j + 4)
                    dve.wait_ge(sem("tf_ready"), NB * c + j + 1)
                    t2 = tf[:, tiles].unsqueeze(2).broadcast_to([P, 4, 2])
                    dve.tensor_scalar(coef[:, tiles, 0:4:3], t2, slope[:, 0:1], level[:, 0, b:b + 1], ALU.mult, ALU.add)
                    dve.tensor_scalar(coef[:, tiles, 1:3], t2, slope[:, 1:2], level[:, 1, b:b + 1], ALU.mult, ALU.add)\
                        .then_inc(sem("coef_ready"), 1)
                for j in range(NB):
                    tiles = slice(4 * j, 4 * j + 4)
                    dve.wait_ge(sem("twist_ready"), NB * c + j + 1)
                    dve.tensor_tensor(cur[:, tiles, :], cur[:, tiles, :], twist[:, tiles, :], ALU.add)\
                        .then_inc(sem("cur_ready"), 1)
            for j in range(NB):
                tiles = slice(4 * j, 4 * j + 4)
                dve.wait_ge(sem("cur_ready"), NB * CYCLES + j + 1)
                dve.scalar_tensor_tensor(x[:, tiles, :], cur[:, tiles, :], gates[:, 3:4], x[:, tiles, :],
                                         ALU.mult, ALU.add).then_inc(sem("x_final"), 1)

        def pool_coupling(pool):
            with pool.Fori(0, CYCLES) as c:
                for j in range(NB):
                    tiles = slice(4 * j, 4 * j + 4)
                    pool.wait_ge(sem("coef_ready"), NB * c + j + 1)
                    for h in range(2):
                        src = slice(128, 256) if h == 0 else slice(0, 128)
                        p = pool.tensor_tensor(
                            twist[:, tiles, h * 128:(h + 1) * 128].rearrange("p t (s n) -> p t s n", s=2),
                            cur[:, tiles, src].rearrange("p t (s n) -> p t s n", s=2),
                            coef[:, tiles, 2 * h:2 * h + 2].unsqueeze(3).broadcast_to([P, 4, 2, 64]), ALU.mult)
                    p.then_inc(sem("twist_ready"), 1)

        @block.sync
        def _(sp):
            xs = t_in["x"].rearrange("b s d -> (b s) d").rearrange("(t p) d -> p t d", p=P)
            sp.dma_start(x[:, 0:4], xs[:, 0:4]).then_inc(sem("x_first"), 16)
            c2 = t_in["ctx_768"].rearrange("b s d -> (b s) d")
            sp.dma_start(ctx_rows[:, 0:2], c2[0:256].rearrange("(r p) d -> p r d", p=P)).then_inc(sem("ctx_in"), 16)
            sp.dma_start(ctx_rows[0:KEYS - 256, 2], c2[256:KEYS]).then_inc(sem("ctx_in"), 16)
            for name, g in (("g_xattn", 0), ("g_ffn", 2)):
                sp.dma_start(gates[:, g:g + 2], t_in[name].partition_broadcast(P)).then_inc(sem("gates_in"), 16)
            sp.dma_start(x[:, 4:NT], xs[:, 4:NT]).then_inc(sem("x_rest"), 16)
            load_attention(sp, 0)
            sp.dma_start(Wr[:], t_in["L0_ffn_Wr"].rearrange("(k p) e -> p k e", p=P)).then_inc(sem("wr_in"), 16)
            sp.dma_start(br[:], t_in["L0_ffn_br"].partition_broadcast(P)).then_inc(sem("wr_in"), 16)
            sp.wait_ge(sem("zeros_ready"), 1)
            sp.dma_start(x_slots.rearrange("(j p) d -> p j d", p=P),
                         zeros.unsqueeze(1).broadcast_to([P, SLOTS, D])).then_inc(sem("zero_filled"), 16)
            sp.dma_start(W1, t_in["L0_ffn_W1"].rearrange("e (k p) n -> p e k n", p=P)).then_inc(sem("w1_in"), 16)
            sp.wait_ge(sem("y_done"), NT)
            sp.dma_start(b1[:], t_in["L0_ffn_b1"].rearrange("e n -> (e n)").partition_broadcast(P)
                         .rearrange("p (e n) -> p e n", e=E)).then_inc(sem("b12_in"), 16)
            sp.dma_start(b2[:], t_in["L0_ffn_b2"].rearrange("e n -> (e n)").partition_broadcast(P)
                         .rearrange("p (e n) -> p e n", e=E)).then_inc(sem("b12_in"), 16)
            sp.dma_start(W2[:], t_in["L0_ffn_W2"].rearrange("e (k p) n -> p e k n", p=P)).then_inc(sem("w2_in"), 16)
            sp_experts(sp)
            for r in range(2):
                sp.wait_ge(sem(f"ey_out{r}"), 16 * (SLOTS // 2))
            load_attention(sp, 1)
            load_coupling(sp)
            outs = out.rearrange("b s d -> (b s) d").rearrange("(t p) d -> p t d", p=P)
            for j in range(NB):
                sp.wait_ge(sem("x_final"), j + 1)
                sp.dma_start(outs[:, 4 * j:4 * j + 4], x[:, 4 * j:4 * j + 4]).then_inc(sem("stored"), 16)
            sp.wait_ge(sem("stored"), 16 * NB)

        @block.gpsimd
        def _(pool):
            pool.memset(ident[:], 0.0).then_inc(sem("ident_zero"), 1)
            pool.memset(ones[:], 1.0).then_inc(sem("ones_ready"), 1)
            pool.memset(zeros, 0.0).then_inc(sem("zeros_ready"), 1)
            pool.iota(iota_e[:], [[1, E]], base=0, channel_multiplier=0, allow_small_or_imprecise_dtypes=True)
            pool.iota(iota_t[:], [[P, NT]], base=0, channel_multiplier=0, allow_small_or_imprecise_dtypes=True)
            pool.iota(iota_s[:], [[1, SLOTS]], base=0, channel_multiplier=0, allow_small_or_imprecise_dtypes=True)\
                .then_inc(sem("iota_ready"), 1)
            pool.wait_ge(sem("ones_ready"), 1)
            pool.affine_select(out=before[:], in_=ones[:], compare_op=ALU.is_gt, fill=0.0, base=0,
                               pattern=[[1, P]], channel_multiplier=-1).then_inc(sem("before_ready"), 1)
            pool.memset(eps[:], EPS).then_inc(sem("eps_ready"), 1)
            pool.memset(ctx_rem, 0.0)
            pool.memset(ctx_rem1[:], 0.0).then_inc(sem("rem_zero"), 1)
            pool.wait_ge(sem("ident_zero"), 1)
            pool.affine_select(out=ident[:], in_=ident[:], compare_op=ALU.not_equal, fill=1.0, base=0,
                               pattern=[[-1, P]], channel_multiplier=1).then_inc(sem("ident_ready"), 1)
            pool.memset(K0, 0.0)
            pool.memset(V, 0.0).then_inc(sem("kv_zero"), 1)
            pool.memset(probs, 0.0).then_inc(sem("pads_zero"), 1)
            pool.wait_ge(sem("gates_ready"), 1)
            pool.wait_ge(sem("bo_in"), 16)
            pool.tensor_tensor(gated_bo[:], gated_bo[:], gates[:, 0:1].broadcast_to([P, D]), ALU.mult)\
                .then_inc(sem("gbo_ready"), 1)
            pool.wait_ge(sem("gbo_ready"), 1)
            pool.wait_ge(sem("zero_filled"), 16)
            pool_attention(pool, L0)
            pool_scatter(pool)
            pool_experts(pool)
            pool.wait_ge(sem("ey_sb"), SLOTS)
            pool.memset(V[:, 0], 0.0).then_inc(sem("kv_zero"), 1)
            pool_gather(pool)
            pool.memset(probs, 0.0).then_inc(sem("pads_zero"), 1)
            pool.wait_ge(sem("bo_in"), 32)
            pool.tensor_tensor(gated_bo[:], gated_bo[:], gates[:, 1:2].broadcast_to([P, D]), ALU.mult)\
                .then_inc(sem("gbo_ready"), 1)
            pool.wait_ge(sem("gbo_ready"), 2)
            pool_attention(pool, L1)
            pool_coupling(pool)

        @block.scalar
        def _(act):
            act.wait_ge(sem("gates_in"), 32)
            act.activation(gates[:], gates[:], ACT.Tanh).then_inc(sem("gates_ready"), 1)
            act.wait_ge(sem("eps_ready"), 1)
            act_std(act, 0)
            act_attention(act, L0)
            act_routing(act)
            act_experts(act)
            act_std(act, 2)
            act_attention(act, L1)
            act_std(act, 3)
            act_coupling(act)

        @block.vector
        def _(dve):
            dve.wait_ge(sem("ctxT_ps"), 1)
            dve.tensor_copy(ctxT[:, :, :], banks[0:CK, 0:2, 0:KEYS]).then_inc(sem("ctxT_ready"), 1)
            dve.wait_ge(sem("ctxT_ready"), 1)
            dve.wait_ge(sem("rem_zero"), 1)
            for j in range(4):
                for k in range(2):
                    last = dve.tensor_copy(ctx_rem[:, k, :, j * 32:j * 32 + NKEY - P],
                                           ctxT[:, k, :].rearrange("p (b n) -> p b n", b=2)[:, :, P:NKEY])
            last.then_inc(sem("rem_ready"), 1)
            for j in range(2):
                last = dve.tensor_copy(ctx_rem1[:, :, j * 64:j * 64 + KEYS - 256], ctxT[:, :, 256:KEYS])
            last.then_inc(sem("rem_ready"), 1)
            dve.wait_ge(sem("kv_zero"), 1)
            dve_kv(dve, L0)
            dve_stats(dve, 0)
            dve_attention(dve, L0)
            dve.wait_ge(sem("iota_ready"), 1)
            dve_routing(dve)
            dve_experts(dve)
            dve.wait_ge(sem("kv_zero"), 2)
            dve_kv(dve, L1)
            dve_mix(dve)
            dve_stats(dve, 2)
            dve_attention(dve, L1)
            dve_coupling(dve)

        @block.tensor
        def _(pe):
            pe.wait_ge(sem("ctx_in"), 32)
            pe.wait_ge(sem("ident_ready"), 1)
            for k in range(2):
                for r in range(3):
                    n = P if r < 2 else KEYS - 256
                    mm = pe.transpose(banks[0:CK, k, r * P:r * P + n], ctx_rows[0:n, r, k * CK:(k + 1) * CK],
                                      ident[0:n, 0:n])
            mm.then_inc(sem("ctxT_ps"), 1)
            pe.wait_ge(sem("ctxT_ready"), 1)
            pe_kv(pe, L0)
            pe_attention(pe, L0)
            pe_routing(pe)
            pe_experts(pe)
            pe_kv(pe, L1)
            pe_attention(pe, L1)
            pe_coupling(pe)


_INS = ["x", "ctx_768", "g_xattn", "g_ffn"] + [f"L0_xattn_{n}" for n in ("Wq", "Wk", "Wv", "Wo", "bo")] \
    + [f"L0_ffn_{n}" for n in ("W1", "b1", "W2", "b2", "Wr", "br")] \
    + [f"L1_xattn_{n}" for n in ("Wq", "Wk", "Wv", "Wout", "bout")] \
    + [f"L1_ffn_cn_{n}{i}" for i in (1, 2, 3, 4) for n in ("w", "b")] \
    + [f"L1_ffn_gc_{n}{i}" for i in (1, 2, 3) for n in ("w", "b")] + ["L1_ffn_adaptive_range"]


def kernel(**inputs):
    import concourse.bacc as bacc
    from concourse.bass_utils import run_bass_kernel_spmd

    nc = bacc.Bacc("TRN2", target_bir_lowering=False, num_devices=1)
    arrays, aps = {}, {}
    for name in _INS:
        a = np.ascontiguousarray(inputs[name])
        arrays[f"in_{name}"] = a
        aps[name] = nc.dram_tensor(f"in_{name}", a.shape, mybir.dt.from_np(a.dtype), kind="ExternalInput").ap()
    shape = arrays["in_x"].shape
    out = nc.dram_tensor("out", shape, F32, kind="ExternalOutput").ap()
    flamingo(nc, aps, out)
    r = run_bass_kernel_spmd(nc, [arrays], core_ids=[0])
    return r.results[0]["out"]
```

```python
from contextlib import ExitStack

import numpy as np

import concourse.bass as bass
from concourse import mybir

F32 = mybir.dt.float32
U32 = mybir.dt.uint32
ALU = mybir.AluOpType
ACT = mybir.ActivationFunctionType
AX = mybir.AxisListType

P = 128
EPS = 1e-5


class Attention:

    def __init__(self, index, heads_per_step, keys, remainder_width, scale, bodies):
        self.index = index
        self.hs = heads_per_step
        self.dh = 256 // heads_per_step
        self.keys = keys
        self.rw = remainder_width
        self.chunks = 4 // heads_per_step
        self.rem = keys - 128 * self.chunks
        self.width = 128 * self.chunks + remainder_width
        self.scale = scale
        self.bodies = bodies
        self.batches = 2 if keys == 154 else 1
        self.score_cols = 308 + index


def flamingo(nc, t_in, out):
    B, S, D = t_in["x"].shape
    T = B * S
    NT = T // P
    DK = D // P
    _, NKEY, DC = t_in["ctx_768"].shape
    CK = DC // 2
    KEYS = B * NKEY
    INNER = t_in["L0_xattn_Wq"].shape[1]
    NC = INNER // P
    E, _, H2 = t_in["L0_ffn_W1"].shape
    H = H2 // 2
    HK = H // P

    L0 = Attention(0, 4, NKEY, 32, 64 ** -0.5,
                   [(0, 1, True, 0, 0, 0), (1, 3, False, 0, 0, 0), (3, 4, True, 0, 0, 1),
                    (4, 5, True, 0, 1, 1), (5, 7, False, 1, 1, 1), (7, 8, True, 1, 1, 1)])
    L1 = Attention(1, 2, KEYS, 64, 1.5 * 128 ** -0.5,
                   [(0, 1, True, 0, 0, 0), (1, 5, False, 0, 0, 0), (5, 6, True, 0, 0, 0), (6, 7, True, 0, 0, 0),
                    (7, 8, True, 0, 0, 0)])
    STEPS = 4 * NT
    TOP = 2
    SLOTS = (TOP * T + E * (P - 1)) // P
    SLOTS += SLOTS % 2

    with ExitStack() as ctx:
        def sb(name, shape, dt=F32):
            return ctx.enter_context(nc.sbuf_tensor(name, shape, dt))

        sems = {}

        def sem(name):
            if name not in sems:
                sems[name] = ctx.enter_context(nc.semaphore(name))
            return sems[name]

        banks = ctx.enter_context(nc.psum_tensor("banks", [P, 8, 512], F32))
        x = sb("x", [P, NT, D])
        ident = sb("ident", [P, P])
        gates = sb("gates", [P, 4])
        stats = sb("stats", [P, NT, 6])
        mean_var = sb("mean_var", [P, NT, 2])
        moments = sb("moments", [P, 4, 2])
        loop_stats = sb("loop_stats", [P, 4, 6])
        zero_eps = sb("zero_eps", [P, 2])
        minus_half = sb("minus_half", [P, NT])
        rstd = sb("rstd", [P, NT])
        xn = sb("xn", [P, D])
        x_biased = sb("x_biased", [P, 2, D])
        xT = sb("xT", [P, 2, DK, P])
        gated_bo = sb("gated_bo", [P, D])
        ctxT = sb("ctxT", [CK, 2, KEYS])
        ctx_rem1 = sb("ctx_rem1", [CK, 2, P])
        BLK = 4 * P
        NB = T // BLK
        CYCLES = 3
        ones = sb("ones", [P, P])
        before = sb("before", [P, P])
        w1_region = sb("W1", [P, E * DK * H2])
        W1 = w1_region[:].rearrange("p (e k n) -> p e k n", e=E, k=DK)
        class Region:
            def __init__(self, name, size):
                self.buffer, self.at = sb(name, [P, size]), 0

            def part(self, n, pattern="p n -> p n", rows=P, dt=F32, **dims):
                view = self.buffer[0:rows, self.at:self.at + n]
                self.at += n
                if dt != F32:
                    view = view.bitcast(dt)
                return view.rearrange(pattern, **dims) if dims else view

        reg_a = Region("region_a", 2 * NC * 308 + 2 * NC * 3 * P + 6 * 640 + 4 * NC * P)
        K0 = reg_a.part(2 * NC * 308, "p (b c n) -> p b c n", b=2, c=NC)
        V = reg_a.part(2 * NC * 3 * P, "p (b c i n) -> p b c i n", b=2, c=NC, i=3)
        probs = reg_a.part(2 * 640, "p (r n) -> p r n", r=2)
        normed = reg_a.part(2 * 640, "p (r n) -> p r n", r=2)
        probsT = reg_a.part(2 * 640, "p (r n) -> p r n", r=2)
        q = reg_a.part(2 * NC * P, "p (r c n) -> p r c n", r=2, c=NC)
        oT = reg_a.part(2 * NC * P, "p (r c n) -> p r c n", r=2, c=NC)
        ctx_rem = oT.rearrange("p r c n -> p (r c n)")[0:CK, 0:4 * P].rearrange("p (k b n) -> p k b n", k=2, b=2)
        ctx_rows = probsT.rearrange("p r n -> p (r n)")[:, 0:3 * DC].rearrange("p (r d) -> p r d", r=3)
        K1 = K0.rearrange("p b c n -> p (b c n)")[:, 0:NC * 309].rearrange("p (c n) -> p c n", c=NC)
        reg_a.at = 0
        b1 = reg_a.part(E * H2, "p (e n) -> p e n", e=E)
        W2 = reg_a.part(E * HK * D, "p (e k n) -> p e k n", e=E, k=HK)
        b2 = reg_a.part(E * D, "p (e n) -> p e n", e=E)
        reg_a.at = 0
        h1T = reg_a.part(NB * 2 * BLK, "p (j m n) -> p j m n", j=NB, m=2)
        h2T = reg_a.part(NB * BLK, "p (j n) -> p j n", j=NB)
        h3T = reg_a.part(NB * BLK, "p (j n) -> p j n", j=NB)
        twist = reg_a.part(4 * D * NB, "p (t d) -> p t d", d=D)

        reg_b = Region("region_b", 8704)
        Wk = reg_b.part(2 * INNER, "p (k n) -> p k n", rows=CK, k=2)
        Wv = reg_b.part(2 * INNER, "p (k n) -> p k n", rows=CK, k=2)
        Wq = reg_b.part(DK * INNER, "p (k n) -> p k n", k=DK)
        Wo = reg_b.part(NC * D, "p (c n) -> p c n", c=NC)
        reg_b.at = 0
        xn_all = reg_b.part(NT * D, "p (t d) -> p t d", t=NT)
        xg = reg_b.part(2 * D, "p (r d) -> p r d", r=2)
        xgT = reg_b.part(2 * D, "p (r k n) -> p r k n", r=2, k=DK)
        y_slot = reg_b.part(2 * D, "p (r d) -> p r d", r=2)
        a_act = reg_b.part(2 * H, "p (r n) -> p r n", r=2)
        g_act = reg_b.part(2 * H, "p (r n) -> p r n", r=2)
        xeT = reg_b.buffer[:, reg_b.at - 4 * H:reg_b.at - 4 * H + 4 * D].rearrange("p (r k n) -> p r k n", r=4, k=DK)
        actT = reg_b.part(2 * H, "p (r k n) -> p r k n", r=2, k=HK)

        F16 = mybir.dt.float16
        reg_b.at = NT * D
        in_row = reg_b.part(TOP * NT * P // 2, "p (q m) -> p q m", dt=F16, q=TOP * NT)
        numbered = reg_b.part(TOP * NT * SLOTS // 2, "p (q j) -> p q j", dt=F16, q=TOP * NT)
        in_tile = reg_b.part(TOP * NT * SLOTS, "p (q j) -> p q j", q=TOP * NT)

        reg_b.at = 6 * INNER + NC * D
        iota_s = reg_b.part(SLOTS)
        slot_start = reg_b.part(SLOTS)
        iota_row = reg_b.part(P)
        token_id = reg_b.part(NT)

        at = [0]

        def late(n, pattern="p n -> p n", rows=P, **dims):
            view = w1_region[0:rows, at[0]:at[0] + n]
            at[0] += n
            return view.rearrange(pattern, **dims) if dims else view

        cur = late(NT * D, "p (t d) -> p t d", t=NT)
        curT = late(NB * DK * BLK, "p (j k n) -> p j k n", j=NB, k=DK)
        cw1 = late(DK * 256, "p (k n) -> p k n", k=DK)
        cw2 = late(2 * 128, "p (k n) -> p k n", k=2)
        cw3, cw4 = late(64), late(1, rows=64)
        cb1, cb2, cb3, cb4 = late(2), late(1), late(1, rows=64), late(1)
        gw1 = late(DK * 128, "p (k n) -> p k n", k=DK)
        gw2, gw3 = late(64), late(1, rows=64)
        gb1, gb2, gb3 = late(1), late(1, rows=64), late(1)
        reach = late(1)
        gw3_wide = late(P, rows=64)
        mean_sb = late(4, "p (k b) -> p k b", k=DK)
        g1, g2, g3 = late(2), late(2, rows=64), late(2)
        half_b4, half_gb3 = late(1), late(1)
        slope = late(2)
        level = late(4, "p (q b) -> p q b", q=2)
        level_part = late(2)
        block_sum = late(DK * NB, "p (k j) -> p k j", k=DK)
        mean_sum = late(4, "p (k b) -> p k b", k=DK)
        tf = late(NT)
        y_pair = late(4 * D, "p (r i d) -> p r i d", r=2, i=2)
        coef = late(NT * 4, "p (t q) -> p t q", t=NT)

        Wr = sb("Wr", [P, DK, E])
        br = sb("br", [P, E])
        logits = sb("logits", [P, NT, E])
        top = sb("top", [P, NT, 8])
        top_at = sb("top_at", [P, NT, 8], U32)
        top_atf = sb("top_atf", [P, NT, TOP])
        chosen = sb("chosen", [P, TOP, NT, E])
        either = sb("either", [P, NT, E])
        totals = sb("totals", [P, NT, E])
        upto = sb("upto", [P, NT, E])
        place = sb("place", [P, NT, E])
        place_i = sb("place_i", [P, NT, E])
        slot_f = sb("slot_f", [P, TOP, NT])
        slot = sb("slot", [P, TOP, NT], U32)
        slot_now = sb("slot_now", [P, 2, TOP], U32)
        weight = sb("weight", [P, 4, NT])
        tiles_cmp = sb("tiles_cmp", [P, E, NT])
        tiles_of = sb("tiles_of", [P, E])
        tiles_end = sb("tiles_end", [P, E])
        tiles_base = sb("tiles_base", [P, E])
        iota_e = sb("iota_e", [P, E])
        iota_t = sb("iota_t", [P, NT])
        slot_part = sb("slot_part", [P, 2, TOP, NT])
        slot_low = sb("slot_low", [P, TOP, NT], U32)
        token_of = sb("token_of", [P, SLOTS + 1], U32)
        token_now = sb("token_now", [P, 2], U32)
        owner_cmp = xT.ap().rearrange("p r k n -> p (r k n)")[0:1, 0:SLOTS * E].rearrange("p (s e) -> p s e", s=SLOTS)
        owner_f = sb("owner_f", [1, SLOTS])
        owner = sb("owner", [1, SLOTS], mybir.dt.int32)
        xn_rows = nc.dram_tensor("xn_rows", [T, D], F32, kind="Internal").ap()
        y_slots = nc.dram_tensor("y_slots", [SLOTS * P, D], F32, kind="Internal").ap()

        row_of = slot_part[:, 0].rearrange("p c t -> p (c t)")
        start_of = slot_part[:, 1].rearrange("p c t -> p (c t)")
        negmax = sb("negmax", [P, 2, 4])
        bias1 = sb("bias1", [P, 2, 4])
        shifted = sb("shifted", [P, 2, 4])
        sums = sb("sums", [P, 2, 4])
        recip = sb("recip", [P, 2, 4])
        kmean = sb("kmean", [P, NC])

        scores = banks[:, 0:4, :].rearrange("p (r u) n -> p r u n", r=2)
        probsT_ps = banks[:, 4:6, :].rearrange("p u n -> p (u n)")
        o_ps = banks[:, 6, :]
        misc_ps = banks[:, 7, :]

        block = ctx.enter_context(nc.Block())

        def finals(eng, *names_counts):
            for name, count in names_counts:
                eng.wait_ge(sem(name), count)

        def load_keys_values(eng, layer):
            for w, dst, name in (("Wk", Wk, "wk_in"), ("Wv", Wv, "wv_in")):
                src = t_in[f"L{layer}_xattn_{w}"].rearrange("(k p) n -> p k n", p=CK)
                eng.dma_start(dst, src).then_inc(sem(name), 16)

        def load_attention(eng, layer):
            n = f"L{layer}_xattn_"
            eng.dma_start(Wq[:], t_in[n + "Wq"].rearrange("(k p) n -> p k n", p=P)).then_inc(sem("wq_in"), 16)
            wo, bo = ("Wo", "bo") if layer == 0 else ("Wout", "bout")
            eng.dma_start(Wo[:], t_in[n + wo].rearrange("(k p) n -> p k n", p=P)).then_inc(sem("wo_in"), 16)
            eng.dma_start(gated_bo[:], t_in[n + bo].partition_broadcast(P)).then_inc(sem("bo_in"), 16)

        def kv_units(L):
            units = [("k", c, 0) for c in range(NC)]
            if L.index == 0:
                units += [("v", b, half) for b in range(2) for half in range(2)]
            else:
                units += [("v", chunk, half) for chunk in range(2) for half in range(2)]
            units += [("r", b, half) for b in range(L.batches) for half in range(2)]
            return units

        KV0 = len(kv_units(L0))
        KV1 = KV0 + len(kv_units(L1))

        def kv_bank(n):
            return banks[:, n % 4] if n < NC else banks[:, 4 + (n - NC) % 3]

        def pe_kv(pe, L, kinds):
            base = KV0 * L.index
            pe.wait_ge(sem("wk_in"), 16 * (L.index + 1))
            for n, (kind, a, half) in enumerate(kv_units(L)):
                if kind not in kinds:
                    continue
                if n == NC:
                    pe.wait_ge(sem("wv_in"), 16 * (L.index + 1))
                    pe.wait_ge(sem("rem_ready"), 2)
                if n >= (4 if n < NC else NC + 3):
                    pe.wait_ge(sem("kv_sb"), base + n - (3 if n < NC else 2))
                bank = kv_bank(n)
                for k in range(2):
                    if kind == "k":
                        o, l, r = bank[:, 0:KEYS], Wk[:, k, a * P:(a + 1) * P], ctxT[:, k, :]
                    else:
                        r = Wv[:, k, half * 512:(half + 1) * 512]
                        start = a * (NKEY if L.index == 0 else P)
                        l = ctxT[:, k, start:start + P] if kind == "v" else (
                            ctx_rem[:, k, a, :] if L.index == 0 else ctx_rem1[:, k, :])
                        o = bank
                    mm = pe.matmul(o, l, r, start=(k == 0), stop=(k == 1))
                mm.then_inc(sem("kv_ps"), 1)

        def dve_kv(dve, L, kinds):
            base = KV0 * L.index
            for n, (kind, a, half) in enumerate(kv_units(L)):
                if kind not in kinds:
                    continue
                dve.wait_ge(sem("kv_ps"), base + n + 1)
                bank = kv_bank(n)
                if kind == "k" and L.index == 0:
                    for i in range(2):
                        rows = slice(64 * i, 64 * i + 64)
                        last = dve.tensor_scalar_mul(K0[rows, :, a, i * NKEY:(i + 1) * NKEY],
                                                     bank[rows, 0:KEYS].rearrange("p (b n) -> p b n", b=2), L.scale)
                elif kind == "k":
                    last = dve.tensor_scalar(K1[:, a, 0:KEYS], bank[:, 0:KEYS], L.scale, 0.0, ALU.mult, ALU.add,
                                             accum_out=kmean[:, a:a + 1])
                elif kind == "v" and L.index == 0:
                    for i in range(2):
                        last = dve.tensor_copy(
                            V[:, a, half * 4:half * 4 + 4, i, i * 64:(i + 1) * 64],
                            bank.rearrange("p (c i n) -> p c i n", c=4, i=2)[:, :, i, :])
                elif kind == "v":
                    last = dve.tensor_copy(V[:, 0, half * 4:half * 4 + 4, a, :],
                                           bank.rearrange("p (c n) -> p c n", c=4))
                else:
                    for j in range(L.hs):
                        rows = slice(L.rw * j, L.rw * (j + 1))
                        blk = (2 * j) // L.hs
                        col = (j * L.dh) % P
                        for g in range(2):
                            last = dve.tensor_copy(
                                V[rows, a, half * 4 + 2 * g + blk, 2, col:col + L.dh],
                                bank[rows, (g * L.hs + j) * L.dh:(g * L.hs + j + 1) * L.dh])
                last.then_inc(sem("kv_sb"), 1)

        def bodies(eng, L, emit):
            for first, end, peeled, before, batch, after in L.bodies:
                if peeled:
                    emit(first, first == 0, end == NT // 2, before, batch, after)
                else:
                    with eng.Fori(first, end) as i:
                        emit(i, False, False, before, batch, after)

        def pe_scores(pe, L, s, g, r, b):
            for u in range(2):
                K = K0[:, b, 2 * g + u, :] if L.index == 0 else K1[:, 2 * g + u, :]
                mm = pe.matmul(scores[:, g % 2, u, 0:L.score_cols], q[:, r, 2 * g + u, :], K, start=True, stop=True)
            mm.then_inc(sem("s_ps"), 1)

        def pe_transpose_x(pe, src):
            for k in range(DK):
                mm = pe.transpose(misc_ps[:, k * P:(k + 1) * P], src[:, k * P:(k + 1) * P], ident[:])
            mm.then_inc(sem("xt_ps"), 1)

        def pe_q(pe, r, half):
            for c in range(4):
                for k in range(DK):
                    mm = pe.matmul(misc_ps[:, c * P:(c + 1) * P], Wq[:, k, (4 * half + c) * P:(4 * half + c + 1) * P],
                                   xT[:, r, k, :], start=(k == 0), stop=(k == DK - 1))
            mm.then_inc(sem("q_ps"), 1)

        def pe_probsT(pe, L, g):
            for m in range(5):
                mm = pe.transpose(probsT_ps[:, m * P:(m + 1) * P], normed[:, g % 2, m * P:(m + 1) * P], ident[:])
            mm.then_inc(sem("pt_ps"), 1)

        def pe_pv(pe, g, b):
            for u in range(2):
                for i in range(3):
                    m = 2 * u + i if i < 2 else 4
                    mm = pe.matmul(o_ps[:, u * P:(u + 1) * P], V[:, b, 2 * g + u, i, :],
                                   probsT[:, g % 2, m * P:(m + 1) * P], start=(i == 0), stop=(i == 2))
            mm.then_inc(sem("o_ps"), 1)

        def pe_out(pe, r):
            for c in range(NC):
                mm = pe.matmul(misc_ps[:, 0:D], oT[:, r, c, :], Wo[:, c, :], start=(c == 0), stop=(c == NC - 1))
            mm.then_inc(sem("y_ps"), 1)

        def pe_attention(pe, L):
            t0, s0 = NT * L.index, STEPS * L.index
            pe_kv(pe, L, "k")
            pe.wait_ge(sem("xn_ready"), t0 + 1)
            pe_transpose_x(pe, xn)
            pe.wait_ge(sem("wq_in"), 16 * (L.index + 1))
            pe.wait_ge(sem("xt_sb"), t0 + 1)
            pe_q(pe, 0, 0)
            pe.wait_ge(sem("q_sb"), 2 * t0 + 1)
            pe_q(pe, 0, 1)
            pe.wait_ge(sem("kv_sb"), KV0 * L.index + NC)
            if L.index == 1:
                pe.wait_ge(sem("kmean_done"), 1)
            pe_scores(pe, L, 0, 0, 0, 0)
            pe_kv(pe, L, "vr")
            pe.wait_ge(sem("kv_sb"), KV0 if L.index == 0 else KV1)

            def emit(i, first, last, before, batch, after):
                for r in range(2):
                    t = 2 * i + r
                    t_first, t_last = first and r == 0, last and r == 1
                    for g in range(4):
                        s = 4 * t + g
                        if not (t_last and g == 3):
                            gn = (g + 1) % 4
                            if gn == 0:
                                pe.wait_ge(sem("q_sb"), 2 * (t0 + t) + 3)
                            elif gn == 2:
                                pe.wait_ge(sem("q_sb"), 2 * (t0 + t) + 2)
                            if not (t_first and g == 0):
                                pe.wait_ge(sem("p_exp"), s0 + s)
                            nb = after if (g == 3 and r == 1) else batch
                            pe_scores(pe, L, s + 1, gn, r if g < 3 else 1 - r, nb)
                        if not (t_first and g == 0):
                            pe.wait_ge(sem("p_norm"), s0 + s)
                            if not (t_first and g == 1):
                                pe.wait_ge(sem("pt_sb_act"), s0 + s - 1)
                                pe.wait_ge(sem("pt_sb_dve"), s0 + s - 1)
                            pe_probsT(pe, L, (g - 1) % 4)
                        if g == 0 and not t_last:
                            pe.wait_ge(sem("q_sb"), 2 * (t0 + t) + 2)
                            if not first:
                                pe.wait_ge(sem("y_done"), t0 + t - 1)
                            pe.wait_ge(sem("xn_ready"), t0 + t + 2)
                            pe_transpose_x(pe, xn)
                        if g == 1 and not t_last:
                            pe.wait_ge(sem("xt_sb"), t0 + t + 2)
                            pe_q(pe, 1 - r, 0)
                        if g == 2 and not t_last:
                            pe.wait_ge(sem("q_sb"), 2 * (t0 + t) + 3)
                            pe_q(pe, 1 - r, 1)
                        if g == 3 and not t_first:
                            if not t_last:
                                pe.wait_ge(sem("q_sb"), 2 * (t0 + t) + 4)
                            else:
                                pe.wait_ge(sem("y_done"), t0 + t - 1)
                            pe.wait_ge(sem("o_sb"), s0 + 4 * t)
                            pe_out(pe, 1 - r)
                        if not (t_first and g < 2):
                            pe.wait_ge(sem("pt_sb_act"), s0 + s - 1)
                            pe.wait_ge(sem("pt_sb_dve"), s0 + s - 1)
                            if not (t_first and g == 2):
                                pe.wait_ge(sem("o_sb"), s0 + s - 2)
                            pe_pv(pe, (g - 2) % 4, before if (g < 2 and r == 0) else batch)

            if L.index == 0:
                pe.wait_ge(sem("wo_in"), 16)
            else:
                pe.wait_ge(sem("wo_in"), 32)
            bodies(pe, L, emit)
            pe.wait_ge(sem("p_norm"), s0 + STEPS)
            pe.wait_ge(sem("pt_sb_act"), s0 + STEPS - 1)
            pe.wait_ge(sem("pt_sb_dve"), s0 + STEPS - 1)
            pe_probsT(pe, L, 3)
            for s in (STEPS - 2, STEPS - 1):
                pe.wait_ge(sem("pt_sb_act"), s0 + s + 1)
                pe.wait_ge(sem("pt_sb_dve"), s0 + s + 1)
                pe.wait_ge(sem("o_sb"), s0 + s)
                pe_pv(pe, s % 4, L.bodies[-1][4])
            pe.wait_ge(sem("o_sb"), s0 + STEPS)
            pe.wait_ge(sem("y_done"), t0 + NT - 1)
            pe_out(pe, 1)

        def stats_of(dve, t, which, slot=None):
            into = stats[:, t, :] if slot is None else loop_stats[:, slot, :]
            dve.bn_stats(into, tile_of(x, t)).then_inc(sem(f"stats_{which}"), 1)

        def aggregate(dve, t, which, count, signal=True, slot=None):
            if count is not None:
                dve.wait_ge(sem(f"stats_{which}"), count)
            into = mean_var[:, t] if slot is None else moments[:, slot]
            a = dve.bn_aggr(into, stats[:, t, :] if slot is None else loop_stats[:, slot, :])
            if signal:
                a.then_inc(sem(f"var_{which}"), 1)

        def pool_rstd(pool, t, n, which, count, slot=None):
            at = slice(t, t + n) if isinstance(t, int) else bass.ds(t, n)
            source = mean_var[:, at] if slot is None else moments[:, slot:slot + 1]
            pool.wait_ge(sem(f"var_{which}"), count)
            pool.tensor_tensor(mean_var[:, at], source, zero_eps[:, :].unsqueeze(1).broadcast_to([P, n, 2]), ALU.add)\
                .then_inc(sem(f"shift_{which}"), 1)
            pool.wait_ge(sem(f"shift_{which}"), count)
            pool.tensor_tensor(rstd[:, at], mean_var[:, at, 1], minus_half[:, 0:n], ALU.pow)\
                .then_inc(sem(f"rstd_{which}"), 1)

        OUT = NT - 1

        def tile_of(buf, t):
            if isinstance(t, int):
                return buf[:, t, :]
            return buf[:, bass.ds(t, 1), :].rearrange("p a d -> p (a d)")

        def column_of(buf, t):
            return buf[:, t:t + 1] if isinstance(t, int) else buf[:, bass.ds(t, 1)]

        def dve_normalize(dve, t):
            dve.tensor_scalar(xn[:], tile_of(x, t), column_of(mean_var[:, :, 0], t), column_of(rstd, t),
                              ALU.subtract, ALU.mult).then_inc(sem("xn_ready"), 1)

        def mix(dve, t, r, c):
            if c == 0:
                dve.wait_ge(sem(f"gathered{r}"), 32 * (t // 2 + 1) if isinstance(t, int) else (t - r) * 16 + 32)
            else:
                dve.wait_ge(sem("mixed_first"), t + 1)
            w = weight[:, 2 + c, :]
            dve.scalar_tensor_tensor(tile_of(x, t), y_pair[:, r, c, :], column_of(w, t), tile_of(x, t),
                                     ALU.mult, ALU.add).then_inc(sem("mixed" if c else "mixed_first"), 1)

        def dve_attention(dve, L):
            t0, s0 = NT * L.index, STEPS * L.index
            if L.index == 0:
                dve.wait_ge(sem("x_first"), 16)
                for t in range(4):
                    stats_of(dve, t, "in")
                for t in range(4):
                    aggregate(dve, t, "in", 4, t == 3)
                dve.wait_ge(sem("kv_zero"), 1)
            else:
                dve.wait_ge(sem("kv_zero"), 2)
            dve_kv(dve, L, "k")
            if L.index == 1:
                for t in range(4):
                    for c in range(TOP):
                        mix(dve, t, t % 2, c)
                for t in range(4):
                    dve.wait_ge(sem("mixed"), t + 1)
                    stats_of(dve, t, "in")
                for t in range(4):
                    aggregate(dve, t, "in", NT + 4, t == 3)
            if L.index == 1:
                dve.wait_ge(sem("kv_sb"), KV0 + NC)
                dve.tensor_scalar_mul(K1[:, :, KEYS], kmean[:, :], -1.0 / (3 * KEYS)).then_inc(sem("kmean_done"), 1)
            dve.wait_ge(sem("rstd_in"), 1 if L.index == 0 else 3)
            dve_normalize(dve, 0)
            dve.wait_ge(sem("xt_ps"), t0 + 1)
            dve_normalize(dve, 1)
            if L.index == 0:
                dve.wait_ge(sem("x_rest"), 16)
                for t in range(4, NT):
                    stats_of(dve, t, "in")
                for t in range(4, NT):
                    aggregate(dve, t, "in", NT, t == NT - 1)

            def row_max(g, s):
                dve.wait_ge(sem("s_ps"), s0 + s + 1)
                if L.index == 0:
                    dve.tensor_reduce(negmax[:, g % 2, :].rearrange("p (u i) -> p u i", u=2),
                                      scores[:, g % 2, :, 0:KEYS].rearrange("p u (i n) -> p u i n", i=2),
                                      AX.X, ALU.max, negate=True).then_inc(sem("bias_ready"), 1)
                    return
                m = scores[:, g % 2, :, KEYS]
                dve.tensor_reduce(negmax[:, g % 2, 0:2], scores[:, g % 2, :, 0:KEYS], AX.X, ALU.max,
                                  negate=True).then_inc(sem("negmax_done"), 1)
                dve.wait_ge(sem("negmax_done"), s + 1)
                dve.tensor_tensor(shifted[:, g % 2, 0:2], negmax[:, g % 2, 0:2], m,
                                  ALU.subtract).then_inc(sem("shifted_done"), 1)
                dve.wait_ge(sem("shifted_done"), s + 1)
                dve.tensor_tensor(bias1[:, g % 2, 0:2], shifted[:, g % 2, 0:2], m, ALU.add).then_inc(sem("bias_ready"), 1)

            row_max(0, 0)
            dve_kv(dve, L, "vr")
            if L.index == 0:
                dve.wait_ge(sem("rstd_in"), 2)

            def evacuate_probsT(s, parity):
                dve.wait_ge(sem("pt_ps"), s0 + s + 1)
                dve.tensor_copy(probsT[:, parity, 0:512], probsT_ps[:, 0:512]).then_inc(sem("pt_sb_dve"), 1)

            def evacuate_o(s, g, r):
                dve.wait_ge(sem("o_ps"), s0 + s + 1)
                dve.tensor_copy(oT[:, r, 2 * g:2 * g + 2, :],
                                o_ps[:, 0:2 * P].rearrange("p (u n) -> p u n", u=2)).then_inc(sem("o_sb"), 1)

            def add_y(t, r):
                dve.wait_ge(sem("y_ps"), t0 + t + 1)
                dve.wait_ge(sem("xb_ready"), t0 + t + 1)
                dve.scalar_tensor_tensor(tile_of(x, t), misc_ps[:, 0:D], gates[:, L.index:L.index + 1],
                                         x_biased[:, r, :], ALU.mult, ALU.add).then_inc(sem("y_done"), 1)

            def emit(i, first, last, before, batch, after):
                for r in range(2):
                    t = 2 * i + r
                    t_first, t_last = first and r == 0, last and r == 1
                    for g in range(4):
                        s = 4 * t + g
                        mixing = L.index == 1 and (not isinstance(t, int) or t + 4 < NT)
                        if g == 0 and not first:
                            dve.wait_ge(sem("y_done"), t0 + t - 1)
                        if g == 2 and not first:
                            dve.wait_ge(sem("stats_out"), t0 + t - 1)
                        if g == 2 and mixing:
                            dve.wait_ge(sem("mixed"), t + 5)
                        if g == 3 and mixing:
                            dve.wait_ge(sem("stats_in"), NT + 1 + t + 4)
                        dve.wait_ge(sem("p_exp"), s0 + s + 1)
                        dve.reciprocal(recip[:, g % 2, 0:L.hs], sums[:, g % 2, 0:L.hs]).then_inc(sem("recip_ready"), 1)
                        if not (t_last and g == 3):
                            row_max((g + 1) % 4, s + 1)
                        if not (t_first and g == 0):
                            evacuate_probsT(s - 1, (g - 1) % 2)
                        if not (t_first and g < 2):
                            evacuate_o(s - 2, (g - 2) % 4, r if g >= 2 else 1 - r)
                        if g == 0 and not first:
                            stats_of(dve, t - 2, "out", slot=r)
                        if g == 0 and mixing:
                            mix(dve, t + 4, r, 0)
                        if g == 1 and not last:
                            dve.wait_ge(sem("xt_ps"), t0 + t + 2)
                            if L.index == 1:
                                dve.wait_ge(sem("rstd_in"), max(3, t + 2) if isinstance(t, int) else t + 2)
                            dve_normalize(dve, t + 2)
                        if g == 1 and mixing:
                            mix(dve, t + 4, r, 1)
                        if g == 2 and not first:
                            aggregate(dve, t - 2, "out", None, slot=r)
                        if g == 2 and mixing:
                            stats_of(dve, t + 4, "in", slot=2 + r)
                        if g == 3 and not t_first:
                            add_y(t - 1, 1 - r)
                        if L.index == 1 and isinstance(t, int) and t >= NT - 5 and g < 3:
                            early = 3 * (t - (NT - 5)) + g
                            if early <= t - 3:
                                dve.wait_ge(sem("rstd_out"), OUT + early + 1)
                                first_cur(dve, early)
                        if g == 3 and mixing:
                            aggregate(dve, t + 4, "in", None, slot=2 + r)

            bodies(dve, L, emit)
            evacuate_probsT(STEPS - 1, 1)
            evacuate_o(STEPS - 2, 2, 1)
            evacuate_o(STEPS - 1, 3, 1)
            add_y(NT - 1, 1)
            for t in (NT - 2, NT - 1):
                dve.wait_ge(sem("y_done"), t0 + t + 1)
                stats_of(dve, t, "out")
            for t in (NT - 2, NT - 1):
                aggregate(dve, t, "out", t0 + t + 1, t == NT - 1)

        def act_attention(act, L):
            t0, s0 = NT * L.index, STEPS * L.index

            def evacuate_xT(t, r):
                act.wait_ge(sem("xt_ps"), t0 + t + 1)
                act.copy(xT[:, r], misc_ps[:, 0:D].rearrange("p (k n) -> p k n", k=DK)).then_inc(sem("xt_sb"), 1)

            def evacuate_probsT(s, parity):
                act.wait_ge(sem("pt_ps"), s0 + s + 1)
                act.copy(probsT[:, parity, 512:640], probsT_ps[:, 512:640]).then_inc(sem("pt_sb_act"), 1)

            def evacuate_q(t, r, half):
                act.wait_ge(sem("q_ps"), 2 * (t0 + t) + half + 1)
                act.copy(q[:, r, 4 * half:4 * half + 4, :],
                         misc_ps.rearrange("p (c n) -> p c n", c=4)).then_inc(sem("q_sb"), 1)

            def exponentials(g, s):
                act.wait_ge(sem("bias_ready"), s0 + s + 1)
                bias = negmax if L.index == 0 else bias1
                pr = probs[:, g % 2, :].rearrange("p (j n) -> p j n", j=L.hs)
                for j in range(L.hs):
                    u, i = (j // 2, j % 2) if L.index == 0 else (j, 0)
                    e = act.activation(pr[:, j, 0:L.keys], scores[:, g % 2, u, i * L.keys:(i + 1) * L.keys], ACT.Exp,
                                       bias=bias[:, g % 2, j:j + 1], accum_out=sums[:, g % 2, j:j + 1])
                e.then_inc(sem("p_exp"), 1)

            evacuate_xT(0, 0)
            evacuate_q(0, 0, 0)
            evacuate_q(0, 0, 1)
            act.wait_ge(sem("pads_zero"), 1 + L.index)
            exponentials(0, 0)

            def emit(i, first, last, before, batch, after):
                for r in range(2):
                    t = 2 * i + r
                    t_first, t_last = first and r == 0, last and r == 1
                    for g in range(4):
                        s = 4 * t + g
                        if not (t_last and g == 3):
                            if not (t_first and g == 0):
                                act.wait_ge(sem("p_norm"), s0 + s)
                            exponentials((g + 1) % 4, s + 1)
                        if not (t_first and g == 0):
                            evacuate_probsT(s - 1, (g - 1) % 2)
                        if not t_last:
                            if g == 0:
                                evacuate_xT(t + 1, 1 - r)
                            if g == 1:
                                evacuate_q(t + 1, 1 - r, 0)
                            if g == 2:
                                evacuate_q(t + 1, 1 - r, 1)

            bodies(act, L, emit)
            evacuate_probsT(STEPS - 1, 1)

        def slots_now(pool, t, r, reused):
            if isinstance(t, int):
                now = slot[:, :, t]
            else:
                now = slot[:, :, bass.ds(t, 1)].rearrange("p c a -> p (c a)")
            if reused is not None:
                pool.wait_ge(sem("mixed"), reused if not isinstance(reused, int) else t - 1)
            pool.tensor_copy(slot_now[:, r, :], now).then_inc(sem("slot_now_ready"), 1)

        def gather(pool, t, r):
            for c in range(TOP):
                pool.indirect_dma_start(out=y_pair[:, r, c, :], out_offset=None, in_=y_slots,
                                        in_offset=bass.IndirectOffsetOnAxis(ap=slot_now[:, r, c:c + 1], axis=0))\
                    .then_inc(sem(f"gathered{r}"), 16)

        def pool_attention(pool, L):
            t0, s0 = NT * L.index, STEPS * L.index

            def emit(i, first, last, before, batch, after):
                for r in range(2):
                    t = 2 * i + r
                    for g in range(4):
                        s = 4 * t + g
                        pool.wait_ge(sem("recip_ready"), s0 + s + 1)
                        gathering = L.index == 1 and (not isinstance(t, int) or t + 5 < NT)
                        if g == 1 and gathering:
                            pool.wait_ge(sem("slot_now_ready"), t + 6)
                        if not (first and r == 0 and g < 2):
                            pool.wait_ge(sem("pt_ps"), s0 + s - 1)
                        pr = probs[:, g % 2, :].rearrange("p (j n) -> p j n", j=L.hs)
                        whole = normed[:, g % 2, 0:512].rearrange("p (j n) -> p j n", j=L.hs)
                        rest = normed[:, g % 2, 512:640].rearrange("p (j n) -> p j n", j=L.hs)
                        rc = recip[:, g % 2, 0:L.hs].unsqueeze(2)
                        split = L.chunks * P
                        pool.tensor_tensor(whole, pr[:, :, 0:split], rc.broadcast_to([P, L.hs, split]), ALU.mult)
                        pool.tensor_tensor(rest, pr[:, :, split:L.width], rc.broadcast_to([P, L.hs, L.rw]),
                                           ALU.mult).then_inc(sem("p_norm"), 1)
                        if L.index == 1 and g == 0 and (not isinstance(t, int) or 1 <= t <= NT - 4):
                            pool_rstd(pool, t + 3, 1, "in", t + 3, slot=3 - r)
                        if g == 0 and gathering:
                            slots_now(pool, t + 5, 1 - r, t + 4)
                        if g == 1 and gathering:
                            gather(pool, t + 5, 1 - r)
                        if g == 3 and not first:
                            pool_rstd(pool, t - 2, 1, "out", OUT * L.index + t - 1, slot=r)
                        if g == 2:
                            pool.wait_ge(sem("xn_ready"), t0 + t + 1)
                            if not first:
                                pool.wait_ge(sem("y_done"), t0 + t - 1)
                            pool.tensor_tensor(x_biased[:, r, :], tile_of(x, t), gated_bo[:],
                                               ALU.add).then_inc(sem("xb_ready"), 1)

            if L.index == 0:
                pool.wait_ge(sem("eps_ready"), 1)
                pool_rstd(pool, 0, 4, "in", 1)
                pool.wait_ge(sem("gates_ready"), 1)
                pool.wait_ge(sem("bo_in"), 16)
                pool.tensor_tensor(gated_bo[:], gated_bo[:], gates[:, 0:1].broadcast_to([P, D]), ALU.mult)\
                    .then_inc(sem("gbo_ready"), 1)
                pool_rstd(pool, 4, NT - 4, "in", 2)
                pool.wait_ge(sem("gbo_ready"), 1)
            else:
                pool_rstd(pool, 0, 4, "in", 3)
            bodies(pool, L, emit)
            pool_rstd(pool, NT - 2, 2, "out", OUT * (L.index + 1))

        def pe_routing(pe):
            pe.wait_ge(sem("wr_in"), 32)
            pe.wait_ge(sem("y_done"), NT)
            for n in range(NT + 3):
                if n < NT:
                    pe.wait_ge(sem("xe_ready"), n + 1)
                    if n >= 4:
                        pe.wait_ge(sem("xet_sb"), n - 3)
                    for k in range(DK):
                        mm = pe.transpose(banks[:, n % 4, k * P:(k + 1) * P], xn_all[:, n, k * P:(k + 1) * P], ident[:])
                    mm.then_inc(sem("xet_ps"), 1)
                if n >= 3:
                    t = n - 3
                    pe.wait_ge(sem("xet_sb"), t + 1)
                    for k in range(DK):
                        mm = pe.matmul(misc_ps[:, t * E:(t + 1) * E], xeT[:, t % 4, k, :], Wr[:, k, :],
                                       start=(k == 0), stop=(k == DK - 1), skip_group_check=True)
                    mm.then_inc(sem("logit_ps"), 1)
            pe.wait_ge(sem("either_ready"), 1)
            pe.matmul(banks[:, 4, 0:NT * E], before[:], either.rearrange("p t e -> p (t e)"), start=True, stop=True)
            pe.matmul(banks[:, 5, 0:NT * E], ones[:], either.rearrange("p t e -> p (t e)"), start=True, stop=True)\
                .then_inc(sem("rank_ps"), 1)
            pe.wait_ge(sem("numbered_ready"), 1)
            for n in range(TOP * NT):
                if n % 8 == 0:
                    pe.wait_ge(sem("in_row_ready"), n // 8 + 1)
                mm = pe.matmul(banks[:, 6, 0:SLOTS], in_row[:, n, :], numbered[:, n, :], start=(n == 0),
                               stop=(n == TOP * NT - 1))
            mm.then_inc(sem("token_ps"), 1)

        def dve_routing(dve):
            steps = [0]

            def link(ins):
                steps[0] += 1
                ins.then_inc(sem("route_step"), 1)
                dve.wait_ge(sem("route_step"), steps[0])

            dve.wait_ge(sem("rstd_out"), OUT)
            for t in range(NT):
                dve.tensor_scalar(xn_all[:, t, :], x[:, t, :], mean_var[:, t, 0:1], rstd[:, t:t + 1],
                                  ALU.subtract, ALU.mult).then_inc(sem("xe_ready"), 1)
            dve.wait_ge(sem("logit_ps"), NT)
            link(dve.tensor_tensor(logits[:], misc_ps[:, 0:NT * E].rearrange("p (t e) -> p t e", t=NT),
                                   br[:, :].unsqueeze(1).broadcast_to([P, NT, E]), ALU.add))
            for t in range(NT):
                last = dve.max(top[:, t, :], logits[:, t, :])
            link(last)
            for t in range(NT):
                last = dve.max_index(top_at[:, t, :], top[:, t, :], logits[:, t, :])
            link(last)
            dve.tensor_tensor(weight[:, 0, :], top[:, :, 1], top[:, :, 0], ALU.subtract).then_inc(sem("margin_ready"), 1)
            link(dve.tensor_copy(top_atf[:], top_at[:, :, 0:TOP]))
            for c in range(TOP):
                last = dve.tensor_tensor(chosen[:, c], iota_e[:].unsqueeze(1).broadcast_to([P, NT, E]),
                                         top_atf[:, :, c].unsqueeze(2).broadcast_to([P, NT, E]), ALU.is_equal)
            link(last)
            dve.tensor_tensor(either[:], chosen[:, 0], chosen[:, 1], ALU.add).then_inc(sem("either_ready"), 1)
            dve.wait_ge(sem("rank_ps"), 1)
            link(dve.tensor_copy(totals[:], banks[:, 5, 0:NT * E].rearrange("p (t e) -> p t e", t=NT)))
            for e in range(E):
                last = dve.tensor_tensor_scan(upto[:, :, e], ones[:, 0:NT], totals[:, :, e], 0.0, ALU.mult, ALU.add)
            link(last)
            link(dve.tensor_tensor(tiles_cmp[:], upto[:, NT - 1, :].unsqueeze(2).broadcast_to([P, E, NT]),
                                   iota_t[:].unsqueeze(1).broadcast_to([P, E, NT]), ALU.is_gt))
            link(dve.tensor_reduce(tiles_of[:], tiles_cmp[:], AX.X, ALU.add))
            link(dve.tensor_tensor_scan(tiles_end[:], ones[:, 0:E], tiles_of[:], 0.0, ALU.mult, ALU.add))
            link(dve.tensor_tensor(owner_cmp, iota_s[0:1, :].unsqueeze(2).broadcast_to([1, SLOTS, E]),
                                   tiles_end[0:1, :].unsqueeze(1).broadcast_to([1, SLOTS, E]), ALU.is_ge))
            link(dve.tensor_reduce(owner_f[:], owner_cmp, AX.X, ALU.add))
            dve.tensor_scalar(owner[:], owner_f[:], float(E - 1), None, ALU.min).then_inc(sem("owner_ready"), 1)
            link(dve.tensor_tensor(tiles_base[:], tiles_end[:], tiles_of[:], ALU.subtract))
            link(dve.tensor_tensor(place_i[:], upto[:], totals[:], ALU.subtract))
            link(dve.tensor_tensor(place[:], place_i[:], banks[:, 4, 0:NT * E].rearrange("p (t e) -> p t e", t=NT), ALU.add))
            link(dve.scalar_tensor_tensor(place_i[:], tiles_base[:].unsqueeze(1).broadcast_to([P, NT, E]), float(P),
                                          place[:], ALU.mult, ALU.add))
            for c in range(TOP):
                link(dve.tensor_tensor(place[:], chosen[:, c], place_i[:], ALU.mult))
                link(dve.tensor_reduce(slot_f[:, c, :], place[:], AX.X, ALU.add))
            link(dve.tensor_copy(slot[:], slot_f[:]))
            link(dve.tensor_scalar(slot_low[:], slot[:], P - 1, None, ALU.bitwise_and))
            link(dve.tensor_copy(slot_part[:, 0], slot_low[:]))
            link(dve.tensor_tensor(slot_part[:, 1], slot_f[:], slot_part[:, 0], ALU.subtract))
            link(dve.tensor_tensor(in_tile, slot_start.unsqueeze(1).broadcast_to([P, TOP * NT, SLOTS]),
                                   start_of.unsqueeze(2).broadcast_to([P, TOP * NT, SLOTS]), ALU.is_equal))
            for c in range(TOP):
                n = slice(c * NT, (c + 1) * NT)
                last = dve.tensor_tensor(numbered[:, n], in_tile[:, n],
                                         token_id.unsqueeze(2).broadcast_to([P, NT, SLOTS]), ALU.mult)
            last.then_inc(sem("numbered_ready"), 1)
            for n in range(0, TOP * NT, 8):
                dve.tensor_tensor(in_row[:, n:n + 8], iota_row.unsqueeze(1).broadcast_to([P, 8, P]),
                                  row_of[:, n:n + 8].unsqueeze(2).broadcast_to([P, 8, P]), ALU.is_equal)\
                    .then_inc(sem("in_row_ready"), 1)
            dve.wait_ge(sem("token_ps"), 1)
            dve.tensor_copy(token_of[:, 0:SLOTS], banks[:, 6, 0:SLOTS]).then_inc(sem("token_ready"), 1)
            dve.wait_ge(sem("margin_exp"), 1)
            link(dve.tensor_scalar_add(weight[:, 2, :], weight[:, 1, :], 1.0))
            link(dve.reciprocal(weight[:, 0, :], weight[:, 2, :]))
            link(dve.tensor_scalar_mul(weight[:, 2, :], weight[:, 0, :], gates[:, 2:3]))
            dve.tensor_tensor(weight[:, 3, :], weight[:, 1, :], weight[:, 2, :], ALU.mult).then_inc(sem("weight_ready"), 1)

        def act_routing(act):
            for t in range(NT):
                act.wait_ge(sem("xet_ps"), t + 1)
                if t >= 4:
                    act.wait_ge(sem("logit_ps"), t - 3)
                act.copy(xeT[:, t % 4], banks[:, t % 4, 0:D].rearrange("p (k n) -> p k n", k=DK)).then_inc(sem("xet_sb"), 1)
            act.wait_ge(sem("margin_ready"), 1)
            act.activation(weight[:, 1, :], weight[:, 0, :], ACT.Exp).then_inc(sem("margin_exp"), 1)

        def slot_bodies(eng, emit):
            emit(0, True, False)
            with eng.Fori(1, SLOTS // 2 - 1) as i:
                emit(i, False, False)
            emit(SLOTS // 2 - 1, False, True)

        def owner_of(eng, j):
            return eng.value_load(owner[0:1, j:j + 1] if isinstance(j, int) else owner[0:1, bass.ds(j, 1)],
                                  min_val=0, max_val=E - 1)

        def sp_experts(sp):
            ys = y_slots.rearrange("(j p) d -> p j d", p=P)
            sp.wait_ge(sem("xn_stored"), 16)
            sp.wait_ge(sem("logit_ps"), NT)
            load_keys_values(sp, 1)

            def emit(i, first, last):
                for r in range(2):
                    j = 2 * i + r
                    sp.wait_ge(sem("ey_sb"), j + 1)
                    sp.dma_start(tile_of(ys, j), y_slot[:, r]).then_inc(sem(f"ey_out{r}"), 16)

            slot_bodies(sp, emit)

        def pe_experts(pe):
            pe.wait_ge(sem("w1_in"), 16)
            pe.wait_ge(sem("owner_ready"), 1)
            pe.wait_ge(sem("token_ready"), 1)

            def turn_x(j, i, r):
                pe.wait_ge(sem(f"xg_in{r}"), 16 * (i + 1))
                for k in range(DK):
                    mm = pe.transpose(misc_ps[:, k * P:(k + 1) * P], xg[:, r, k * P:(k + 1) * P], ident[:])
                mm.then_inc(sem("xgt_ps"), 1)

            def hidden(e, r, part):
                for k in range(DK):
                    w = W1[:, bass.ds(e, 1), k, part * H:(part + 1) * H].rearrange("p a n -> p (a n)")
                    mm = pe.matmul(banks[:, 2 * r + part, :], xgT[:, r, k, :], w, start=(k == 0), stop=(k == DK - 1))
                mm.then_inc(sem("hg_ps" if part else "ha_ps"), 1)

            turn_x(0, 0, 0)
            pe.wait_ge(sem("xgt_sb"), 1)
            turn_x(1, 0, 1)
            e = owner_of(pe, 0)
            hidden(e, 0, 0)
            hidden(e, 0, 1)
            pe.wait_ge(sem("w2_in"), 16)

            def emit(i, first, last):
                for r in range(2):
                    j = 2 * i + r
                    final = last and r == 1
                    if not final:
                        e_next = owner_of(pe, j + 1)
                        pe.wait_ge(sem("xgt_sb"), j + 2)
                        if not (first and r == 0):
                            pe.wait_ge(sem("a_read"), j)
                        hidden(e_next, 1 - r, 0)
                    pe.wait_ge(sem("act_ready"), j + 1)
                    if not first:
                        pe.wait_ge(sem("at_sb"), j - 1)
                    for k in range(HK):
                        mm = pe.transpose(banks[:, 4 + r, k * P:(k + 1) * P], a_act[:, r, k * P:(k + 1) * P], ident[:])
                    mm.then_inc(sem("at_ps"), 1)
                    if not final:
                        if not (first and r == 0):
                            pe.wait_ge(sem("g_read"), j)
                        hidden(e_next, 1 - r, 1)
                    if not last:
                        turn_x(j + 2, i + 1, r)
                    e = owner_of(pe, j)
                    pe.wait_ge(sem("at_sb"), j + 1)
                    if not (first and r == 0):
                        pe.wait_ge(sem("ey_sb"), j)
                    for k in range(HK):
                        w = W2[:, bass.ds(e, 1), k, :].rearrange("p a n -> p (a n)")
                        mm = pe.matmul(o_ps[:, 0:D], actT[:, r, k, :], w, start=(k == 0), stop=(k == HK - 1))
                    mm.then_inc(sem("ey_ps"), 1)

            slot_bodies(pe, emit)

        def act_experts(act):
            def evacuate_x(j, r):
                act.wait_ge(sem("xgt_ps"), j + 1)
                act.copy(xgT[:, r], misc_ps[:, 0:D].rearrange("p (k n) -> p k n", k=DK)).then_inc(sem("xgt_sb"), 1)

            def silu(j, r):
                act.wait_ge(sem("a_read"), j + 1)
                act.activation(a_act[:, r, :], a_act[:, r, :], ACT.Silu).then_inc(sem("silu_done"), 1)

            evacuate_x(0, 0)
            evacuate_x(1, 1)
            silu(0, 0)

            def emit(i, first, last):
                for r in range(2):
                    j = 2 * i + r
                    act.wait_ge(sem("at_ps"), j + 1)
                    if not first:
                        act.wait_ge(sem("ey_ps"), j - 1)
                    act.copy(actT[:, r], banks[:, 4 + r, :].rearrange("p (k n) -> p k n", k=HK)).then_inc(sem("at_sb"), 1)
                    if not (last and r == 1):
                        silu(j + 1, 1 - r)
                    if not last:
                        evacuate_x(j + 2, r)

            slot_bodies(act, emit)

        def dve_experts(dve):
            dve.wait_ge(sem("owner_ready"), 1)
            dve.wait_ge(sem("b12_in"), 32)

            def inputs(j, r, wait_free):
                e = owner_of(dve, j)
                for part, buf, ps, read in ((0, a_act, "ha_ps", "a_read"), (1, g_act, "hg_ps", "g_read")):
                    dve.wait_ge(sem(ps), j + 1)
                    if wait_free:
                        if part == 0:
                            dve.wait_ge(sem("at_ps"), j - 1)
                        else:
                            dve.wait_ge(sem("act_ready"), j - 1)
                    dve.tensor_tensor(buf[:, r, :], banks[:, 2 * r + part, :],
                                      b1[:, bass.ds(e, 1), part * H:(part + 1) * H].rearrange("p a n -> p (a n)"),
                                      ALU.add).then_inc(sem(read), 1)

            inputs(0, 0, False)

            def emit(i, first, last):
                for r in range(2):
                    j = 2 * i + r
                    if not (last and r == 1):
                        inputs(j + 1, 1 - r, not (first and r == 0))
                    e = owner_of(dve, j)
                    dve.wait_ge(sem("ey_ps"), j + 1)
                    if not first:
                        dve.wait_ge(sem(f"ey_out{r}"), 16 * i)
                    dve.tensor_tensor(y_slot[:, r], o_ps[:, 0:D], b2[:, bass.ds(e, 1), :].rearrange("p a n -> p (a n)"),
                                      ALU.add).then_inc(sem("ey_sb"), 1)

            slot_bodies(dve, emit)

        def pool_experts(pool):
            def tokens_now(j, r):
                pool.tensor_copy(token_now[:, r:r + 1], column_of(token_of, j)).then_inc(sem("token_now_ready"), 1)

            def gather_x(r):
                pool.indirect_dma_start(out=xg[:, r, :], out_offset=None, in_=xn_rows,
                                        in_offset=bass.IndirectOffsetOnAxis(ap=token_now[:, r:r + 1], axis=0))\
                    .then_inc(sem(f"xg_in{r}"), 16)

            pool.wait_ge(sem("token_ready"), 1)
            for j in range(2):
                tokens_now(j, j)
            pool.wait_ge(sem("xn_stored"), 16)
            for j in range(2):
                pool.wait_ge(sem("token_now_ready"), j + 1)
                gather_x(j)
            pool.wait_ge(sem("xg_in0"), 16)
            tokens_now(2, 0)

            def emit(i, first, last):
                for r in range(2):
                    j = 2 * i + r
                    if not last:
                        pool.wait_ge(sem("xgt_ps"), j + 1)
                        pool.wait_ge(sem("token_now_ready"), j + 3)
                    pool.wait_ge(sem("silu_done"), j + 1)
                    pool.wait_ge(sem("g_read"), j + 1)
                    pool.tensor_tensor(a_act[:, r, :], a_act[:, r, :], g_act[:, r, :], ALU.mult).then_inc(sem("act_ready"), 1)
                    if not last:
                        gather_x(r)
                        pool.wait_ge(sem(f"xg_in{1 - r}"), 16 * (i + 1 + r))
                        tokens_now(j + 3, 1 - r)

            slot_bodies(pool, emit)

        def load_coupling(eng):
            n = "L1_ffn_"
            def ld(dst, src):
                eng.dma_start(dst, src).then_inc(sem("coupling_in"), 16)
            ld(cw1, t_in[n + "cn_w1"].rearrange("(k p) n -> p k n", p=P))
            ld(cw2, t_in[n + "cn_w2"].rearrange("(k p) n -> p k n", p=P))
            ld(cw3, t_in[n + "cn_w3"])
            ld(cw4, t_in[n + "cn_w4"])
            ld(gw1, t_in[n + "gc_w1"].rearrange("(k p) n -> p k n", p=P))
            ld(gw2, t_in[n + "gc_w2"])
            ld(gw3, t_in[n + "gc_w3"])
            for m in range(2):
                ld(cb1[:, m:m + 1], t_in[n + "cn_b1"][m * P:(m + 1) * P].unsqueeze(1))
            for dst, src in ((cb2, "cn_b2"), (cb3, "cn_b3"), (gb1, "gc_b1"), (gb2, "gc_b2")):
                ld(dst, t_in[n + src].unsqueeze(1))
            for dst, src in ((cb4, "cn_b4"), (gb3, "gc_b3"), (reach, "adaptive_range")):
                ld(dst, t_in[n + src].partition_broadcast(P))

        LOADS = 16

        ORDER = [("turn", 0), ("turn", 1), ("l1", 0), ("turn", 2), ("l1", 1), ("turn", 3), ("l2", 0), ("l1", 2),
                 ("l2", 1), ("l3", 0), ("l1", 3), ("l2", 2), ("l3", 1), ("l4", 0), ("l2", 3), ("l3", 2), ("l4", 1),
                 ("l3", 3), ("l4", 2), ("l4", 3)]

        def cycles(eng, emit):
            emit(0)
            with eng.Fori(1, CYCLES) as c:
                emit(c)

        def pe_coupling(pe):
            def stage(kind, j, c):
                if kind == "turn":
                    if isinstance(c, int):
                        pe.wait_ge(sem("cur_first"), 4 * j + 4)
                    else:
                        pe.wait_ge(sem("cur_ready"), NB * (c - 1) + j + 1)
                    for k in range(DK):
                        for t in range(4):
                            mm = pe.transpose(banks[:, 2 * j + k, t * P:(t + 1) * P],
                                              cur[:, 4 * j + t, k * P:(k + 1) * P], ident[:])
                    mm.then_inc(sem("turn_ps"), 1)
                elif kind == "l1":
                    pe.wait_ge(sem("turn_sb"), NB * c + j + 1)
                    for m in range(2):
                        for k in range(DK):
                            mm = pe.matmul(banks[:, 2 * j + m, :], cw1[:, k, m * P:(m + 1) * P], curT[:, j, k, :],
                                           start=(k == 0), stop=(k == DK - 1))
                    mm.then_inc(sem("l1_ps"), 1)
                elif kind == "l2":
                    pe.wait_ge(sem("l1_sb"), NB * c + j + 1)
                    for k in range(2):
                        mm = pe.matmul(banks[:, 2 * j, :], cw2[:, k, :], h1T[:, j, k, :], start=(k == 0), stop=(k == 1))
                    mm.then_inc(sem("l2_ps"), 1)
                elif kind == "l3":
                    pe.wait_ge(sem("l2_sb"), NB * c + j + 1)
                    pe.matmul(banks[0:64, 2 * j + 1, :], cw3, h2T[:, j, :], start=True, stop=True).then_inc(sem("l3_ps"), 1)
                else:
                    pe.wait_ge(sem("l3_sb"), NB * c + j + 1)
                    for t in range(4):
                        mm = pe.matmul(banks[:, 2 * j, t:t + 1], h3T[0:64, j, t * P:(t + 1) * P], cw4, start=True, stop=True)
                    mm.then_inc(sem("l4_ps"), 1)

            def global_layer(n):
                o = banks[:, 2 * NB - 1, 2 * n:2 * n + 2]
                if n == 0:
                    pe.wait_ge(sem("mean_sb"), 1)
                    for k in range(DK):
                        mm = pe.matmul(o, gw1[:, k, :], mean_sb[:, k, :], start=(k == 0), stop=(k == DK - 1))
                elif n == 1:
                    pe.wait_ge(sem("g_sb"), 1)
                    mm = pe.matmul(o[0:64], gw2, g1, start=True, stop=True)
                else:
                    pe.wait_ge(sem("g_sb"), 2)
                    pe.wait_ge(sem("gw3_wide_ready"), 1)
                    mm = pe.matmul(o, gw3_wide, g2, start=True, stop=True)
                mm.then_inc(sem("g_ps"), 1)

            pe.wait_ge(sem("coupling_in"), 16 * LOADS)

            def emit(c):
                for kind, j in ORDER:
                    if isinstance(c, int) and (kind, j) in AFTER:
                        global_layer(AFTER.index((kind, j)))
                    if isinstance(c, int) and (kind, j) == ("l1", NB - 1):
                        pe.wait_ge(sem("g_sb"), 3)
                    stage(kind, j, c)

            cycles(pe, emit)

        AFTER = [("l1", 2), ("l2", 1), ("l3", 0)]

        def act_coupling(act):
            act.wait_ge(sem("coupling_in"), 16 * LOADS)
            act.wait_ge(sem("halves_ready"), 1)

            def global_layer(n):
                dst, rows, bias = ((g1, P, gb1), (g2, 64, gb2), (g3, P, half_gb3))[n]
                src = banks[0:rows, 2 * NB - 1, 2 * n:2 * n + 2]
                act.wait_ge(sem("g_ps"), n + 1)
                if n < 2:
                    act.activation(dst, src, ACT.Gelu, bias=bias).then_inc(sem("g_sb"), 1)
                else:
                    act.activation(dst, src, ACT.Tanh, bias=bias, scale=0.5).then_inc(sem("g_sb"), 1)

            def stage(kind, j, c):
                if kind == "turn":
                    act.wait_ge(sem("turn_ps"), NB * c + j + 1)
                    if isinstance(c, int):
                        for k in range(DK):
                            a = act.activation(curT[:, j, k, :], banks[:, 2 * j + k, :], ACT.Copy,
                                               accum_out=block_sum[:, k, j:j + 1])
                    else:
                        a = act.copy(curT[:, j], banks[:, 2 * j:2 * j + 2, :])
                    a.then_inc(sem("turn_sb"), 1)
                elif kind == "l1":
                    act.wait_ge(sem("l1_ps"), NB * c + j + 1)
                    for m in range(2):
                        a = act.activation(h1T[:, j, m, :], banks[:, 2 * j + m, :], ACT.Gelu, bias=cb1[:, m:m + 1])
                    a.then_inc(sem("l1_sb"), 1)
                elif kind == "l2":
                    act.wait_ge(sem("l2_ps"), NB * c + j + 1)
                    act.activation(h2T[:, j, :], banks[:, 2 * j, :], ACT.Gelu, bias=cb2).then_inc(sem("l2_sb"), 1)
                elif kind == "l3":
                    act.wait_ge(sem("l3_ps"), NB * c + j + 1)
                    act.activation(h3T[0:64, j, :], banks[0:64, 2 * j + 1, :], ACT.Gelu, bias=cb3).then_inc(sem("l3_sb"), 1)
                else:
                    act.wait_ge(sem("l4_ps"), NB * c + j + 1)
                    act.activation(tf[:, 4 * j:4 * j + 4], banks[:, 2 * j, 0:4], ACT.Tanh, bias=half_b4,
                                   scale=0.5).then_inc(sem("tf_ready"), 1)

            def emit(c):
                for kind, j in ORDER:
                    if isinstance(c, int) and (kind, j) in AFTER:
                        global_layer(AFTER.index((kind, j)))
                    stage(kind, j, c)

            cycles(act, emit)

        def first_cur(dve, t):
            dve.tensor_scalar(tile_of(cur, t), tile_of(x, t), column_of(mean_var[:, :, 0], t), column_of(rstd, t),
                              ALU.subtract, ALU.mult).then_inc(sem("cur_first"), 1)

        def dve_coupling(dve):
            dve.wait_ge(sem("rstd_out"), 2 * OUT)
            for t in (NT - 3, NT - 2, NT - 1):
                first_cur(dve, t)
            dve.wait_ge(sem("coupling_in"), 16 * LOADS)
            dve.tensor_scalar_mul(half_b4, cb4, 0.5)
            dve.tensor_scalar_mul(half_gb3, gb3, 0.5).then_inc(sem("halves_ready"), 1)
            dve.tensor_scalar_mul(slope[:, 0:1], reach, 0.3)
            dve.tensor_scalar_mul(slope[:, 1:2], reach, -0.3)
            dve.tensor_copy(gw3_wide, gw3.broadcast_to([64, P])).then_inc(sem("gw3_wide_ready"), 1)
            dve.wait_ge(sem("turn_sb"), NB)
            sums_of = block_sum.rearrange("p k (b j) -> p k b j", b=B)
            dve.tensor_reduce(mean_sum, sums_of, AX.X, ALU.add).then_inc(sem("level_step"), 1)
            dve.wait_ge(sem("level_step"), 1)
            dve.tensor_scalar_mul(mean_sb, mean_sum, 1.0 / S).then_inc(sem("mean_sb"), 1)
            dve.wait_ge(sem("g_sb"), 3)
            dve.tensor_scalar(level_part, g3, reach, 0.7, ALU.mult, ALU.mult).then_inc(sem("level_step"), 1)
            dve.wait_ge(sem("level_step"), 2)
            dve.tensor_scalar(level[:, 0, :], level_part, 1.0, 0.1, ALU.mult, ALU.add)
            dve.tensor_scalar(level[:, 1, :], level_part, -1.0, -0.1, ALU.mult, ALU.add).then_inc(sem("level_step"), 1)
            dve.wait_ge(sem("level_step"), 3)

            def coefficients(j, c):
                b = j // (NB // B)
                tiles = slice(4 * j, 4 * j + 4)
                dve.wait_ge(sem("tf_ready"), NB * c + j + 1)
                t2 = tf[:, tiles].unsqueeze(2).broadcast_to([P, 4, 2])
                dve.tensor_scalar(coef[:, tiles, 0:4:3], t2, slope[:, 0:1], level[:, 0, b:b + 1], ALU.mult, ALU.add)
                dve.tensor_scalar(coef[:, tiles, 1:3], t2, slope[:, 1:2], level[:, 1, b:b + 1], ALU.mult, ALU.add)\
                    .then_inc(sem("coef_ready"), 1)

            def update(j, c):
                tiles = slice(4 * j, 4 * j + 4)
                dve.wait_ge(sem("twist_ready"), NB * c + j + 1)
                dve.tensor_tensor(cur[:, tiles, :], cur[:, tiles, :], twist[:, tiles, :], ALU.add)\
                    .then_inc(sem("cur_ready"), 1)

            def emit(c):
                coefficients(0, c)
                coefficients(1, c)
                update(0, c)
                coefficients(2, c)
                coefficients(3, c)
                for j in range(1, NB):
                    update(j, c)

            cycles(dve, emit)
            for j in range(NB):
                tiles = slice(4 * j, 4 * j + 4)
                dve.wait_ge(sem("cur_ready"), NB * (CYCLES - 1) + j + 1)
                dve.scalar_tensor_tensor(x[:, tiles, :], cur[:, tiles, :], gates[:, 3:4], x[:, tiles, :],
                                         ALU.mult, ALU.add).then_inc(sem("x_final"), 1)

        def pool_coupling(pool):
            with pool.Fori(0, CYCLES) as c:
                for j in range(NB):
                    tiles = slice(4 * j, 4 * j + 4)
                    pool.wait_ge(sem("coef_ready"), NB * c + j + 1)
                    for h in range(2):
                        src = slice(128, 256) if h == 0 else slice(0, 128)
                        p = pool.tensor_tensor(
                            twist[:, tiles, h * 128:(h + 1) * 128].rearrange("p t (s n) -> p t s n", s=2),
                            cur[:, tiles, src].rearrange("p t (s n) -> p t s n", s=2),
                            coef[:, tiles, 2 * h:2 * h + 2].unsqueeze(3).broadcast_to([P, 4, 2, 64]), ALU.mult)
                    p.then_inc(sem("twist_ready"), 1)

        @block.sync
        def _(sp):
            xs = t_in["x"].rearrange("b s d -> (b s) d").rearrange("(t p) d -> p t d", p=P)
            c2 = t_in["ctx_768"].rearrange("b s d -> (b s) d")
            sp.dma_start(ctx_rows[:, 0:2], c2[0:256].rearrange("(r p) d -> p r d", p=P)).then_inc(sem("ctx_in"), 16)
            sp.dma_start(ctx_rows[0:KEYS - 256, 2], c2[256:KEYS]).then_inc(sem("ctx_in"), 16)
            sp.dma_start(x[:, 0:4], xs[:, 0:4]).then_inc(sem("x_first"), 16)
            load_keys_values(sp, 0)
            for name, g in (("g_xattn", 0), ("g_ffn", 2)):
                sp.dma_start(gates[:, g:g + 2], t_in[name].partition_broadcast(P)).then_inc(sem("gates_in"), 16)
            load_attention(sp, 0)
            sp.dma_start(x[:, 4:NT], xs[:, 4:NT]).then_inc(sem("x_rest"), 16)
            sp.dma_start(Wr[:], t_in["L0_ffn_Wr"].rearrange("(k p) e -> p k e", p=P)).then_inc(sem("wr_in"), 16)
            sp.dma_start(br[:], t_in["L0_ffn_br"].partition_broadcast(P)).then_inc(sem("wr_in"), 16)
            sp.dma_start(W1, t_in["L0_ffn_W1"].rearrange("e (k p) n -> p e k n", p=P)).then_inc(sem("w1_in"), 16)
            sp.wait_ge(sem("xe_ready"), NT)
            sp.dma_start(xn_rows.rearrange("(t p) d -> p t d", p=P), xn_all).then_inc(sem("xn_stored"), 16)
            sp.dma_start(b1[:], t_in["L0_ffn_b1"].rearrange("e n -> (e n)").partition_broadcast(P)
                         .rearrange("p (e n) -> p e n", e=E)).then_inc(sem("b12_in"), 16)
            sp.dma_start(b2[:], t_in["L0_ffn_b2"].rearrange("e n -> (e n)").partition_broadcast(P)
                         .rearrange("p (e n) -> p e n", e=E)).then_inc(sem("b12_in"), 16)
            sp.dma_start(W2[:], t_in["L0_ffn_W2"].rearrange("e (k p) n -> p e k n", p=P)).then_inc(sem("w2_in"), 16)
            sp_experts(sp)
            for r in range(2):
                sp.wait_ge(sem(f"ey_out{r}"), 16 * (SLOTS // 2))
            load_attention(sp, 1)
            load_coupling(sp)
            outs = out.rearrange("b s d -> (b s) d").rearrange("(t p) d -> p t d", p=P)
            for j in range(NB):
                sp.wait_ge(sem("x_final"), j + 1)
                sp.dma_start(outs[:, 4 * j:4 * j + 4], x[:, 4 * j:4 * j + 4]).then_inc(sem("stored"), 16)
            sp.wait_ge(sem("stored"), 16 * NB)

        @block.gpsimd
        def _(pool):
            pool.memset(ident[:], 0.0).then_inc(sem("ident_zero"), 1)
            pool.memset(ones[:], 1.0).then_inc(sem("ones_ready"), 1)
            pool.iota(iota_e[:], [[1, E]], base=0, channel_multiplier=0, allow_small_or_imprecise_dtypes=True)
            pool.iota(iota_t[:], [[P, NT]], base=0, channel_multiplier=0, allow_small_or_imprecise_dtypes=True)
            pool.iota(iota_s, [[1, SLOTS]], base=0, channel_multiplier=0, allow_small_or_imprecise_dtypes=True)
            pool.iota(slot_start, [[P, SLOTS]], base=0, channel_multiplier=0, allow_small_or_imprecise_dtypes=True)
            pool.iota(iota_row, [[1, P]], base=0, channel_multiplier=0, allow_small_or_imprecise_dtypes=True)
            pool.iota(token_id, [[P, NT]], base=0, channel_multiplier=1, allow_small_or_imprecise_dtypes=True)\
                .then_inc(sem("iota_ready"), 1)
            pool.wait_ge(sem("ones_ready"), 1)
            pool.affine_select(out=before[:], in_=ones[:], compare_op=ALU.is_gt, fill=0.0, base=0,
                               pattern=[[1, P]], channel_multiplier=-1).then_inc(sem("before_ready"), 1)
            pool.memset(zero_eps[:, 0:1], 0.0)
            pool.memset(zero_eps[:, 1:2], EPS)
            pool.memset(token_of[:, SLOTS:], 0)
            pool.memset(minus_half[:], -0.5).then_inc(sem("eps_ready"), 1)
            pool.memset(ctx_rem, 0.0)
            pool.memset(ctx_rem1[:], 0.0).then_inc(sem("rem_zero"), 1)
            pool.wait_ge(sem("ident_zero"), 1)
            pool.affine_select(out=ident[:], in_=ident[:], compare_op=ALU.not_equal, fill=1.0, base=0,
                               pattern=[[-1, P]], channel_multiplier=1).then_inc(sem("ident_ready"), 1)
            pool.memset(K0, 0.0)
            pool.memset(V, 0.0).then_inc(sem("kv_zero"), 1)
            pool.memset(probs, 0.0).then_inc(sem("pads_zero"), 1)
            pool_attention(pool, L0)
            pool_experts(pool)
            pool.wait_ge(sem("ey_sb"), SLOTS)
            pool.memset(V[:, 0], 0.0).then_inc(sem("kv_zero"), 1)
            for r in range(2):
                pool.wait_ge(sem(f"ey_out{r}"), 16 * (SLOTS // 2))
            for t in range(5):
                slots_now(pool, t, t % 2, None if t < 2 else t - 1)
                pool.wait_ge(sem("slot_now_ready"), t + 1)
                gather(pool, t, t % 2)
                if t == 1:
                    pool.memset(probs, 0.0).then_inc(sem("pads_zero"), 1)
                    pool.wait_ge(sem("bo_in"), 32)
                    pool.tensor_tensor(gated_bo[:], gated_bo[:], gates[:, 1:2].broadcast_to([P, D]), ALU.mult)\
                        .then_inc(sem("gbo_ready"), 1)
                    pool.wait_ge(sem("gbo_ready"), 2)
            pool_attention(pool, L1)
            pool_coupling(pool)

        @block.scalar
        def _(act):
            act.wait_ge(sem("gates_in"), 32)
            act.activation(gates[:], gates[:], ACT.Tanh).then_inc(sem("gates_ready"), 1)
            act_attention(act, L0)
            act_routing(act)
            act_experts(act)
            act_attention(act, L1)
            act_coupling(act)

        @block.vector
        def _(dve):
            dve.wait_ge(sem("ctxT_ps"), 1)
            dve.tensor_copy(ctxT[:, :, :], banks[0:CK, 0:2, 0:KEYS]).then_inc(sem("ctxT_ready"), 1)
            dve.wait_ge(sem("ctxT_ready"), 1)
            dve.wait_ge(sem("rem_zero"), 1)
            for j in range(4):
                for k in range(2):
                    last = dve.tensor_copy(ctx_rem[:, k, :, j * 32:j * 32 + NKEY - P],
                                           ctxT[:, k, :].rearrange("p (b n) -> p b n", b=2)[:, :, P:NKEY])
            last.then_inc(sem("rem_ready"), 1)
            for j in range(2):
                last = dve.tensor_copy(ctx_rem1[:, :, j * 64:j * 64 + KEYS - 256], ctxT[:, :, 256:KEYS])
            last.then_inc(sem("rem_ready"), 1)
            dve_attention(dve, L0)
            dve.wait_ge(sem("iota_ready"), 1)
            dve_routing(dve)
            dve_experts(dve)
            dve.wait_ge(sem("weight_ready"), 1)
            dve_attention(dve, L1)
            dve_coupling(dve)

        @block.tensor
        def _(pe):
            pe.wait_ge(sem("ctx_in"), 32)
            pe.wait_ge(sem("ident_ready"), 1)
            for k in range(2):
                for r in range(3):
                    n = P if r < 2 else KEYS - 256
                    mm = pe.transpose(banks[0:CK, k, r * P:r * P + n], ctx_rows[0:n, r, k * CK:(k + 1) * CK],
                                      ident[0:n, 0:n])
            mm.then_inc(sem("ctxT_ps"), 1)
            pe.wait_ge(sem("ctxT_ready"), 1)
            pe_attention(pe, L0)
            pe_routing(pe)
            pe_experts(pe)
            pe_attention(pe, L1)
            pe_coupling(pe)


_INS = ["x", "ctx_768", "g_xattn", "g_ffn"] + [f"L0_xattn_{n}" for n in ("Wq", "Wk", "Wv", "Wo", "bo")] \
    + [f"L0_ffn_{n}" for n in ("W1", "b1", "W2", "b2", "Wr", "br")] \
    + [f"L1_xattn_{n}" for n in ("Wq", "Wk", "Wv", "Wout", "bout")] \
    + [f"L1_ffn_cn_{n}{i}" for i in (1, 2, 3, 4) for n in ("w", "b")] \
    + [f"L1_ffn_gc_{n}{i}" for i in (1, 2, 3) for n in ("w", "b")] + ["L1_ffn_adaptive_range"]


def kernel(**inputs):
    import concourse.bacc as bacc
    from concourse.bass_utils import run_bass_kernel_spmd

    nc = bacc.Bacc("TRN2", target_bir_lowering=False, num_devices=1)
    arrays, aps = {}, {}
    for name in _INS:
        a = np.ascontiguousarray(inputs[name])
        arrays[f"in_{name}"] = a
        aps[name] = nc.dram_tensor(f"in_{name}", a.shape, mybir.dt.from_np(a.dtype), kind="ExternalInput").ap()
    shape = arrays["in_x"].shape
    out = nc.dram_tensor("out", shape, F32, kind="ExternalOutput").ap()
    flamingo(nc, aps, out)
    r = run_bass_kernel_spmd(nc, [arrays], core_ids=[0])
    return r.results[0]["out"]
```

```python
from contextlib import ExitStack

import numpy as np

import concourse.bass as bass
from concourse import mybir

F32 = mybir.dt.float32
F32R = mybir.dt.float32r
U32 = mybir.dt.uint32
ALU = mybir.AluOpType
ACT = mybir.ActivationFunctionType
AX = mybir.AxisListType

P = 128
EPS = 1e-5


class Attention:

    def __init__(self, index, heads_per_step, keys, remainder_width, scale, bodies):
        self.index = index
        self.hs = heads_per_step
        self.dh = 256 // heads_per_step
        self.keys = keys
        self.rw = remainder_width
        self.chunks = 4 // heads_per_step
        self.rem = keys - 128 * self.chunks
        self.width = 128 * self.chunks + remainder_width
        self.scale = scale
        self.bodies = bodies
        self.batches = 2 if keys == 154 else 1
        self.score_cols = 308 + 2 * index


def flamingo(nc, t_in, out):
    B, S, D = t_in["x"].shape
    T = B * S
    NT = T // P
    DK = D // P
    _, NKEY, DC = t_in["ctx_768"].shape
    CK = DC // 2
    KEYS = B * NKEY
    INNER = t_in["L0_xattn_Wq"].shape[1]
    NC = INNER // P
    E, _, H2 = t_in["L0_ffn_W1"].shape
    H = H2 // 2
    HK = H // P

    L0 = Attention(0, 4, NKEY, 32, 64 ** -0.5,
                   [(0, 1, True, 0, 0, 0), (1, 3, False, 0, 0, 0), (3, 4, True, 0, 0, 1),
                    (4, 5, True, 0, 1, 1), (5, 7, False, 1, 1, 1), (7, 8, True, 1, 1, 1)])
    L1 = Attention(1, 2, KEYS, 64, 1.5 * 128 ** -0.5,
                   [(0, 1, True, 0, 0, 0), (1, 5, False, 0, 0, 0), (5, 6, True, 0, 0, 0), (6, 7, True, 0, 0, 0),
                    (7, 8, True, 0, 0, 0)])
    STEPS = 4 * NT
    TOP = 2
    SLOTS = (TOP * T + E * (P - 1)) // P
    assert SLOTS % 2 == 1

    with ExitStack() as ctx:
        def sb(name, shape, dt=F32):
            return ctx.enter_context(nc.sbuf_tensor(name, shape, dt))

        sems = {}

        def sem(name):
            if name not in sems:
                sems[name] = ctx.enter_context(nc.semaphore(name))
            return sems[name]

        banks = ctx.enter_context(nc.psum_tensor("banks", [P, 8, 512], F32))
        x = sb("x", [P, NT, D])
        ident = sb("ident", [P, P])
        gates = sb("gates", [P, 4])
        stats = sb("stats", [P, NT, 6])
        mean_var = sb("mean_var", [P, NT, 2])
        moments = sb("moments", [P, 4, 2])
        loop_stats = sb("loop_stats", [P, 4, 6])
        zero_eps = sb("zero_eps", [P, 2])
        table = sb("table", [P, 3])
        minus_half = sb("minus_half", [P, NT])
        rstd = sb("rstd", [P, NT])
        xn = sb("xn", [P, D])
        x_biased = sb("x_biased", [P, 2, D])
        xT = sb("xT", [P, 2, DK, P])
        gated_bo = sb("gated_bo", [P, D])
        ctxT = sb("ctxT", [CK, 2, KEYS])
        ctx_rem1 = sb("ctx_rem1", [CK, 2, P])
        ones = sb("ones", [P, P])
        before = sb("before", [P, P])

        def split_parts(offset, **shapes):
            with ExitStack() as place:
                if offset:
                    place.enter_context(nc.sbuf_tensor("before_" + "_".join(shapes), [P, offset], F32))
                return [place.enter_context(nc.sbuf_tensor(n, shape, F32R)) for n, shape in shapes.items()]

        KW = KEYS + 2
        K_low, Wo_low = split_parts(E * DK * H2 - NC * (KW + D), K_low=[P, NC, KW], Wo_low=[P, NC, D])
        BLK = 4 * P
        NB = T // BLK
        CYCLES = 3
        curT_high, = split_parts(NT * D, curT_high=[P, NB, DK, BLK])
        cw1_high, cw1_low = split_parts(E * DK * H2 - NC * (KW + D) - 2 * DK * 256, cw1_high=[P, DK, 256],
                                        cw1_low=[P, DK, 256])
        w1_region = sb("W1", [P, E * DK * H2])
        W1 = w1_region[:].rearrange("p (e k n) -> p e k n", e=E, k=DK)
        class Region:
            def __init__(self, name, size):
                self.buffer, self.at = sb(name, [P, size]), 0

            def part(self, n, pattern="p n -> p n", rows=P, dt=F32, **dims):
                view = self.buffer[0:rows, self.at:self.at + n]
                self.at += n
                if dt != F32:
                    view = view.bitcast(dt)
                return view.rearrange(pattern, **dims) if dims else view

        A_SIZE = 2 * NC * 308 + 2 * NC * 3 * P + 6 * 640 + 4 * NC * P
        Wo_high, = split_parts(NC * KW, Wo_high=[P, NC, D])
        K_high, = split_parts(2 * NC * 308 + NC * 3 * P, K_high=[P, NC, KW])
        oT0_high, = split_parts(A_SIZE - 2 * NC * P, oT0_high=[P, 2, NC, P])
        q_high, q_low = split_parts(A_SIZE - 4 * NC * P, q_high=[P, 2, NC, P], q_low=[P, 2, NC, P])
        reg_a = Region("region_a", A_SIZE)
        K0 = reg_a.part(2 * NC * 308, "p (b c n) -> p b c n", b=2, c=NC)
        V = reg_a.part(2 * NC * 3 * P, "p (b c i n) -> p b c i n", b=2, c=NC, i=3)
        probs = reg_a.part(2 * 640, "p (r n) -> p r n", r=2)
        normed = reg_a.part(2 * 640, "p (r n) -> p r n", r=2)
        probsT = reg_a.part(2 * 640, "p (r n) -> p r n", r=2)
        q = reg_a.part(2 * NC * P, "p (r c n) -> p r c n", r=2, c=NC)
        oT = reg_a.part(2 * NC * P, "p (r c n) -> p r c n", r=2, c=NC)
        ctx_rem = oT.rearrange("p r c n -> p (r c n)")[0:CK, 0:4 * P].rearrange("p (k b n) -> p k b n", k=2, b=2)
        ctx_rows = probsT.rearrange("p r n -> p (r n)")[:, 0:3 * DC].rearrange("p (r d) -> p r d", r=3)
        K1 = K0.rearrange("p b c n -> p (b c n)")[:, 0:NC * KW].rearrange("p (c n) -> p c n", c=NC)
        reg_a.at = 0
        b1 = reg_a.part(E * H2, "p (e n) -> p e n", e=E)
        W2 = reg_a.part(E * HK * D, "p (e k n) -> p e k n", e=E, k=HK)
        b2 = reg_a.part(E * D, "p (e n) -> p e n", e=E)
        reg_a.at = 0
        h1T = reg_a.part(NB * 2 * BLK, "p (j m n) -> p j m n", j=NB, m=2)
        h2T = reg_a.part(NB * BLK, "p (j n) -> p j n", j=NB)
        h3T = reg_a.part(NB * BLK, "p (j n) -> p j n", j=NB)
        twist = reg_a.part(4 * D * NB, "p (t d) -> p t d", d=D)

        Wo0_high, Wo0_low = split_parts(0, Wo0_high=[P, NC, D], Wo0_low=[P, NC, D])
        oT_high, oT_low = split_parts(0, oT_high=[P, 2, NC, P], oT_low=[P, 2, NC, P])
        curT_low, = split_parts(NC * 2 * 2 * P, curT_low=[P, NB, DK, BLK])
        oT0_low, = split_parts(6 * INNER, oT0_low=[P, 2, NC, P])
        oT_parts = ((oT0_high, oT0_low), (oT_high, oT_low))
        Wo_parts = ((Wo0_high, Wo0_low), (Wo_high, Wo_low))
        reg_b = Region("region_b", 8704)
        Wk = reg_b.part(2 * INNER, "p (k n) -> p k n", rows=CK, k=2)
        Wv = reg_b.part(2 * INNER, "p (k n) -> p k n", rows=CK, k=2)
        Wq = reg_b.part(DK * INNER, "p (k n) -> p k n", k=DK)
        Wo = reg_b.part(NC * D, "p (c n) -> p c n", c=NC)
        reg_b.at = 0
        xn_all = reg_b.part(NT * D, "p (t d) -> p t d", t=NT)
        xg = reg_b.part(2 * D, "p (r d) -> p r d", r=2)
        xgT = reg_b.part(2 * D, "p (r k n) -> p r k n", r=2, k=DK)
        y_slot = reg_b.part(2 * D, "p (r d) -> p r d", r=2)
        a_act = reg_b.part(2 * H, "p (r n) -> p r n", r=2)
        g_act = reg_b.part(2 * H, "p (r n) -> p r n", r=2)
        xeT = reg_b.buffer[:, reg_b.at - 4 * H:reg_b.at - 4 * H + 4 * D].rearrange("p (r k n) -> p r k n", r=4, k=DK)
        actT = reg_b.part(2 * H, "p (r k n) -> p r k n", r=2, k=HK)

        F16 = mybir.dt.float16
        reg_b.at = NT * D
        in_row = reg_b.part(TOP * NT * P // 2, "p (q m) -> p q m", dt=F16, q=TOP * NT)
        numbered = reg_b.part(TOP * NT * SLOTS // 2, "p (q j) -> p q j", dt=F16, q=TOP * NT)
        in_tile = reg_b.part(TOP * NT * SLOTS, "p (q j) -> p q j", q=TOP * NT)

        reg_b.at = 6 * INNER + NC * D
        iota_s = reg_b.part(SLOTS)
        slot_start = reg_b.part(SLOTS)
        iota_row = reg_b.part(P)
        token_id = reg_b.part(NT)
        iota_row16 = reg_b.part(P // 2, dt=F16)

        at = [0]

        def late(n, pattern="p n -> p n", rows=P, **dims):
            view = w1_region[0:rows, at[0]:at[0] + n]
            at[0] += n
            return view.rearrange(pattern, **dims) if dims else view

        cur = late(NT * D, "p (t d) -> p t d", t=NT)
        late(NB * DK * BLK)
        cw1 = late(DK * 256, "p (k n) -> p k n", k=DK)
        cw2 = late(2 * 128, "p (k n) -> p k n", k=2)
        cw3, cw4 = late(64), late(1, rows=64)
        cb1, cb2, cb3, cb4 = late(2), late(1), late(1, rows=64), late(1)
        gw1 = late(DK * 128, "p (k n) -> p k n", k=DK)
        gw2, gw3 = late(64), late(1, rows=64)
        gb1, gb2, gb3 = late(1), late(1, rows=64), late(1)
        reach = late(1)
        gw3_wide = late(P, rows=64)
        mean_sb = late(4, "p (k b) -> p k b", k=DK)
        g1, g2, g3 = late(2), late(2, rows=64), late(2)
        half_b4, half_gb3 = late(1), late(1)
        slope = late(2)
        level = late(4, "p (q b) -> p q b", q=2)
        level_part = late(2)
        block_sum = late(DK * NB, "p (k j) -> p k j", k=DK)
        mean_sum = late(4, "p (k b) -> p k b", k=DK)
        tf = late(NT)
        y_pair = late(4 * D, "p (r i d) -> p r i d", r=2, i=2)
        coef = late(NT * 4, "p (t q) -> p t q", t=NT)

        assert at[0] <= E * DK * H2 - NC * (KW + D) - 2 * DK * 256

        Wr = sb("Wr", [P, DK, E])
        br = sb("br", [P, E])
        logits = sb("logits", [P, NT, E])
        top = sb("top", [P, NT, 8])
        top_at = sb("top_at", [P, NT, 8], U32)
        top_atf = sb("top_atf", [P, NT, TOP])
        chosen = sb("chosen", [P, TOP, NT, E])
        either = sb("either", [P, NT, E])
        totals = sb("totals", [P, NT, E])
        upto = sb("upto", [P, NT, E])
        place = sb("place", [P, NT, E])
        place_i = sb("place_i", [P, NT, E])
        slot_f = sb("slot_f", [P, TOP, NT])
        slot = sb("slot", [P, TOP, NT], U32)
        slot_now = sb("slot_now", [P, 2, TOP], U32)
        weight = sb("weight", [P, 4, NT])
        tiles_cmp = sb("tiles_cmp", [P, E, NT])
        tiles_of = sb("tiles_of", [P, E])
        tiles_end = sb("tiles_end", [P, E])
        tiles_base = sb("tiles_base", [P, E])
        iota_e = sb("iota_e", [P, E])
        iota_t = sb("iota_t", [P, NT])
        slot_part = sb("slot_part", [P, 2, TOP, NT])
        slot_low = sb("slot_low", [P, TOP, NT], U32)
        token_of = sb("token_of", [P, SLOTS], U32)
        token_now = sb("token_now", [P, 2], U32)
        owner_cmp = xT.ap().rearrange("p r k n -> p (r k n)")[0:1, 0:SLOTS * E].rearrange("p (s e) -> p s e", s=SLOTS)
        owner_f = sb("owner_f", [1, SLOTS])
        owner = sb("owner", [1, SLOTS], mybir.dt.int32)
        xn_rows = nc.dram_tensor("xn_rows", [T, D], F32, kind="Internal").ap()
        y_slots = nc.dram_tensor("y_slots", [SLOTS * P, D], F32, kind="Internal").ap()

        row_of = slot_part[:, 0].rearrange("p c t -> p (c t)")
        start_of = slot_part[:, 1].rearrange("p c t -> p (c t)")
        negmax = sb("negmax", [P, 2, 4])
        bias1 = sb("bias1", [P, 2, 4])
        shifted = sb("shifted", [P, 2, 4])
        sums = sb("sums", [P, 2, 4])
        recip = sb("recip", [P, 2, 4])
        kmean = sb("kmean", [P, NC])

        scores = banks[:, 0:4, :].rearrange("p (r u) n -> p r u n", r=2)
        probsT_ps = banks[:, 4:6, :].rearrange("p u n -> p (u n)")
        o_ps = banks[:, 6, :]
        misc_ps = banks[:, 7, :]

        block = ctx.enter_context(nc.Block())

        def finals(eng, *names_counts):
            for name, count in names_counts:
                eng.wait_ge(sem(name), count)

        def load_keys_values(eng, layer):
            for w, dst, name in (("Wk", Wk, "wk_in"), ("Wv", Wv, "wv_in")):
                src = t_in[f"L{layer}_xattn_{w}"].rearrange("(k p) n -> p k n", p=CK)
                eng.dma_start(dst, src).then_inc(sem(name), 16)

        def load_attention(eng, layer):
            n = f"L{layer}_xattn_"
            eng.dma_start(Wq[:], t_in[n + "Wq"].rearrange("(k p) n -> p k n", p=P)).then_inc(sem("wq_in"), 16)
            wo, bo = ("Wo", "bo") if layer == 0 else ("Wout", "bout")
            eng.dma_start(Wo[:], t_in[n + wo].rearrange("(k p) n -> p k n", p=P)).then_inc(sem("wo_in"), 16)
            eng.dma_start(gated_bo[:], t_in[n + bo].partition_broadcast(P)).then_inc(sem("bo_in"), 16)

        def kv_units(L):
            units = [("k", c, 0) for c in range(NC)]
            if L.index == 0:
                units += [("v", b, half) for b in range(2) for half in range(2)]
            else:
                units += [("v", chunk, half) for chunk in range(2) for half in range(2)]
            units += [("r", b, half) for b in range(L.batches) for half in range(2)]
            return units

        KV0 = len(kv_units(L0))
        KV1 = KV0 + len(kv_units(L1))

        def kv_bank(n):
            return banks[:, n % 4] if n < NC else banks[:, 4 + (n - NC) % 3]

        def pe_kv(pe, L, kinds):
            base = KV0 * L.index
            pe.wait_ge(sem("wk_in"), 16 * (L.index + 1))
            for n, (kind, a, half) in enumerate(kv_units(L)):
                if kind not in kinds:
                    continue
                if n == NC:
                    pe.wait_ge(sem("wv_in"), 16 * (L.index + 1))
                    pe.wait_ge(sem("rem_ready"), 2)
                if n >= (4 if n < NC else NC + 3):
                    pe.wait_ge(sem("kv_sb"), base + n - (3 if n < NC else 2))
                bank = kv_bank(n)
                for k in range(2):
                    if kind == "k":
                        o, l, r = bank[:, 0:KEYS], Wk[:, k, a * P:(a + 1) * P], ctxT[:, k, :]
                    else:
                        r = Wv[:, k, half * 512:(half + 1) * 512]
                        start = a * (NKEY if L.index == 0 else P)
                        l = ctxT[:, k, start:start + P] if kind == "v" else (
                            ctx_rem[:, k, a, :] if L.index == 0 else ctx_rem1[:, k, :])
                        o = bank
                    mm = pe.matmul(o, l, r, start=(k == 0), stop=(k == 1))
                mm.then_inc(sem("kv_ps"), 1)

        def dve_kv(dve, L, kinds, halves=range(NC)):
            base = KV0 * L.index
            for n, (kind, a, half) in enumerate(kv_units(L)):
                if kind not in kinds or a not in halves:
                    continue
                dve.wait_ge(sem("kv_ps"), base + n + 1)
                bank = kv_bank(n)
                if kind == "k" and L.index == 0:
                    for i in range(2):
                        rows = slice(64 * i, 64 * i + 64)
                        last = dve.tensor_scalar_mul(K0[rows, :, a, i * NKEY:(i + 1) * NKEY],
                                                     bank[rows, 0:KEYS].rearrange("p (b n) -> p b n", b=2), L.scale)
                elif kind == "k":
                    last = dve.tensor_scalar(K1[:, a, 0:KEYS], bank[:, 0:KEYS], L.scale, 0.0, ALU.mult, ALU.add,
                                             accum_out=kmean[:, a:a + 1])
                elif kind == "v" and L.index == 0:
                    for i in range(2):
                        last = dve.tensor_copy(
                            V[:, a, half * 4:half * 4 + 4, i, i * 64:(i + 1) * 64],
                            bank.rearrange("p (c i n) -> p c i n", c=4, i=2)[:, :, i, :])
                elif kind == "v":
                    last = dve.tensor_copy(V[:, 0, half * 4:half * 4 + 4, a, :],
                                           bank.rearrange("p (c n) -> p c n", c=4))
                else:
                    for j in range(L.hs):
                        rows = slice(L.rw * j, L.rw * (j + 1))
                        blk = (2 * j) // L.hs
                        col = (j * L.dh) % P
                        for g in range(2):
                            last = dve.tensor_copy(
                                V[rows, a, half * 4 + 2 * g + blk, 2, col:col + L.dh],
                                bank[rows, (g * L.hs + j) * L.dh:(g * L.hs + j + 1) * L.dh])
                last.then_inc(sem("kv_sb"), 1)

        def bodies(eng, L, emit):
            for first, end, peeled, before, batch, after in L.bodies:
                if peeled:
                    emit(first, first == 0, end == NT // 2, before, batch, after)
                else:
                    with eng.Fori(first, end) as i:
                        emit(i, False, False, before, batch, after)

        def pe_split(pe, o, left, right, start, stop):
            pe.matmul(o, left[0], right[0], start=start, stop=False)
            pe.matmul(o, left[0], right[1], start=False, stop=False)
            return pe.matmul(o, left[1], right[0], start=False, stop=stop)

        def pe_scores(pe, L, s, g, r, b):
            for u in range(2):
                c, o = 2 * g + u, scores[:, g % 2, u, 0:L.score_cols]
                if L.index == 0:
                    mm = pe.matmul(o, q[:, r, c, :], K0[:, b, c, :], start=True, stop=True)
                else:
                    mm = pe_split(pe, o, (q_high[:, r, c, :], q_low[:, r, c, :]), (K_high[:, c, :], K_low[:, c, :]),
                                  True, True)
            mm.then_inc(sem("s_ps"), 1)

        def pe_transpose_x(pe, src):
            for k in range(DK):
                mm = pe.transpose(misc_ps[:, k * P:(k + 1) * P], src[:, k * P:(k + 1) * P], ident[:])
            mm.then_inc(sem("xt_ps"), 1)

        def pe_q(pe, r, half):
            for c in range(4):
                for k in range(DK):
                    mm = pe.matmul(misc_ps[:, c * P:(c + 1) * P], Wq[:, k, (4 * half + c) * P:(4 * half + c + 1) * P],
                                   xT[:, r, k, :], start=(k == 0), stop=(k == DK - 1))
            mm.then_inc(sem("q_ps"), 1)

        def pe_probsT(pe, L, g):
            for m in range(5):
                mm = pe.transpose(probsT_ps[:, m * P:(m + 1) * P], normed[:, g % 2, m * P:(m + 1) * P], ident[:])
            mm.then_inc(sem("pt_ps"), 1)

        def pe_pv(pe, g, b):
            for u in range(2):
                for i in range(3):
                    m = 2 * u + i if i < 2 else 4
                    mm = pe.matmul(o_ps[:, u * P:(u + 1) * P], V[:, b, 2 * g + u, i, :],
                                   probsT[:, g % 2, m * P:(m + 1) * P], start=(i == 0), stop=(i == 2))
            mm.then_inc(sem("o_ps"), 1)

        def pe_out(pe, L, r):
            for c in range(NC):
                mm = pe_split(pe, misc_ps[:, 0:D], [part[:, r, c, :] for part in oT_parts[L.index]],
                              [part[:, c, :] for part in Wo_parts[L.index]], c == 0, c == NC - 1)
            mm.then_inc(sem("y_ps"), 1)

        def pe_attention(pe, L):
            t0, s0 = NT * L.index, STEPS * L.index
            pe_kv(pe, L, "k" if L.index == 0 else "kv")
            pe.wait_ge(sem("xn_ready"), t0 + 1)
            pe_transpose_x(pe, xn)
            pe.wait_ge(sem("wq_in"), 16 * (L.index + 1))
            pe.wait_ge(sem("xt_sb"), t0 + 1)
            pe_q(pe, 0, 0)
            pe.wait_ge(sem("q_sb"), 2 * t0 + 1)
            pe_q(pe, 0, 1)
            pe.wait_ge(sem("kv_sb"), KV0 * L.index + NC)
            if L.index == 1:
                pe.wait_ge(sem("K_split"), 1)
            pe_scores(pe, L, 0, 0, 0, 0)
            pe_scores(pe, L, 1, 1, 0, 0)
            pe_kv(pe, L, "vr" if L.index == 0 else "r")
            pe.wait_ge(sem("kv_sb"), KV0 if L.index == 0 else KV1)

            def emit(i, first, last, before, batch, after):
                for r in range(2):
                    t = 2 * i + r
                    t_first, t_last = first and r == 0, last and r == 1
                    for g in range(4):
                        s = 4 * t + g
                        if not (t_last and g == 3) and not (t_first and g == 0):
                            gn = (g + 1) % 4
                            if gn == 0:
                                pe.wait_ge(sem("q_sb"), 2 * (t0 + t) + 3)
                            elif gn == 2:
                                pe.wait_ge(sem("q_sb"), 2 * (t0 + t) + 2)
                            pe.wait_ge(sem("p_exp"), s0 + s)
                            nb = after if (g == 3 and r == 1) else batch
                            pe_scores(pe, L, s + 1, gn, r if g < 3 else 1 - r, nb)
                        if not (t_first and g == 0):
                            pe.wait_ge(sem("p_norm"), s0 + s)
                            if not (t_first and g == 1):
                                pe.wait_ge(sem("pt_sb_act"), s0 + s - 1)
                                pe.wait_ge(sem("pt_sb_dve"), s0 + s - 1)
                            pe_probsT(pe, L, (g - 1) % 4)
                        if g == 0 and not t_last:
                            pe.wait_ge(sem("q_sb"), 2 * (t0 + t) + 2)
                            if not first:
                                pe.wait_ge(sem("y_done"), t0 + t - 1)
                            pe.wait_ge(sem("xn_ready"), t0 + t + 2)
                            pe_transpose_x(pe, xn)
                        if g == 1 and not t_last:
                            pe.wait_ge(sem("xt_sb"), t0 + t + 2)
                            pe_q(pe, 1 - r, 0)
                        if g == 2 and not t_last:
                            pe.wait_ge(sem("q_sb"), 2 * (t0 + t) + 3)
                            pe_q(pe, 1 - r, 1)
                        if g == 3 and not t_first:
                            if not t_last:
                                pe.wait_ge(sem("q_sb"), 2 * (t0 + t) + 4)
                            else:
                                pe.wait_ge(sem("y_done"), t0 + t - 1)
                            pe.wait_ge(sem("o_sb"), s0 + 4 * t)
                            if first:
                                pe.wait_ge(sem("Wo_split"), 2 * (L.index + 1))
                            pe_out(pe, L, 1 - r)
                        if not (t_first and g < 2):
                            pe.wait_ge(sem("pt_sb_act"), s0 + s - 1)
                            pe.wait_ge(sem("pt_sb_dve"), s0 + s - 1)
                            if not (t_first and g == 2):
                                pe.wait_ge(sem("o_sb"), s0 + s - 2)
                            pe_pv(pe, (g - 2) % 4, before if (g < 2 and r == 0) else batch)

            bodies(pe, L, emit)
            pe.wait_ge(sem("p_norm"), s0 + STEPS)
            pe.wait_ge(sem("pt_sb_act"), s0 + STEPS - 1)
            pe.wait_ge(sem("pt_sb_dve"), s0 + STEPS - 1)
            pe_probsT(pe, L, 3)
            for s in (STEPS - 2, STEPS - 1):
                if L.index == 1:
                    pe_stage(pe, *EARLY[s - (STEPS - 2)], 0)
                pe.wait_ge(sem("pt_sb_act"), s0 + s + 1)
                pe.wait_ge(sem("pt_sb_dve"), s0 + s + 1)
                pe.wait_ge(sem("o_sb"), s0 + s)
                pe_pv(pe, s % 4, L.bodies[-1][4])
            pe.wait_ge(sem("o_sb"), s0 + STEPS)
            pe.wait_ge(sem("y_done"), t0 + NT - 1)
            pe_out(pe, L, 1)

        def stats_of(dve, t, which, slot=None):
            into = stats[:, t, :] if slot is None else loop_stats[:, slot, :]
            dve.bn_stats(into, tile_of(x, t)).then_inc(sem(f"stats_{which}"), 1)

        def aggregate(dve, t, which, count, signal=True, slot=None):
            if count is not None:
                dve.wait_ge(sem(f"stats_{which}"), count)
            into = mean_var[:, t] if slot is None else moments[:, slot]
            a = dve.bn_aggr(into, stats[:, t, :] if slot is None else loop_stats[:, slot, :])
            if signal:
                a.then_inc(sem(f"var_{which}"), 1)

        def pool_rstd(pool, t, n, which, count, slot=None):
            at = slice(t, t + n) if isinstance(t, int) else bass.ds(t, n)
            source = mean_var[:, at] if slot is None else moments[:, slot:slot + 1]
            pool.wait_ge(sem(f"var_{which}"), count)
            pool.tensor_tensor(mean_var[:, at], source, zero_eps[:, :].unsqueeze(1).broadcast_to([P, n, 2]), ALU.add)\
                .then_inc(sem(f"shift_{which}"), 1)
            pool.wait_ge(sem(f"shift_{which}"), count)
            pool.tensor_tensor(rstd[:, at], mean_var[:, at, 1], minus_half[:, 0:n], ALU.pow)\
                .then_inc(sem(f"rstd_{which}"), 1)

        OUT = NT - 1

        def tile_of(buf, t):
            if isinstance(t, int):
                return buf[:, t, :]
            return buf[:, bass.ds(t, 1), :].rearrange("p a d -> p (a d)")

        def column_of(buf, t):
            return buf[:, t:t + 1] if isinstance(t, int) else buf[:, bass.ds(t, 1)]

        def dve_normalize(dve, t):
            dve.tensor_scalar(xn[:], tile_of(x, t), column_of(mean_var[:, :, 0], t), column_of(rstd, t),
                              ALU.subtract, ALU.mult).then_inc(sem("xn_ready"), 1)

        def mix(dve, t, r, c):
            if c == 0:
                dve.wait_ge(sem(f"gathered{r}"), 32 * (t // 2 + 1) if isinstance(t, int) else (t - r) * 16 + 32)
            else:
                dve.wait_ge(sem("mixed_first"), t + 1)
            w = weight[:, 2 + c, :]
            dve.scalar_tensor_tensor(tile_of(x, t), y_pair[:, r, c, :], column_of(w, t), tile_of(x, t),
                                     ALU.mult, ALU.add).then_inc(sem("mixed" if c else "mixed_first"), 1)

        def dve_attention(dve, L):
            t0, s0 = NT * L.index, STEPS * L.index
            if L.index == 0:
                dve.wait_ge(sem("x_first"), 16)
                for t in range(4):
                    stats_of(dve, t, "in")
                for t in range(4):
                    aggregate(dve, t, "in", 4, t == 3)
                dve.wait_ge(sem("kv_zero"), 1)
            else:
                dve.wait_ge(sem("kv_zero"), 2)
            dve_kv(dve, L, "k")

            def q_rest(t, r, half):
                dve.wait_ge(sem("q_high"), 2 * t + half + 1)
                part = slice(4 * half, 4 * half + 4)
                dve.tensor_tensor(q_low[:, r, part, :], misc_ps.rearrange("p (c n) -> p c n", c=4),
                                  q_high[:, r, part, :].bitcast(F32), ALU.subtract).then_inc(sem("q_sb"), 1)

            def mixed_pair(t):
                for n in (t, t + 1):
                    for c in range(TOP):
                        mix(dve, n, n % 2, c)
                for n in (t, t + 1):
                    dve.wait_ge(sem("mixed"), n + 1)
                    stats_of(dve, n, "in")
                for n in (t, t + 1):
                    aggregate(dve, n, "in", NT + t + 2, n == t + 1)

            if L.index == 1:
                dve.wait_ge(sem("kv_sb"), KV0 + NC)
                dve.memset(K1[:, :, KEYS + 1], 0.0)
                dve.tensor_scalar_mul(K1[:, :, KEYS], kmean[:, :], -1.0 / (3 * KEYS)).then_inc(sem("kmean_done"), 1)
                dve_kv(dve, L, "v", (0,))
                mixed_pair(0)
                dve_kv(dve, L, "v", (1,))
            dve.wait_ge(sem("rstd_in"), 1 if L.index == 0 else 3)
            dve_normalize(dve, 0)
            if L.index == 1:
                dve.wait_ge(sem("K_high"), 1)
                dve.tensor_tensor(K_low[:], K1[:], K_high[:].bitcast(F32), ALU.subtract).then_inc(sem("K_split"), 1)
            dve.wait_ge(sem("xt_ps"), t0 + 1)
            dve_normalize(dve, 1)
            if L.index == 1:
                q_rest(0, 0, 0)
                mixed_pair(2)
                q_rest(0, 0, 1)
            if L.index == 0:
                dve.wait_ge(sem("x_rest"), 16)
                for t in range(4, NT):
                    stats_of(dve, t, "in")
                for t in range(4, NT):
                    aggregate(dve, t, "in", NT, t == NT - 1)

            def row_max(g, s):
                dve.wait_ge(sem("s_ps"), s0 + s + 1)
                if L.index == 0:
                    dve.tensor_reduce(negmax[:, g % 2, :].rearrange("p (u i) -> p u i", u=2),
                                      scores[:, g % 2, :, 0:KEYS].rearrange("p u (i n) -> p u i n", i=2),
                                      AX.X, ALU.max, negate=True).then_inc(sem("bias_ready"), 1)
                    return
                m = scores[:, g % 2, :, KEYS]
                dve.tensor_reduce(negmax[:, g % 2, 0:2], scores[:, g % 2, :, 0:KEYS], AX.X, ALU.max,
                                  negate=True).then_inc(sem("negmax_done"), 1)
                dve.wait_ge(sem("negmax_done"), s + 1)
                dve.tensor_tensor(shifted[:, g % 2, 0:2], negmax[:, g % 2, 0:2], m,
                                  ALU.subtract).then_inc(sem("shifted_done"), 1)
                dve.wait_ge(sem("shifted_done"), s + 1)
                dve.tensor_tensor(bias1[:, g % 2, 0:2], shifted[:, g % 2, 0:2], m, ALU.add).then_inc(sem("bias_ready"), 1)

            def reciprocals(g, s):
                dve.wait_ge(sem("p_exp"), s0 + s + 1)
                dve.reciprocal(recip[:, g % 2, 0:L.hs], sums[:, g % 2, 0:L.hs]).then_inc(sem("recip_ready"), 1)

            row_max(0, 0)
            row_max(1, 1)
            if L.index == 0:
                dve_kv(dve, L, "v")
            reciprocals(0, 0)
            dve_kv(dve, L, "r")
            if L.index == 0:
                dve.wait_ge(sem("rstd_in"), 2)

            def evacuate_probsT(s, parity):
                dve.wait_ge(sem("pt_ps"), s0 + s + 1)
                dve.tensor_copy(probsT[:, parity, 0:512], probsT_ps[:, 0:512]).then_inc(sem("pt_sb_dve"), 1)

            def evacuate_o(s, g, r):
                high, low = oT_parts[L.index]
                dve.wait_ge(sem("o_high"), s0 + s + 1)
                part = slice(2 * g, 2 * g + 2)
                dve.tensor_tensor(low[:, r, part, :], o_ps[:, 0:2 * P].rearrange("p (u n) -> p u n", u=2),
                                  high[:, r, part, :].bitcast(F32), ALU.subtract).then_inc(sem("o_sb"), 1)

            def add_y(t, r):
                dve.wait_ge(sem("y_ps"), t0 + t + 1)
                dve.wait_ge(sem("xb_ready"), t0 + t + 1)
                dve.scalar_tensor_tensor(tile_of(x, t), misc_ps[:, 0:D], gates[:, L.index:L.index + 1],
                                         x_biased[:, r, :], ALU.mult, ALU.add).then_inc(sem("y_done"), 1)

            def emit(i, first, last, before, batch, after):
                for r in range(2):
                    t = 2 * i + r
                    t_first, t_last = first and r == 0, last and r == 1
                    for g in range(4):
                        s = 4 * t + g
                        mixing = L.index == 1 and (not isinstance(t, int) or t + 4 < NT)
                        if g == 0 and not first:
                            dve.wait_ge(sem("y_done"), t0 + t - 1)
                        if g == 2 and not first:
                            dve.wait_ge(sem("stats_out"), t0 + t - 1)
                        if g == 2 and mixing:
                            dve.wait_ge(sem("mixed"), t + 5)
                        if g == 3 and mixing:
                            dve.wait_ge(sem("stats_in"), NT + 1 + t + 4)
                        if not (t_first and g == 0):
                            reciprocals(g, s)
                        if L.index == 1 and g >= 2 and not t_last:
                            q_rest(t + 1, 1 - r, g - 2)
                        if L.index == 0 and t_first and g == 3:
                            dve.wait_ge(sem("Wo_split"), 2)
                        if not (t_first and g < 3):
                            evacuate_o(s - 3, (g - 3) % 4, r if g == 3 else 1 - r)
                        if not (t_last and g == 3) and not (t_first and g == 0):
                            row_max((g + 1) % 4, s + 1)
                        if not (t_first and g == 0):
                            evacuate_probsT(s - 1, (g - 1) % 2)
                        if g == 0 and not first:
                            stats_of(dve, t - 2, "out", slot=r)
                        if g == 0 and mixing:
                            mix(dve, t + 4, r, 0)
                        if g == 1 and not last:
                            dve.wait_ge(sem("xt_ps"), t0 + t + 2)
                            if L.index == 1:
                                dve.wait_ge(sem("rstd_in"), max(4, t + 3) if isinstance(t, int) else t + 3)
                            dve_normalize(dve, t + 2)
                        if g == 1 and mixing:
                            mix(dve, t + 4, r, 1)
                        if g == 2 and not first:
                            aggregate(dve, t - 2, "out", None, slot=r)
                        if g == 2 and mixing:
                            stats_of(dve, t + 4, "in", slot=2 + r)
                        if g == 3 and not t_first:
                            add_y(t - 1, 1 - r)
                        if L.index == 1 and isinstance(t, int) and t >= NT - 5 and g < 3:
                            early = 3 * (t - (NT - 5)) + g
                            if early <= t - 3:
                                dve.wait_ge(sem("rstd_out"), OUT + early + 1)
                                first_cur(dve, early)
                        if g == 3 and mixing:
                            aggregate(dve, t + 4, "in", None, slot=2 + r)

            bodies(dve, L, emit)
            evacuate_o(STEPS - 3, 1, 1)
            evacuate_probsT(STEPS - 1, 1)
            evacuate_o(STEPS - 2, 2, 1)
            evacuate_o(STEPS - 1, 3, 1)
            if L.index == 1:
                turned_rest(dve, 0, 0)
            add_y(NT - 1, 1)
            for t in (NT - 2, NT - 1):
                dve.wait_ge(sem("y_done"), t0 + t + 1)
                stats_of(dve, t, "out")
            for t in (NT - 2, NT - 1):
                aggregate(dve, t, "out", t0 + t + 1, t == NT - 1)

        def act_attention(act, L):
            t0, s0 = NT * L.index, STEPS * L.index

            def evacuate_xT(t, r):
                act.wait_ge(sem("xt_ps"), t0 + t + 1)
                act.copy(xT[:, r], misc_ps[:, 0:D].rearrange("p (k n) -> p k n", k=DK)).then_inc(sem("xt_sb"), 1)

            def evacuate_probsT(s, parity):
                act.wait_ge(sem("pt_ps"), s0 + s + 1)
                act.copy(probsT[:, parity, 512:640], probsT_ps[:, 512:640]).then_inc(sem("pt_sb_act"), 1)

            def evacuate_q(t, r, half):
                act.wait_ge(sem("q_ps"), 2 * (t0 + t) + half + 1)
                into = q if L.index == 0 else q_high
                act.copy(into[:, r, 4 * half:4 * half + 4, :],
                         misc_ps.rearrange("p (c n) -> p c n", c=4)).then_inc(sem("q_sb" if L.index == 0 else "q_high"), 1)

            def evacuate_o(s, g, r):
                act.wait_ge(sem("o_ps"), s0 + s + 1)
                act.copy(oT_parts[L.index][0][:, r, 2 * g:2 * g + 2, :],
                         o_ps[:, 0:2 * P].rearrange("p (u n) -> p u n", u=2)).then_inc(sem("o_high"), 1)

            def exponentials(g, s):
                act.wait_ge(sem("bias_ready"), s0 + s + 1)
                bias = negmax if L.index == 0 else bias1
                pr = probs[:, g % 2, :].rearrange("p (j n) -> p j n", j=L.hs)
                for j in range(L.hs):
                    u, i = (j // 2, j % 2) if L.index == 0 else (j, 0)
                    e = act.activation(pr[:, j, 0:L.keys], scores[:, g % 2, u, i * L.keys:(i + 1) * L.keys], ACT.Exp,
                                       bias=bias[:, g % 2, j:j + 1], accum_out=sums[:, g % 2, j:j + 1])
                e.then_inc(sem("p_exp"), 1)

            if L.index == 1:
                act.wait_ge(sem("kmean_done"), 1)
                act.copy(K_high[:], K1[:]).then_inc(sem("K_high"), 1)
                act.wait_ge(sem("wo_in"), 32)
                act.copy(Wo_high[:], Wo[:]).then_inc(sem("Wo_high"), 1)
            evacuate_xT(0, 0)
            evacuate_q(0, 0, 0)
            evacuate_q(0, 0, 1)
            act.wait_ge(sem("pads_zero"), 1 + L.index)
            exponentials(0, 0)
            exponentials(1, 1)
            if L.index == 0:
                act.wait_ge(sem("kv_ps"), NC)
                act.wait_ge(sem("wo_in"), 16)
                act.copy(Wo0_high[:], Wo[:]).then_inc(sem("Wo_high"), 1)

            def emit(i, first, last, before, batch, after):
                for r in range(2):
                    t = 2 * i + r
                    t_first, t_last = first and r == 0, last and r == 1
                    for g in range(4):
                        s = 4 * t + g
                        if not (t_last and g == 3) and not (t_first and g == 0):
                            act.wait_ge(sem("p_norm"), s0 + s)
                            exponentials((g + 1) % 4, s + 1)
                        if not (t_first and g == 0):
                            evacuate_probsT(s - 1, (g - 1) % 2)
                        if not t_last:
                            if g == 0:
                                evacuate_xT(t + 1, 1 - r)
                            if g == 1:
                                evacuate_q(t + 1, 1 - r, 0)
                            if g == 2:
                                evacuate_q(t + 1, 1 - r, 1)
                        if not (t_first and g < 2):
                            evacuate_o(s - 2, (g - 2) % 4, r if g >= 2 else 1 - r)

            bodies(act, L, emit)
            if L.index == 1:
                act.activation(table[:, 2:3], zero_eps[:, 0:1], ACT.Gelu)
            evacuate_probsT(STEPS - 1, 1)
            for n in range(2):
                if L.index == 1:
                    act_stage(act, *EARLY[n], 0)
                evacuate_o(STEPS - 2 + n, 2 + n, 1)

        def slots_now(pool, t, r, reused):
            if isinstance(t, int):
                now = slot[:, :, t]
            else:
                now = slot[:, :, bass.ds(t, 1)].rearrange("p c a -> p (c a)")
            if reused is not None:
                pool.wait_ge(sem("mixed"), reused if not isinstance(reused, int) else t - 1)
            pool.tensor_copy(slot_now[:, r, :], now).then_inc(sem("slot_now_ready"), 1)

        def gather(pool, t, r):
            for c in range(TOP):
                pool.indirect_dma_start(out=y_pair[:, r, c, :], out_offset=None, in_=y_slots,
                                        in_offset=bass.IndirectOffsetOnAxis(ap=slot_now[:, r, c:c + 1], axis=0))\
                    .then_inc(sem(f"gathered{r}"), 16)

        def pool_attention(pool, L):
            t0, s0 = NT * L.index, STEPS * L.index

            def emit(i, first, last, before, batch, after):
                for r in range(2):
                    t = 2 * i + r
                    for g in range(4):
                        s = 4 * t + g
                        pool.wait_ge(sem("recip_ready"), s0 + s + 1)
                        gathering = L.index == 1 and (not isinstance(t, int) or t + 5 < NT)
                        if g == 1 and gathering:
                            pool.wait_ge(sem("slot_now_ready"), t + 6)
                        if not (first and r == 0 and g < 2):
                            pool.wait_ge(sem("pt_ps"), s0 + s - 1)
                        pr = probs[:, g % 2, :].rearrange("p (j n) -> p j n", j=L.hs)
                        whole = normed[:, g % 2, 0:512].rearrange("p (j n) -> p j n", j=L.hs)
                        rest = normed[:, g % 2, 512:640].rearrange("p (j n) -> p j n", j=L.hs)
                        rc = recip[:, g % 2, 0:L.hs].unsqueeze(2)
                        split = L.chunks * P
                        pool.tensor_tensor(whole, pr[:, :, 0:split], rc.broadcast_to([P, L.hs, split]), ALU.mult)
                        pool.tensor_tensor(rest, pr[:, :, split:L.width], rc.broadcast_to([P, L.hs, L.rw]),
                                           ALU.mult).then_inc(sem("p_norm"), 1)
                        if first and r == 0 and g // 2 == L.index:
                            high, low = Wo_parts[L.index]
                            pool.wait_ge(sem("Wo_high"), L.index + 1)
                            pool.wait_ge(sem("kv_ps"), KV0)
                            part = slice(g % 2 * NC // 2, (g % 2 + 1) * NC // 2)
                            pool.tensor_tensor(low[:, part], Wo[:, part], high[:, part].bitcast(F32),
                                               ALU.subtract).then_inc(sem("Wo_split"), 1)
                        if L.index == 1 and g == 0 and (not isinstance(t, int) or 1 <= t <= NT - 4):
                            pool_rstd(pool, t + 3, 1, "in", t + 4, slot=3 - r)
                        if g == 0 and gathering:
                            slots_now(pool, t + 5, 1 - r, t + 4)
                        if g == 1 and gathering:
                            gather(pool, t + 5, 1 - r)
                        if g == 3 and not first:
                            pool_rstd(pool, t - 2, 1, "out", OUT * L.index + t - 1, slot=r)
                        if g == 2:
                            pool.wait_ge(sem("xn_ready"), t0 + t + 1)
                            if not first:
                                pool.wait_ge(sem("y_done"), t0 + t - 1)
                            pool.tensor_tensor(x_biased[:, r, :], tile_of(x, t), gated_bo[:],
                                               ALU.add).then_inc(sem("xb_ready"), 1)

            if L.index == 0:
                pool.wait_ge(sem("eps_ready"), 1)
                pool_rstd(pool, 0, 4, "in", 1)
                pool.wait_ge(sem("gates_ready"), 1)
                pool.wait_ge(sem("bo_in"), 16)
                pool.tensor_tensor(gated_bo[:], gated_bo[:], gates[:, 0:1].broadcast_to([P, D]), ALU.mult)\
                    .then_inc(sem("gbo_ready"), 1)
                pool_rstd(pool, 4, NT - 4, "in", 2)
                pool.wait_ge(sem("gbo_ready"), 1)
            else:
                pool.wait_ge(sem("bo_in"), 32)
                pool.tensor_tensor(gated_bo[:], gated_bo[:], gates[:, 1:2].broadcast_to([P, D]), ALU.mult)\
                    .then_inc(sem("gbo_ready"), 1)
                pool_rstd(pool, 2, 2, "in", 4)
                pool.wait_ge(sem("gbo_ready"), 2)
            bodies(pool, L, emit)
            if L.index == 1:
                pool.wait_ge(sem("coupling_in"), 16 * LOADS)
                pool.tensor_copy(cw1_high[:], cw1).then_inc(sem("cw1_high"), 1)
                pool.wait_ge(sem("cw1_high"), 1)
                pool.tensor_tensor(cw1_low[:], cw1, cw1_high[:].bitcast(F32), ALU.subtract).then_inc(sem("cw1_split"), 1)
            pool_rstd(pool, NT - 2, 2, "out", OUT * (L.index + 1))

        def pe_routing(pe):
            pe.wait_ge(sem("wr_in"), 32)
            pe.wait_ge(sem("y_done"), NT)
            for n in range(NT + 3):
                if n < NT:
                    pe.wait_ge(sem("xe_ready"), n + 1)
                    if n >= 4:
                        pe.wait_ge(sem("xet_sb"), n - 3)
                    for k in range(DK):
                        mm = pe.transpose(banks[:, n % 4, k * P:(k + 1) * P], xn_all[:, n, k * P:(k + 1) * P], ident[:])
                    mm.then_inc(sem("xet_ps"), 1)
                if n >= 3:
                    t = n - 3
                    pe.wait_ge(sem("xet_sb"), t + 1)
                    for k in range(DK):
                        mm = pe.matmul(banks[:, 4 + t // 4, t * E:(t + 1) * E], xeT[:, t % 4, k, :], Wr[:, k, :],
                                       start=(k == 0), stop=(k == DK - 1), skip_group_check=True)
                    mm.then_inc(sem("logit_ps"), 1)
            pe.wait_ge(sem("either_ready"), NT // 4)
            pe.wait_ge(sem("before_ready"), 1)
            pe.matmul(banks[:, 4, 0:NT * E], before[:], either.rearrange("p t e -> p (t e)"), start=True, stop=True)
            pe.matmul(banks[:, 5, 0:NT * E], ones[:], either.rearrange("p t e -> p (t e)"), start=True, stop=True)\
                .then_inc(sem("rank_ps"), 1)
            for n in range(TOP * NT):
                if n % 8 == 0:
                    pe.wait_ge(sem("numbered_ready"), n // NT + 1)
                    pe.wait_ge(sem("in_row_ready"), n // 8 + 1)
                mm = pe.matmul(banks[:, 6, 0:SLOTS], in_row[:, n, :], numbered[:, n, :], start=(n == 0),
                               stop=(n == TOP * NT - 1))
            mm.then_inc(sem("token_ps"), 1)

        def pool_routing(pool):
            pool.wait_ge(sem("in_tile_ready"), 1)
            for c in range(TOP):
                n = slice(c * NT, (c + 1) * NT)
                pool.tensor_tensor(numbered[:, n], in_tile[:, n], token_id.unsqueeze(2).broadcast_to([P, NT, SLOTS]),
                                   ALU.mult).then_inc(sem("numbered_ready"), 1)

        def dve_routing(dve):
            steps = [0]

            def link(ins):
                steps[0] += 1
                ins.then_inc(sem("route_step"), 1)
                dve.wait_ge(sem("route_step"), steps[0])

            dve.tensor_copy(iota_row16, iota_row).then_inc(sem("iota16_ready"), 1)
            dve.wait_ge(sem("rstd_out"), OUT)
            for t in range(NT):
                dve.tensor_scalar(xn_all[:, t, :], x[:, t, :], mean_var[:, t, 0:1], rstd[:, t:t + 1],
                                  ALU.subtract, ALU.mult).then_inc(sem("xe_ready"), 1)
            for t0 in range(0, NT, 4):
                at = slice(t0, t0 + 4)
                dve.wait_ge(sem("logit_ps"), t0 + 4)
                link(dve.tensor_tensor(logits[:, at], banks[:, 4 + t0 // 4, t0 * E:(t0 + 4) * E].rearrange("p (t e) -> p t e", t=4),
                                       br[:, :].unsqueeze(1).broadcast_to([P, 4, E]), ALU.add))
                for t in range(t0, t0 + 4):
                    last = dve.max(top[:, t, :], logits[:, t, :])
                link(last)
                for t in range(t0, t0 + 4):
                    last = dve.max_index(top_at[:, t, :], top[:, t, :], logits[:, t, :])
                link(last)
                link(dve.tensor_copy(top_atf[:, at], top_at[:, at, 0:TOP]))
                for c in range(TOP):
                    last = dve.tensor_tensor(chosen[:, c, at], iota_e[:].unsqueeze(1).broadcast_to([P, 4, E]),
                                             top_atf[:, at, c].unsqueeze(2).broadcast_to([P, 4, E]), ALU.is_equal)
                link(last)
                dve.tensor_tensor(either[:, at], chosen[:, 0, at], chosen[:, 1, at], ALU.add)\
                    .then_inc(sem("either_ready"), 1)
            dve.tensor_tensor(weight[:, 0, :], top[:, :, 1], top[:, :, 0], ALU.subtract).then_inc(sem("margin_ready"), 1)
            dve.wait_ge(sem("rank_ps"), 1)
            link(dve.tensor_copy(totals[:], banks[:, 5, 0:NT * E].rearrange("p (t e) -> p t e", t=NT)))
            for e in range(E):
                last = dve.tensor_tensor_scan(upto[:, :, e], ones[:, 0:NT], totals[:, :, e], 0.0, ALU.mult, ALU.add)
            link(last)
            link(dve.tensor_tensor(tiles_cmp[:], upto[:, NT - 1, :].unsqueeze(2).broadcast_to([P, E, NT]),
                                   iota_t[:].unsqueeze(1).broadcast_to([P, E, NT]), ALU.is_gt))
            link(dve.tensor_reduce(tiles_of[:], tiles_cmp[:], AX.X, ALU.add))
            link(dve.tensor_tensor_scan(tiles_end[:], ones[:, 0:E], tiles_of[:], 0.0, ALU.mult, ALU.add))
            link(dve.tensor_tensor(owner_cmp, iota_s[0:1, :].unsqueeze(2).broadcast_to([1, SLOTS, E]),
                                   tiles_end[0:1, :].unsqueeze(1).broadcast_to([1, SLOTS, E]), ALU.is_ge))
            link(dve.tensor_reduce(owner_f[:], owner_cmp, AX.X, ALU.add))
            dve.tensor_scalar(owner[:], owner_f[:], float(E - 1), None, ALU.min).then_inc(sem("owner_ready"), 1)
            link(dve.tensor_tensor(tiles_base[:], tiles_end[:], tiles_of[:], ALU.subtract))
            link(dve.tensor_tensor(place_i[:], upto[:], totals[:], ALU.subtract))
            link(dve.tensor_tensor(place[:], place_i[:], banks[:, 4, 0:NT * E].rearrange("p (t e) -> p t e", t=NT), ALU.add))
            link(dve.scalar_tensor_tensor(place_i[:], tiles_base[:].unsqueeze(1).broadcast_to([P, NT, E]), float(P),
                                          place[:], ALU.mult, ALU.add))
            for c in range(TOP):
                link(dve.tensor_tensor(place[:], chosen[:, c], place_i[:], ALU.mult))
                link(dve.tensor_reduce(slot_f[:, c, :], place[:], AX.X, ALU.add))
            link(dve.tensor_copy(slot[:], slot_f[:]))
            link(dve.tensor_scalar(slot_low[:], slot[:], P - 1, None, ALU.bitwise_and))
            dve.tensor_copy(slot_part[:, 0], slot_low[:]).then_inc(sem("row_ready"), 1)
            dve.wait_ge(sem("row_ready"), 1)
            link(dve.tensor_tensor(slot_part[:, 1], slot_f[:], slot_part[:, 0], ALU.subtract))
            dve.tensor_tensor(in_tile, slot_start.unsqueeze(1).broadcast_to([P, TOP * NT, SLOTS]),
                              start_of.unsqueeze(2).broadcast_to([P, TOP * NT, SLOTS]), ALU.is_equal)\
                .then_inc(sem("in_tile_ready"), 1)
            dve.wait_ge(sem("iota16_ready"), 1)
            for n in range(TOP * NT):
                rows = dve.tensor_scalar(in_row[:, n], iota_row16, row_of[:, n:n + 1], None, ALU.is_equal)
                if n % 8 == 7:
                    rows.then_inc(sem("in_row_ready"), 1)
            dve.wait_ge(sem("token_ps"), 1)
            dve.tensor_copy(token_of[:], banks[:, 6, 0:SLOTS]).then_inc(sem("token_ready"), 1)
            dve.wait_ge(sem("margin_exp"), 1)
            link(dve.tensor_scalar_add(weight[:, 2, :], weight[:, 1, :], 1.0))
            link(dve.reciprocal(weight[:, 0, :], weight[:, 2, :]))
            link(dve.tensor_scalar_mul(weight[:, 2, :], weight[:, 0, :], gates[:, 2:3]))
            dve.tensor_tensor(weight[:, 3, :], weight[:, 1, :], weight[:, 2, :], ALU.mult).then_inc(sem("weight_ready"), 1)

        def act_routing(act):
            for t in range(NT):
                act.wait_ge(sem("xet_ps"), t + 1)
                if t >= 4:
                    act.wait_ge(sem("logit_ps"), t - 3)
                act.copy(xeT[:, t % 4], banks[:, t % 4, 0:D].rearrange("p (k n) -> p k n", k=DK)).then_inc(sem("xet_sb"), 1)
            act.wait_ge(sem("margin_ready"), 1)
            act.activation(weight[:, 1, :], weight[:, 0, :], ACT.Exp).then_inc(sem("margin_exp"), 1)
            act.activation(table[:, 0:1], zero_eps[:, 0:1], ACT.Silu)

        def slot_bodies(eng, emit):
            emit(0)
            with eng.Fori(1, SLOTS // 2 - 1) as i:
                emit(i)
            emit(SLOTS // 2 - 1)
            emit(SLOTS // 2)

        def is_tile(j):
            return not isinstance(j, int) or j < SLOTS

        def body_tiles(i):
            return [(2 * i + r, r) for r in range(2) if is_tile(2 * i + r)]

        def owner_of(eng, j):
            return eng.value_load(owner[0:1, j:j + 1] if isinstance(j, int) else owner[0:1, bass.ds(j, 1)],
                                  min_val=0, max_val=E - 1)

        def sp_experts(sp):
            ys = y_slots.rearrange("(j p) d -> p j d", p=P)
            sp.wait_ge(sem("xn_stored"), 16)

            def emit(i):
                first = isinstance(i, int) and i == 0
                for j, r in body_tiles(i):
                    sp.wait_ge(sem("ey_sb"), j + 1)
                    sp.dma_start(tile_of(ys, j), y_slot[:, r]).then_inc(sem(f"ey_out{r}"), 16)
                    if first and r == 0:
                        load_keys_values(sp, 1)

            slot_bodies(sp, emit)

        def pe_experts(pe):
            pe.wait_ge(sem("w1_in"), 16)
            pe.wait_ge(sem("owner_ready"), 1)
            pe.wait_ge(sem("token_ready"), 1)

            def turn_x(j, i, r):
                pe.wait_ge(sem(f"xg_in{r}"), 16 * (i + 1))
                for k in range(DK):
                    mm = pe.transpose(misc_ps[:, k * P:(k + 1) * P], xg[:, r, k * P:(k + 1) * P], ident[:])
                mm.then_inc(sem("xgt_ps"), 1)

            def hidden(e, r, part):
                for k in range(DK):
                    w = W1[:, bass.ds(e, 1), k, part * H:(part + 1) * H].rearrange("p a n -> p (a n)")
                    mm = pe.matmul(banks[:, 2 * r + part, :], xgT[:, r, k, :], w, start=(k == 0), stop=(k == DK - 1))
                mm.then_inc(sem("hg_ps" if part else "ha_ps"), 1)

            turn_x(0, 0, 0)
            e = owner_of(pe, 0)
            pe.wait_ge(sem("xgt_sb"), 1)
            hidden(e, 0, 0)
            turn_x(1, 0, 1)
            hidden(e, 0, 1)
            pe.wait_ge(sem("w2_in"), 16)

            def emit(i):
                first = isinstance(i, int) and i == 0
                for j, r in body_tiles(i):
                    final = not is_tile(j + 1)
                    if not final:
                        e_next = owner_of(pe, j + 1)
                        pe.wait_ge(sem("xgt_sb"), j + 2)
                        if not (first and r == 0):
                            pe.wait_ge(sem("a_read"), j)
                        hidden(e_next, 1 - r, 0)
                    pe.wait_ge(sem("act_ready"), j + 1)
                    if not first:
                        pe.wait_ge(sem("at_sb"), j - 1)
                    for k in range(HK):
                        mm = pe.transpose(banks[:, 4 + r, k * P:(k + 1) * P], a_act[:, r, k * P:(k + 1) * P], ident[:])
                    mm.then_inc(sem("at_ps"), 1)
                    if not final:
                        if not (first and r == 0):
                            pe.wait_ge(sem("g_read"), j)
                        hidden(e_next, 1 - r, 1)
                    if is_tile(j + 2):
                        turn_x(j + 2, i + 1, r)
                    e = owner_of(pe, j)
                    pe.wait_ge(sem("at_sb"), j + 1)
                    if not (first and r == 0):
                        pe.wait_ge(sem("ey_sb"), j)
                    for k in range(HK):
                        w = W2[:, bass.ds(e, 1), k, :].rearrange("p a n -> p (a n)")
                        mm = pe.matmul(o_ps[:, 0:D], actT[:, r, k, :], w, start=(k == 0), stop=(k == HK - 1))
                    mm.then_inc(sem("ey_ps"), 1)

            slot_bodies(pe, emit)

        def act_experts(act):
            def evacuate_x(j, r):
                act.wait_ge(sem("xgt_ps"), j + 1)
                act.copy(xgT[:, r], misc_ps[:, 0:D].rearrange("p (k n) -> p k n", k=DK)).then_inc(sem("xgt_sb"), 1)

            def silu(j, r):
                act.wait_ge(sem("a_read"), j + 1)
                act.activation(a_act[:, r, :], a_act[:, r, :], ACT.Silu).then_inc(sem("silu_done"), 1)

            evacuate_x(0, 0)
            evacuate_x(1, 1)
            silu(0, 0)

            def emit(i):
                first = isinstance(i, int) and i == 0
                for j, r in body_tiles(i):
                    act.wait_ge(sem("at_ps"), j + 1)
                    if not first:
                        act.wait_ge(sem("ey_ps"), j - 1)
                    act.copy(actT[:, r], banks[:, 4 + r, :].rearrange("p (k n) -> p k n", k=HK)).then_inc(sem("at_sb"), 1)
                    if is_tile(j + 1):
                        silu(j + 1, 1 - r)
                    if is_tile(j + 2):
                        evacuate_x(j + 2, r)

            slot_bodies(act, emit)
            act.activation(table[:, 1:2], zero_eps[:, 0:1], ACT.Exp)

        def dve_experts(dve):
            dve.wait_ge(sem("owner_ready"), 1)
            dve.wait_ge(sem("b12_in"), 32)

            def inputs(j, r, wait_free):
                e = owner_of(dve, j)
                for part, buf, ps, read in ((0, a_act, "ha_ps", "a_read"), (1, g_act, "hg_ps", "g_read")):
                    dve.wait_ge(sem(ps), j + 1)
                    if wait_free:
                        if part == 0:
                            dve.wait_ge(sem("at_ps"), j - 1)
                        else:
                            dve.wait_ge(sem("act_ready"), j - 1)
                    dve.tensor_tensor(buf[:, r, :], banks[:, 2 * r + part, :],
                                      b1[:, bass.ds(e, 1), part * H:(part + 1) * H].rearrange("p a n -> p (a n)"),
                                      ALU.add).then_inc(sem(read), 1)

            inputs(0, 0, False)

            def emit(i):
                first = isinstance(i, int) and i == 0
                for j, r in body_tiles(i):
                    if is_tile(j + 1):
                        inputs(j + 1, 1 - r, not (first and r == 0))
                    e = owner_of(dve, j)
                    dve.wait_ge(sem("ey_ps"), j + 1)
                    if not first:
                        dve.wait_ge(sem(f"ey_out{r}"), 16 * i)
                    dve.tensor_tensor(y_slot[:, r], o_ps[:, 0:D], b2[:, bass.ds(e, 1), :].rearrange("p a n -> p (a n)"),
                                      ALU.add).then_inc(sem("ey_sb"), 1)

            slot_bodies(dve, emit)

        def pool_experts(pool):
            def tokens_now(j, r):
                pool.tensor_copy(token_now[:, r:r + 1], column_of(token_of, j)).then_inc(sem("token_now_ready"), 1)

            def gather_x(r):
                pool.indirect_dma_start(out=xg[:, r, :], out_offset=None, in_=xn_rows,
                                        in_offset=bass.IndirectOffsetOnAxis(ap=token_now[:, r:r + 1], axis=0))\
                    .then_inc(sem(f"xg_in{r}"), 16)

            pool.wait_ge(sem("token_ready"), 1)
            for j in range(2):
                tokens_now(j, j)
            pool.wait_ge(sem("xn_stored"), 16)
            for j in range(2):
                pool.wait_ge(sem("token_now_ready"), j + 1)
                gather_x(j)
            pool.wait_ge(sem("xg_in0"), 16)
            tokens_now(2, 0)

            def emit(i):
                first = isinstance(i, int) and i == 0
                for j, r in body_tiles(i):
                    if is_tile(j + 2):
                        pool.wait_ge(sem("xgt_ps"), j + 1)
                        pool.wait_ge(sem("token_now_ready"), j + 3)
                    pool.wait_ge(sem("silu_done"), j + 1)
                    pool.wait_ge(sem("g_read"), j + 1)
                    pool.tensor_tensor(a_act[:, r, :], a_act[:, r, :], g_act[:, r, :], ALU.mult).then_inc(sem("act_ready"), 1)
                    if is_tile(j + 2):
                        gather_x(r)
                    if is_tile(j + 3):
                        pool.wait_ge(sem(f"xg_in{1 - r}"), 16 * (i + 1 + r))
                        tokens_now(j + 3, 1 - r)

            slot_bodies(pool, emit)

        def load_coupling(eng):
            n = "L1_ffn_"
            def ld(dst, src):
                eng.dma_start(dst, src).then_inc(sem("coupling_in"), 16)
            ld(cw1, t_in[n + "cn_w1"].rearrange("(k p) n -> p k n", p=P))
            ld(cw2, t_in[n + "cn_w2"].rearrange("(k p) n -> p k n", p=P))
            ld(cw3, t_in[n + "cn_w3"])
            ld(cw4, t_in[n + "cn_w4"])
            ld(gw1, t_in[n + "gc_w1"].rearrange("(k p) n -> p k n", p=P))
            ld(gw2, t_in[n + "gc_w2"])
            ld(gw3, t_in[n + "gc_w3"])
            for m in range(2):
                ld(cb1[:, m:m + 1], t_in[n + "cn_b1"][m * P:(m + 1) * P].unsqueeze(1))
            for dst, src in ((cb2, "cn_b2"), (cb3, "cn_b3"), (gb1, "gc_b1"), (gb2, "gc_b2")):
                ld(dst, t_in[n + src].unsqueeze(1))
            for dst, src in ((cb4, "cn_b4"), (gb3, "gc_b3"), (reach, "adaptive_range")):
                ld(dst, t_in[n + src].partition_broadcast(P))

        LOADS = 16

        ORDER = [("turn", 0), ("turn", 1), ("l1", 0), ("turn", 2), ("l1", 1), ("turn", 3), ("l2", 0), ("l1", 2),
                 ("l2", 1), ("l3", 0), ("l1", 3), ("l2", 2), ("l3", 1), ("l4", 0), ("l2", 3), ("l3", 2), ("l4", 1),
                 ("l3", 3), ("l4", 2), ("l4", 3)]

        EARLY = [("turn", 0), ("turn", 1)]
        FIRST_ORDER = [("turn", 2), ("l1", 0), ("turn", 3), ("l1", 1)] + \
            [stage for stage in ORDER if stage[0] != "turn" and stage not in (("l1", 0), ("l1", 1))]

        def cycles(eng, emit):
            emit(0)
            with eng.Fori(1, CYCLES - 1) as c:
                emit(c)
            emit(CYCLES - 1)

        def is_first(c):
            return isinstance(c, int) and c == 0

        def is_last(c):
            return isinstance(c, int) and c == CYCLES - 1

        def pe_stage(pe, kind, j, c):
            if kind == "turn":
                if is_first(c):
                    pe.wait_ge(sem("cur_first"), 4 * j + 4)
                else:
                    pe.wait_ge(sem("cur_ready"), NB * (c - 1) + j + 1)
                for k in range(DK):
                    for t in range(4):
                        mm = pe.transpose(banks[:, 2 * j + k, t * P:(t + 1) * P],
                                          cur[:, 4 * j + t, k * P:(k + 1) * P], ident[:])
                mm.then_inc(sem("turn_ps"), 1)
            elif kind == "l1":
                pe.wait_ge(sem("turn_sb"), NB * c + j + 1)
                for m in range(2):
                    for k in range(DK):
                        cols = slice(m * P, (m + 1) * P)
                        mm = pe_split(pe, banks[:, 2 * j + m, :], (cw1_high[:, k, cols], cw1_low[:, k, cols]),
                                      (curT_high[:, j, k, :], curT_low[:, j, k, :]), k == 0, k == DK - 1)
                mm.then_inc(sem("l1_ps"), 1)
            elif kind == "l2":
                pe.wait_ge(sem("l1_sb"), NB * c + j + 1)
                for k in range(2):
                    mm = pe.matmul(banks[:, 2 * j, :], cw2[:, k, :], h1T[:, j, k, :], start=(k == 0), stop=(k == 1))
                mm.then_inc(sem("l2_ps"), 1)
            elif kind == "l3":
                pe.wait_ge(sem("l2_sb"), NB * c + j + 1)
                pe.matmul(banks[0:64, 2 * j + 1, :], cw3, h2T[:, j, :], start=True, stop=True).then_inc(sem("l3_ps"), 1)
            else:
                pe.wait_ge(sem("l3_sb"), NB * c + j + 1)
                for t in range(4):
                    mm = pe.matmul(banks[:, 2 * j, t:t + 1], h3T[0:64, j, t * P:(t + 1) * P], cw4, start=True, stop=True)
                mm.then_inc(sem("l4_ps"), 1)

        def pe_coupling(pe):
            def global_layer(n):
                o = banks[:, 2 * NB - 1, 2 * n:2 * n + 2]
                if n == 0:
                    pe.wait_ge(sem("mean_sb"), 1)
                    for k in range(DK):
                        mm = pe.matmul(o, gw1[:, k, :], mean_sb[:, k, :], start=(k == 0), stop=(k == DK - 1))
                elif n == 1:
                    pe.wait_ge(sem("g_sb"), 1)
                    mm = pe.matmul(o[0:64], gw2, g1, start=True, stop=True)
                else:
                    pe.wait_ge(sem("g_sb"), 2)
                    pe.wait_ge(sem("gw3_wide_ready"), 1)
                    mm = pe.matmul(o, gw3_wide, g2, start=True, stop=True)
                mm.then_inc(sem("g_ps"), 1)

            pe.wait_ge(sem("coupling_in"), 16 * LOADS)
            pe.wait_ge(sem("cw1_split"), 1)

            def emit(c):
                for kind, j in (FIRST_ORDER if is_first(c) else ORDER):
                    if is_first(c) and (kind, j) in AFTER:
                        global_layer(AFTER.index((kind, j)))
                    if is_first(c) and (kind, j) == ("l1", NB - 1):
                        pe.wait_ge(sem("g_sb"), 3)
                    pe_stage(pe, kind, j, c)

            cycles(pe, emit)

        AFTER = [("l2", 1), ("l3", 0), ("l1", 3)]

        def act_stage(act, kind, j, c):
            if kind == "turn":
                act.wait_ge(sem("turn_ps"), NB * c + j + 1)
                act.copy(curT_high[:, j], banks[:, 2 * j:2 * j + 2, :]).then_inc(sem("turn_high"), 1)
            elif kind == "l1":
                act.wait_ge(sem("l1_ps"), NB * c + j + 1)
                for m in range(2):
                    a = act.activation(h1T[:, j, m, :], banks[:, 2 * j + m, :], ACT.Gelu, bias=cb1[:, m:m + 1])
                a.then_inc(sem("l1_sb"), 1)
            elif kind == "l2":
                act.wait_ge(sem("l2_ps"), NB * c + j + 1)
                act.activation(h2T[:, j, :], banks[:, 2 * j, :], ACT.Gelu, bias=cb2).then_inc(sem("l2_sb"), 1)
            elif kind == "l3":
                act.wait_ge(sem("l3_ps"), NB * c + j + 1)
                act.activation(h3T[0:64, j, :], banks[0:64, 2 * j + 1, :], ACT.Gelu, bias=cb3).then_inc(sem("l3_sb"), 1)
            else:
                act.wait_ge(sem("l4_ps"), NB * c + j + 1)
                act.activation(tf[:, 4 * j:4 * j + 4], banks[:, 2 * j, 0:4], ACT.Tanh, bias=half_b4,
                               scale=0.5).then_inc(sem("tf_ready"), 1)

        def act_coupling(act):
            act.wait_ge(sem("coupling_in"), 16 * LOADS)
            act.wait_ge(sem("halves_ready"), 1)

            def global_layer(n):
                dst, rows, bias = ((g1, P, gb1), (g2, 64, gb2), (g3, P, half_gb3))[n]
                src = banks[0:rows, 2 * NB - 1, 2 * n:2 * n + 2]
                act.wait_ge(sem("g_ps"), n + 1)
                if n < 2:
                    act.activation(dst, src, ACT.Gelu, bias=bias).then_inc(sem("g_sb"), 1)
                else:
                    act.activation(dst, src, ACT.Tanh, bias=bias, scale=0.5).then_inc(sem("g_sb"), 1)

            def emit(c):
                for kind, j in (FIRST_ORDER if is_first(c) else ORDER):
                    if is_first(c) and (kind, j) in AFTER:
                        global_layer(AFTER.index((kind, j)))
                    act_stage(act, kind, j, c)

            cycles(act, emit)

        def first_cur(dve, t):
            dve.tensor_scalar(tile_of(cur, t), tile_of(x, t), column_of(mean_var[:, :, 0], t), column_of(rstd, t),
                              ALU.subtract, ALU.mult).then_inc(sem("cur_first"), 1)

        def turned_rest(dve, j, c):
            turned = banks[:, 2 * j:2 * j + 2, :]
            dve.wait_ge(sem("turn_high"), NB * c + j + 1)
            if is_first(c):
                dve.tensor_reduce(block_sum[:, :, j], turned, AX.X, ALU.add)
            dve.tensor_tensor(curT_low[:, j], turned, curT_high[:, j].bitcast(F32), ALU.subtract)\
                .then_inc(sem("turn_sb"), 1)

        def dve_coupling(dve):
            dve.wait_ge(sem("rstd_out"), 2 * OUT)
            for t in (NT - 3, NT - 2, NT - 1):
                first_cur(dve, t)
            turned_rest(dve, 1, 0)
            dve.wait_ge(sem("coupling_in"), 16 * LOADS)
            dve.tensor_scalar_mul(half_b4, cb4, 0.5)
            dve.tensor_scalar_mul(half_gb3, gb3, 0.5).then_inc(sem("halves_ready"), 1)
            dve.tensor_scalar_mul(slope[:, 0:1], reach, 0.3)
            dve.tensor_scalar_mul(slope[:, 1:2], reach, -0.3)
            dve.tensor_copy(gw3_wide, gw3.broadcast_to([64, P])).then_inc(sem("gw3_wide_ready"), 1)
            turned_rest(dve, 2, 0)
            turned_rest(dve, 3, 0)
            dve.wait_ge(sem("turn_sb"), NB)
            sums_of = block_sum.rearrange("p k (b j) -> p k b j", b=B)
            dve.tensor_reduce(mean_sum, sums_of, AX.X, ALU.add).then_inc(sem("level_step"), 1)
            dve.wait_ge(sem("level_step"), 1)
            dve.tensor_scalar_mul(mean_sb, mean_sum, 1.0 / S).then_inc(sem("mean_sb"), 1)
            dve.wait_ge(sem("g_sb"), 3)
            dve.tensor_scalar(level_part, g3, reach, 0.7, ALU.mult, ALU.mult).then_inc(sem("level_step"), 1)
            dve.wait_ge(sem("level_step"), 2)
            dve.tensor_scalar(level[:, 0, :], level_part, 1.0, 0.1, ALU.mult, ALU.add)
            dve.tensor_scalar(level[:, 1, :], level_part, -1.0, -0.1, ALU.mult, ALU.add).then_inc(sem("level_step"), 1)
            dve.wait_ge(sem("level_step"), 3)

            def coefficients(j, c):
                b = j // (NB // B)
                tiles = slice(4 * j, 4 * j + 4)
                dve.wait_ge(sem("tf_ready"), NB * c + j + 1)
                t2 = tf[:, tiles].unsqueeze(2).broadcast_to([P, 4, 2])
                dve.tensor_scalar(coef[:, tiles, 0:4:3], t2, slope[:, 0:1], level[:, 0, b:b + 1], ALU.mult, ALU.add)
                dve.tensor_scalar(coef[:, tiles, 1:3], t2, slope[:, 1:2], level[:, 1, b:b + 1], ALU.mult, ALU.add)\
                    .then_inc(sem("coef_ready"), 1)

            def twisted(j):
                return twist[:, 4 * j:4 * j + 4, :]

            def update(j, c):
                tiles = slice(4 * j, 4 * j + 4)
                dve.wait_ge(sem("twist_ready"), NB * c + j + 1)
                dve.tensor_tensor(cur[:, tiles, :], cur[:, tiles, :], twisted(j), ALU.add)\
                    .then_inc(sem("cur_ready"), 1)

            def gain(j, source, name):
                tiles = slice(4 * j, 4 * j + 4)
                dve.scalar_tensor_tensor(x[:, tiles, :], source, gates[:, 3:4], x[:, tiles, :],
                                         ALU.mult, ALU.add).then_inc(sem(name), 1)

            def last_twist(j):
                dve.wait_ge(sem("coef_ready"), NB * (CYCLES - 1) + j + 1)
                twist_half(dve, j, 1).then_inc(sem("half_twisted"), 1)
                dve.wait_ge(sem("half_twisted"), j + 1)
                dve.wait_ge(sem("twist_ready"), NB * (CYCLES - 1) + j + 1)
                dve.wait_ge(sem("x_partial"), j + 1)
                gain(j, twisted(j), "x_final")

            def emit(c):
                if is_last(c):
                    turned_rest(dve, 2, c)
                    turned_rest(dve, 3, c)
                    for j in range(NB):
                        dve.wait_ge(sem("cur_ready"), NB * (c - 1) + j + 1)
                        gain(j, cur[:, 4 * j:4 * j + 4, :], "x_partial")
                    for j in range(NB):
                        coefficients(j, c)
                        last_twist(j)
                    return
                if not is_first(c):
                    turned_rest(dve, 2, c)
                    turned_rest(dve, 3, c)
                coefficients(0, c)
                coefficients(1, c)
                update(0, c)
                coefficients(2, c)
                coefficients(3, c)
                update(1, c)
                turned_rest(dve, 0, c + 1)
                update(2, c)
                turned_rest(dve, 1, c + 1)
                update(3, c)

            cycles(dve, emit)

        def twist_half(eng, j, h):
            tiles = slice(4 * j, 4 * j + 4)
            src = slice(128, 256) if h == 0 else slice(0, 128)
            return eng.tensor_tensor(
                twist[:, tiles, h * 128:(h + 1) * 128].rearrange("p t (s n) -> p t s n", s=2),
                cur[:, tiles, src].rearrange("p t (s n) -> p t s n", s=2),
                coef[:, tiles, 2 * h:2 * h + 2].unsqueeze(3).broadcast_to([P, 4, 2, 64]), ALU.mult)

        def pool_coupling(pool):
            def emit(c):
                for j in range(NB):
                    pool.wait_ge(sem("coef_ready"), NB * c + j + 1)
                    half = twist_half(pool, j, 0)
                    if not is_last(c):
                        half = twist_half(pool, j, 1)
                    half.then_inc(sem("twist_ready"), 1)

            cycles(pool, emit)

        @block.sync
        def _(sp):
            xs = t_in["x"].rearrange("b s d -> (b s) d").rearrange("(t p) d -> p t d", p=P)
            c2 = t_in["ctx_768"].rearrange("b s d -> (b s) d")
            sp.dma_start(ctx_rows[:, 0:2], c2[0:256].rearrange("(r p) d -> p r d", p=P)).then_inc(sem("ctx_in"), 16)
            sp.dma_start(ctx_rows[0:KEYS - 256, 2], c2[256:KEYS]).then_inc(sem("ctx_in"), 16)
            sp.dma_start(x[:, 0:4], xs[:, 0:4]).then_inc(sem("x_first"), 16)
            load_keys_values(sp, 0)
            for name, g in (("g_xattn", 0), ("g_ffn", 2)):
                sp.dma_start(gates[:, g:g + 2], t_in[name].partition_broadcast(P)).then_inc(sem("gates_in"), 16)
            load_attention(sp, 0)
            sp.dma_start(x[:, 4:NT], xs[:, 4:NT]).then_inc(sem("x_rest"), 16)
            sp.dma_start(Wr[:], t_in["L0_ffn_Wr"].rearrange("(k p) e -> p k e", p=P)).then_inc(sem("wr_in"), 16)
            sp.dma_start(br[:], t_in["L0_ffn_br"].partition_broadcast(P)).then_inc(sem("wr_in"), 16)
            sp.dma_start(W1, t_in["L0_ffn_W1"].rearrange("e (k p) n -> p e k n", p=P)).then_inc(sem("w1_in"), 16)
            sp.wait_ge(sem("xe_ready"), NT)
            sp.dma_start(xn_rows.rearrange("(t p) d -> p t d", p=P), xn_all).then_inc(sem("xn_stored"), 16)
            sp.dma_start(b1[:], t_in["L0_ffn_b1"].rearrange("e n -> (e n)").partition_broadcast(P)
                         .rearrange("p (e n) -> p e n", e=E)).then_inc(sem("b12_in"), 16)
            sp.dma_start(b2[:], t_in["L0_ffn_b2"].rearrange("e n -> (e n)").partition_broadcast(P)
                         .rearrange("p (e n) -> p e n", e=E)).then_inc(sem("b12_in"), 16)
            sp.dma_start(W2[:], t_in["L0_ffn_W2"].rearrange("e (k p) n -> p e k n", p=P)).then_inc(sem("w2_in"), 16)
            sp_experts(sp)
            for r in range(2):
                sp.wait_ge(sem(f"ey_out{r}"), 16 * ((SLOTS + 1 - r) // 2))
            load_attention(sp, 1)
            sp.wait_ge(sem("mixed"), 4)
            load_coupling(sp)
            outs = out.rearrange("b s d -> (b s) d").rearrange("(t p) d -> p t d", p=P)
            for j in range(NB):
                sp.wait_ge(sem("x_final"), j + 1)
                sp.dma_start(outs[:, 4 * j:4 * j + 4], x[:, 4 * j:4 * j + 4]).then_inc(sem("stored"), 16)
            sp.wait_ge(sem("stored"), 16 * NB)

        @block.gpsimd
        def _(pool):
            pool.memset(ident[:], 0.0).then_inc(sem("ident_zero"), 1)
            pool.memset(ones[:], 1.0).then_inc(sem("ones_ready"), 1)
            pool.iota(iota_e[:], [[1, E]], base=0, channel_multiplier=0, allow_small_or_imprecise_dtypes=True)
            pool.iota(iota_t[:], [[P, NT]], base=0, channel_multiplier=0, allow_small_or_imprecise_dtypes=True)
            pool.iota(iota_s, [[1, SLOTS]], base=0, channel_multiplier=0, allow_small_or_imprecise_dtypes=True)
            pool.iota(slot_start, [[P, SLOTS]], base=0, channel_multiplier=0, allow_small_or_imprecise_dtypes=True)
            pool.iota(iota_row, [[1, P]], base=0, channel_multiplier=0, allow_small_or_imprecise_dtypes=True)
            pool.iota(token_id, [[P, NT]], base=0, channel_multiplier=1, allow_small_or_imprecise_dtypes=True)\
                .then_inc(sem("iota_ready"), 1)
            pool.wait_ge(sem("ones_ready"), 1)
            pool.affine_select(out=before[:], in_=ones[:], compare_op=ALU.is_gt, fill=0.0, base=0,
                               pattern=[[1, P]], channel_multiplier=-1).then_inc(sem("before_ready"), 1)
            pool.memset(zero_eps[:, 0:1], 0.0)
            pool.memset(zero_eps[:, 1:2], EPS)
            pool.memset(minus_half[:], -0.5).then_inc(sem("eps_ready"), 1)
            pool.memset(ctx_rem, 0.0)
            pool.memset(ctx_rem1[:], 0.0).then_inc(sem("rem_zero"), 1)
            pool.wait_ge(sem("ident_zero"), 1)
            pool.affine_select(out=ident[:], in_=ident[:], compare_op=ALU.not_equal, fill=1.0, base=0,
                               pattern=[[-1, P]], channel_multiplier=1).then_inc(sem("ident_ready"), 1)
            pool.memset(K0, 0.0)
            pool.memset(V, 0.0).then_inc(sem("kv_zero"), 1)
            pool.memset(probs, 0.0).then_inc(sem("pads_zero"), 1)
            pool_attention(pool, L0)
            pool_routing(pool)
            pool_experts(pool)
            pool.wait_ge(sem("ey_sb"), SLOTS)
            pool.memset(V[:, 0, :, 2, :], 0.0).then_inc(sem("kv_zero"), 1)
            for r in range(2):
                pool.wait_ge(sem(f"ey_out{r}"), 16 * ((SLOTS + 1 - r) // 2))
            for t in range(5):
                if t == 2:
                    pool_rstd(pool, 0, 2, "in", 3)
                slots_now(pool, t, t % 2, None if t < 2 else t - 1)
                pool.wait_ge(sem("slot_now_ready"), t + 1)
                gather(pool, t, t % 2)
                if t == 1:
                    pool.memset(probs, 0.0).then_inc(sem("pads_zero"), 1)
            pool_attention(pool, L1)
            pool_coupling(pool)

        @block.scalar
        def _(act):
            act.wait_ge(sem("gates_in"), 32)
            act.activation(gates[:], gates[:], ACT.Tanh).then_inc(sem("gates_ready"), 1)
            act_attention(act, L0)
            act_routing(act)
            act_experts(act)
            act_attention(act, L1)
            act_coupling(act)

        @block.vector
        def _(dve):
            dve.wait_ge(sem("ctxT_ps"), 1)
            dve.tensor_copy(ctxT[:, :, :], banks[0:CK, 0:2, 0:KEYS]).then_inc(sem("ctxT_ready"), 1)
            dve.wait_ge(sem("ctxT_ready"), 1)
            dve.wait_ge(sem("rem_zero"), 1)
            for j in range(4):
                for k in range(2):
                    last = dve.tensor_copy(ctx_rem[:, k, :, j * 32:j * 32 + NKEY - P],
                                           ctxT[:, k, :].rearrange("p (b n) -> p b n", b=2)[:, :, P:NKEY])
            last.then_inc(sem("rem_ready"), 1)
            for j in range(2):
                last = dve.tensor_copy(ctx_rem1[:, :, j * 64:j * 64 + KEYS - 256], ctxT[:, :, 256:KEYS])
            last.then_inc(sem("rem_ready"), 1)
            dve_attention(dve, L0)
            dve.wait_ge(sem("iota_ready"), 1)
            dve_routing(dve)
            dve_experts(dve)
            dve.wait_ge(sem("weight_ready"), 1)
            dve_attention(dve, L1)
            dve_coupling(dve)

        @block.tensor
        def _(pe):
            pe.wait_ge(sem("ctx_in"), 32)
            pe.wait_ge(sem("ident_ready"), 1)
            for k in range(2):
                for r in range(3):
                    n = P if r < 2 else KEYS - 256
                    mm = pe.transpose(banks[0:CK, k, r * P:r * P + n], ctx_rows[0:n, r, k * CK:(k + 1) * CK],
                                      ident[0:n, 0:n])
            mm.then_inc(sem("ctxT_ps"), 1)
            pe.wait_ge(sem("ctxT_ready"), 1)
            pe_attention(pe, L0)
            pe_routing(pe)
            pe_experts(pe)
            pe_attention(pe, L1)
            pe_coupling(pe)


_INS = ["x", "ctx_768", "g_xattn", "g_ffn"] + [f"L0_xattn_{n}" for n in ("Wq", "Wk", "Wv", "Wo", "bo")] \
    + [f"L0_ffn_{n}" for n in ("W1", "b1", "W2", "b2", "Wr", "br")] \
    + [f"L1_xattn_{n}" for n in ("Wq", "Wk", "Wv", "Wout", "bout")] \
    + [f"L1_ffn_cn_{n}{i}" for i in (1, 2, 3, 4) for n in ("w", "b")] \
    + [f"L1_ffn_gc_{n}{i}" for i in (1, 2, 3) for n in ("w", "b")] + ["L1_ffn_adaptive_range"]


def kernel(**inputs):
    import concourse.bacc as bacc
    from concourse.bass_utils import run_bass_kernel_spmd

    nc = bacc.Bacc("TRN2", target_bir_lowering=False, num_devices=1)
    arrays, aps = {}, {}
    for name in _INS:
        a = np.ascontiguousarray(inputs[name])
        arrays[f"in_{name}"] = a
        aps[name] = nc.dram_tensor(f"in_{name}", a.shape, mybir.dt.from_np(a.dtype), kind="ExternalInput").ap()
    shape = arrays["in_x"].shape
    out = nc.dram_tensor("out", shape, F32, kind="ExternalOutput").ap()
    flamingo(nc, aps, out)
    r = run_bass_kernel_spmd(nc, [arrays], core_ids=[0])
    return r.results[0]["out"]
```
